# Optimizing a Trainium2 kernel written in Bass

```python
import numpy as np
import jax
import jax.numpy as jnp

def _softmax(x, axis=-1):
    return jax.nn.softmax(x, axis=axis)

def _gelu(x):
    return jax.nn.gelu(x, approximate=True)

def _silu(x):
    return jax.nn.silu(x)

def _sigmoid(x):
    return jax.nn.sigmoid(x)

def _layernorm(x, axis=-1, eps=1e-05):
    m = jnp.mean(x, axis=axis, keepdims=True)
    v = jnp.var(x, axis=axis, keepdims=True)
    return (x - m) / jnp.sqrt(v + eps)

def _scatter_add(tgt, idx, src, axis=0):
    return tgt.at[idx].add(src)

def _segment_sum(src, seg, n):
    return jax.ops.segment_sum(src, seg, n)
kernel_name = 'mk_perceiver_d4_seqx_r4_be466f'

def setup_inputs(seed: int=0):
    np.random.seed(seed)
    _w = jnp.asarray

    def _rec_inputs():
        import jax
        import jax.numpy as jnp
        _rk = jax.random.key(seed)
        x = 7.22e-05 + 1 * jax.random.normal(jax.random.fold_in(_rk, 1), (1, 128, 256), jnp.float32)
        _lenS = 128 - jax.random.randint(jax.random.fold_in(_rk, 7), (1,), 0, max(1, 128 // 4) + 1, jnp.int32)
        _lenS2 = 12544 - jax.random.randint(jax.random.fold_in(_rk, 8), (1,), 0, max(1, 12544 // 4) + 1, jnp.int32)
        _ctx_1024P = jax.random.normal(jax.random.fold_in(_rk, 11), (1, 16, 256), jnp.float32)
        _ctx_1024c = jax.random.dirichlet(jax.random.fold_in(_rk, 511), 0.3 * jnp.ones((16,), jnp.float32), (1, 12544))
        _ctx_1024t = jnp.einsum('bsk,bkd->bsd', _ctx_1024c, _ctx_1024P)
        _ctx_1024t = _ctx_1024t * jax.lax.rsqrt(jnp.mean(jnp.square(_ctx_1024t)) + 1e-12) * 0.953939
        ctx_1024 = 4.13588e-05 + 0.999923 * (_ctx_1024t + 0.3 * jax.random.normal(jax.random.fold_in(_rk, 611), (1, 12544, 256), jnp.float32))
        fside_Bx16xSxS2_0 = -6.00028e-05 + 1.00001 * jax.random.normal(jax.random.fold_in(_rk, 12), (1, 16, 128, 12544), jnp.float32)
        _validS = jnp.arange(128)[None, :] < _lenS[:, None]
        _validS2 = jnp.arange(12544)[None, :] < _lenS2[:, None]
        _causal = jnp.tril(jnp.ones((128, 128), dtype=bool))
        mask_BxS2_bf1 = jnp.ones((1, 12544), dtype=bool)
        return (x, ctx_1024, fside_Bx16xSxS2_0, mask_BxS2_bf1)
    x, ctx_1024, fside_Bx16xSxS2_0, mask_BxS2_bf1 = _rec_inputs()

    def _L0_xattn_setup():
        import jax, jax.numpy as jnp
        import numpy as np
        INPUT_DIM = 256
        EMBED_DIM = 256
        key = jax.random.key(seed)
        ks = jax.random.split(key, 6)
        B, S = (4, 512)
        q = jax.random.normal(ks[0], (B, S, INPUT_DIM), dtype=jnp.float32)
        k = jax.random.normal(ks[1], (B, S, INPUT_DIM), dtype=jnp.float32)
        v = jax.random.normal(ks[2], (B, S, INPUT_DIM), dtype=jnp.float32)
        scale = 1.0 / np.sqrt(INPUT_DIM)
        W_q = jax.random.uniform(ks[3], (INPUT_DIM, EMBED_DIM), jnp.float32, -scale, scale)
        W_k = jax.random.uniform(ks[4], (INPUT_DIM, EMBED_DIM), jnp.float32, -scale, scale)
        W_v = jax.random.uniform(ks[5], (INPUT_DIM, EMBED_DIM), jnp.float32, -scale, scale)
        return {'q': q, 'k': k, 'v': v, 'W_q': W_q, 'W_k': W_k, 'W_v': W_v}
    _L0_xattn_all = _L0_xattn_setup()
    _L0_xattn_in = {k: v for k, v in _L0_xattn_all.items() if k in ('W_q', 'W_k', 'W_v')}
    del _L0_xattn_all

    def _L0_attn_setup():
        import jax, jax.numpy as jnp
        import numpy as np
        D_MODEL = 256
        N_HEADS = 16
        D_KEYS = 64
        D_LLM = 256
        LN_EPS = 1e-12
        key = jax.random.key(seed)
        ks = jax.random.split(key, 14)
        B, L, S = (2, 512, 512)
        AH = N_HEADS * D_KEYS
        w = 0.02
        return {'target_embedding': jax.random.normal(ks[0], (B, L, D_MODEL), jnp.float32), 'source_embedding': jax.random.normal(ks[1], (S, D_LLM), jnp.float32), 'value_embedding': jax.random.normal(ks[2], (S, D_LLM), jnp.float32), 'Wq': jax.random.normal(ks[3], (D_MODEL, AH), jnp.float32) * w, 'bq': jnp.zeros((AH,), jnp.float32), 'Wk': jax.random.normal(ks[4], (D_LLM, AH), jnp.float32) * w, 'bk': jnp.zeros((AH,), jnp.float32), 'Wv': jax.random.normal(ks[5], (D_LLM, AH), jnp.float32) * w, 'bv': jnp.zeros((AH,), jnp.float32), 'Wo': jax.random.normal(ks[6], (AH, D_MODEL), jnp.float32) * w, 'bo': jnp.zeros((D_MODEL,), jnp.float32), 'ln_g': jnp.ones((D_MODEL,), jnp.float32), 'ln_b': jnp.zeros((D_MODEL,), jnp.float32)}
    _L0_attn_all = _L0_attn_setup()
    _L0_attn_in = {k: v for k, v in _L0_attn_all.items() if k in ('source_embedding', 'value_embedding', 'Wq', 'bq', 'Wk', 'bk', 'Wv', 'bv', 'Wo', 'bo', 'ln_g', 'ln_b')}
    del _L0_attn_all

    def _L0_ffn_setup():
        import jax, jax.numpy as jnp
        import numpy as np
        TOP_K = 2
        EPS = 1e-20
        key = jax.random.key(seed)
        ks = jax.random.split(key, 8)
        B, S, H, E, D = (4, 512, 256, 8, 512)
        s = 0.02
        return {'x': jax.random.normal(ks[0], (B, S, H), dtype=jnp.float32), 'Wr': jax.random.normal(ks[1], (H, E), dtype=jnp.float32) * s, 'Wg': jax.random.normal(ks[2], (E, H, D), dtype=jnp.float32) * s, 'Wu': jax.random.normal(ks[3], (E, H, D), dtype=jnp.float32) * s, 'Wd': jax.random.normal(ks[4], (E, D, H), dtype=jnp.float32) * s, 'Sg': jax.random.normal(ks[5], (H, D), dtype=jnp.float32) * s, 'Su': jax.random.normal(ks[6], (H, D), dtype=jnp.float32) * s, 'Sd': jax.random.normal(ks[7], (D, H), dtype=jnp.float32) * s}
    _L0_ffn_all = _L0_ffn_setup()
    _L0_ffn_in = {k: v for k, v in _L0_ffn_all.items() if k in ('Wr', 'Wg', 'Wu', 'Wd', 'Sg', 'Su', 'Sd')}
    del _L0_ffn_all

    def _L1_xattn_setup():
        import jax, jax.numpy as jnp
        import numpy as np
        EMBED_DIM = 256
        NUM_HEADS = 16
        HEAD_DIM = EMBED_DIM // NUM_HEADS
        BSZ, TGT, SRC = (4, 256, 512)
        key = jax.random.key(seed)
        ks = jax.random.split(key, 12)
        init = 1.0 / np.sqrt(EMBED_DIM)
        return {'hidden_states': jax.random.normal(ks[0], (BSZ, TGT, EMBED_DIM), jnp.float32), 'key_value_states': jax.random.normal(ks[1], (BSZ, SRC, EMBED_DIM), jnp.float32), 'bias': jax.random.normal(ks[2], (BSZ, NUM_HEADS, TGT, SRC), jnp.float32), 'Wq': jax.random.normal(ks[3], (EMBED_DIM, EMBED_DIM), jnp.float32) * init, 'bq': jax.random.normal(ks[4], (EMBED_DIM,), jnp.float32) * init, 'Wk': jax.random.normal(ks[5], (EMBED_DIM, EMBED_DIM), jnp.float32) * init, 'bk': jax.random.normal(ks[6], (EMBED_DIM,), jnp.float32) * init, 'Wv': jax.random.normal(ks[7], (EMBED_DIM, EMBED_DIM), jnp.float32) * init, 'bv': jax.random.normal(ks[8], (EMBED_DIM,), jnp.float32) * init, 'Wo': jax.random.normal(ks[9], (EMBED_DIM, EMBED_DIM), jnp.float32) * init, 'bo': jax.random.normal(ks[10], (EMBED_DIM,), jnp.float32) * init}
    _L1_xattn_all = _L1_xattn_setup()
    _L1_xattn_in = {k: v for k, v in _L1_xattn_all.items() if k in ('Wq', 'bq', 'Wk', 'bk', 'Wv', 'bv', 'Wo', 'bo')}
    del _L1_xattn_all

    def _L1_attn_setup():
        import jax, jax.numpy as jnp
        import numpy as np
        import math
        D_MODEL = 256
        D_STATE = 64
        DT_MIN, DT_MAX = (0.001, 0.1)
        key = jax.random.key(seed)
        ks = jax.random.split(key, 8)
        x = jax.random.normal(ks[0], (2, 1024, D_MODEL), dtype=jnp.float32)
        lim = 1.0 / math.sqrt(D_MODEL)
        Win = jax.random.uniform(ks[1], (D_MODEL, D_MODEL), minval=-lim, maxval=lim, dtype=jnp.float32)
        bin_ = jax.random.uniform(ks[2], (D_MODEL,), minval=-lim, maxval=lim, dtype=jnp.float32)
        Wout = jax.random.uniform(ks[3], (D_MODEL, D_MODEL), minval=-lim, maxval=lim, dtype=jnp.float32)
        bout = jax.random.uniform(ks[4], (D_MODEL,), minval=-lim, maxval=lim, dtype=jnp.float32)
        A_log = jnp.broadcast_to(jnp.log(jnp.arange(1, D_STATE + 1, dtype=jnp.float32)), (D_MODEL, D_STATE))
        B = 0.1 * jax.random.normal(ks[5], (D_MODEL, D_STATE), dtype=jnp.float32)
        C = 0.1 * jax.random.normal(ks[6], (D_MODEL, D_STATE), dtype=jnp.float32)
        Dp = jnp.ones((D_MODEL,), dtype=jnp.float32)
        log_dt = jax.random.uniform(ks[7], (D_MODEL,), dtype=jnp.float32) * (math.log(DT_MAX) - math.log(DT_MIN)) + math.log(DT_MIN)
        dt = jnp.exp(log_dt)
        return {'x': x, 'Win': Win, 'bin_': bin_, 'A_log': A_log, 'B': B, 'C': C, 'Dp': Dp, 'dt': dt, 'Wout': Wout, 'bout': bout}
    _L1_attn_all = _L1_attn_setup()
    _L1_attn_in = {k: v for k, v in _L1_attn_all.items() if k in ('Win', 'bin_', 'A_log', 'B', 'C', 'Dp', 'dt', 'Wout', 'bout')}
    del _L1_attn_all

    def _L1_ffn_setup():
        import jax, jax.numpy as jnp
        import numpy as np
        IN_DIM = 256
        OUT_DIM = 256
        NUM_EXPERTS = 8
        TOP_K = 2
        key = jax.random.key(seed)
        ks = jax.random.split(key, 5)
        s = 1.0 / np.sqrt(IN_DIM)
        x = jax.random.normal(ks[0], (4, 512, IN_DIM), dtype=jnp.float32)
        Wg = jax.random.uniform(ks[1], (IN_DIM, NUM_EXPERTS), jnp.float32, -s, s)
        bg = jnp.zeros((NUM_EXPERTS,), jnp.float32)
        We = jax.random.uniform(ks[2], (NUM_EXPERTS, OUT_DIM, IN_DIM), jnp.float32, -s, s)
        be = jax.random.uniform(ks[3], (NUM_EXPERTS, OUT_DIM), jnp.float32, -s, s)
        return {'x': x, 'Wg': Wg, 'bg': bg, 'We': We, 'be': be}
    _L1_ffn_all = _L1_ffn_setup()
    _L1_ffn_in = {k: v for k, v in _L1_ffn_all.items() if k in ('Wg', 'bg', 'We', 'be')}
    del _L1_ffn_all

    def _L2_xattn_setup():
        import jax, jax.numpy as jnp
        import numpy as np
        HEADS = 16
        DIM_HEAD = 64
        QUERY_DIM = 256
        INNER = HEADS * DIM_HEAD
        SCALE = DIM_HEAD ** (-0.5)
        key = jax.random.key(seed)
        ks = jax.random.split(key, 6)
        B, N, M = (2, 512, 512)
        x = jax.random.normal(ks[0], (B, N, QUERY_DIM), dtype=jnp.float32)
        context = jax.random.normal(ks[1], (B, M, QUERY_DIM), dtype=jnp.float32)
        s = QUERY_DIM ** (-0.5)
        Wq = jax.random.normal(ks[2], (QUERY_DIM, INNER), dtype=jnp.float32) * s
        Wk = jax.random.normal(ks[3], (QUERY_DIM, INNER), dtype=jnp.float32) * s
        Wv = jax.random.normal(ks[4], (QUERY_DIM, INNER), dtype=jnp.float32) * s
        Wo = jax.random.normal(ks[5], (INNER, QUERY_DIM), dtype=jnp.float32) * INNER ** (-0.5)
        return {'x': x, 'context': context, 'Wq': Wq, 'Wk': Wk, 'Wv': Wv, 'Wo': Wo}
    _L2_xattn_all = _L2_xattn_setup()
    _L2_xattn_in = {k: v for k, v in _L2_xattn_all.items() if k in ('Wq', 'Wk', 'Wv', 'Wo')}
    del _L2_xattn_all

    def _L2_attn_setup():
        import jax, jax.numpy as jnp
        import numpy as np
        B, L, D = (2, 512, 256)
        H, HD = (16, 64)
        LD = 64
        key = jax.random.key(seed)
        ks = jax.random.split(key, 6)
        s = lambda fan_in: 1.0 / np.sqrt(fan_in)
        x_bld = jax.random.normal(ks[0], (B, L, D), dtype=jnp.float32)
        Wq = jax.random.normal(ks[1], (D, H, HD), dtype=jnp.float32) * s(D)
        Wkv_down = jax.random.normal(ks[2], (D, LD), dtype=jnp.float32) * s(D)
        Wk_up = jax.random.normal(ks[3], (LD, H, HD), dtype=jnp.float32) * s(LD)
        Wv_up = jax.random.normal(ks[4], (LD, H, HD), dtype=jnp.float32) * s(LD)
        Wout = jax.random.normal(ks[5], (H, HD, D), dtype=jnp.float32) * s(H * HD)
        return {'x_bld': x_bld, 'Wq': Wq, 'Wkv_down': Wkv_down, 'Wk_up': Wk_up, 'Wv_up': Wv_up, 'Wout': Wout}
    _L2_attn_all = _L2_attn_setup()
    _L2_attn_in = {k: v for k, v in _L2_attn_all.items() if k in ('Wq', 'Wkv_down', 'Wk_up', 'Wv_up', 'Wout')}
    del _L2_attn_all

    def _L2_ffn_setup():
        import jax, jax.numpy as jnp
        import numpy as np
        E = 16
        K = 4
        B, S, H, I = (4, 256, 256, 512)
        key = jax.random.key(seed)
        k0, k1, k2, k3 = jax.random.split(key, 4)
        scale = 0.02
        return {'hidden_states': jax.random.normal(k0, (B, S, H), jnp.float32), 'router_w': jax.random.normal(k1, (H, E), jnp.float32) * scale, 'router_b': jnp.zeros((E,), jnp.float32), 'w1': jax.random.normal(k2, (E, H, I), jnp.float32) * scale, 'b1': jnp.zeros((E, I), jnp.float32), 'w2': jax.random.normal(k3, (E, I, H), jnp.float32) * scale, 'b2': jnp.zeros((E, H), jnp.float32)}
    _L2_ffn_all = _L2_ffn_setup()
    _L2_ffn_in = {k: v for k, v in _L2_ffn_all.items() if k in ('router_w', 'router_b', 'w1', 'b1', 'w2', 'b2')}
    del _L2_ffn_all

    def _L3_xattn_setup():
        import jax, jax.numpy as jnp
        import numpy as np
        N_HEADS = 16
        D_MODEL = 256
        HEAD_DIM = D_MODEL // N_HEADS
        MASK_FILL = -100000000.0

        def _split_heads(x):
            B, S, _ = x.shape
            return x.reshape(B, S, N_HEADS, HEAD_DIM).transpose(0, 2, 1, 3)
        key = jax.random.key(seed)
        ks = jax.random.split(key, 12)
        B, L, P = (2, 512, 512)
        s = 1.0 / np.sqrt(D_MODEL).astype(np.float32)
        inp = {'q': jax.random.normal(ks[0], (B, L, D_MODEL), dtype=jnp.float32), 'k': jax.random.normal(ks[1], (B, P, D_MODEL), dtype=jnp.float32), 'v': jax.random.normal(ks[2], (B, P, D_MODEL), dtype=jnp.float32), 'attention_mask': jnp.ones((B, P), dtype=bool), 'Wq': jax.random.normal(ks[3], (D_MODEL, D_MODEL), dtype=jnp.float32) * s, 'bq': jnp.zeros((D_MODEL,), dtype=jnp.float32), 'Wk': jax.random.normal(ks[4], (D_MODEL, D_MODEL), dtype=jnp.float32) * s, 'bk': jnp.zeros((D_MODEL,), dtype=jnp.float32), 'Wv': jax.random.normal(ks[5], (D_MODEL, D_MODEL), dtype=jnp.float32) * s, 'bv': jnp.zeros((D_MODEL,), dtype=jnp.float32), 'Wo': jax.random.normal(ks[6], (D_MODEL, D_MODEL), dtype=jnp.float32) * s, 'bo': jnp.zeros((D_MODEL,), dtype=jnp.float32)}
        return inp
    _L3_xattn_all = _L3_xattn_setup()
    _L3_xattn_in = {k: v for k, v in _L3_xattn_all.items() if k in ('Wq', 'bq', 'Wk', 'bk', 'Wv', 'bv', 'Wo', 'bo')}
    del _L3_xattn_all

    def _L3_attn_setup():
        import jax, jax.numpy as jnp
        import numpy as np
        D_MODEL = 256
        N_HEADS = 16
        WINDOW = 64
        SEQ = 1024
        BATCH = 1
        NEG_INF = -1e+30
        key = jax.random.key(seed)
        ks = jax.random.split(key, 5)
        scale = 0.02
        inp = {'x': jax.random.normal(ks[0], (BATCH, SEQ, D_MODEL), jnp.float32)}
        for i, name in enumerate(['Wq', 'Wk', 'Wv', 'Wo']):
            inp[name] = jax.random.normal(ks[1 + i], (D_MODEL, D_MODEL), jnp.float32) * scale
        for name in ['bq', 'bk', 'bv', 'bo']:
            inp[name] = jnp.zeros((D_MODEL,), jnp.float32)
        return inp
    _L3_attn_all = _L3_attn_setup()
    _L3_attn_in = {k: v for k, v in _L3_attn_all.items() if k in ('Wq', 'bq', 'Wk', 'bk', 'Wv', 'bv', 'Wo', 'bo')}
    del _L3_attn_all

    def _L3_ffn_setup():
        import jax, jax.numpy as jnp
        import numpy as np
        D = 256
        E = 12
        HS = 2 * D
        HR = 3 * D
        TAU = 1.5

        def _geglu(h):
            a, g = jnp.split(h, 2, axis=-1)
            return a * jax.nn.gelu(g, approximate=False)
        key = jax.random.key(seed)
        ks = jax.random.split(key, 12)

        def xavier(k, shape):
            fan_in, fan_out = (shape[-2], shape[-1])
            lim = jnp.sqrt(6.0 / (fan_in + fan_out))
            return jax.random.uniform(k, shape, jnp.float32, -lim, lim)
        x = jax.random.normal(ks[0], (2, 256, D), jnp.float32)
        Ws1 = xavier(ks[1], (D, 2 * HS))
        bs1 = jnp.zeros((2 * HS,), jnp.float32)
        Ws2 = xavier(ks[2], (HS, D))
        bs2 = jnp.zeros((D,), jnp.float32)
        We1 = xavier(ks[3], (E, D, 2 * HR))
        be1 = jnp.zeros((E, 2 * HR), jnp.float32)
        We2 = xavier(ks[4], (E, HR, D))
        be2 = jnp.zeros((E, D), jnp.float32)
        Wr = xavier(ks[5], (D, E))
        br = jnp.zeros((E,), jnp.float32)
        return {'x': x, 'Ws1': Ws1, 'bs1': bs1, 'Ws2': Ws2, 'bs2': bs2, 'We1': We1, 'be1': be1, 'We2': We2, 'be2': be2, 'Wr': Wr, 'br': br}
    _L3_ffn_all = _L3_ffn_setup()
    _L3_ffn_in = {k: v for k, v in _L3_ffn_all.items() if k in ('Ws1', 'bs1', 'Ws2', 'bs2', 'We1', 'be1', 'We2', 'be2', 'Wr', 'br')}
    del _L3_ffn_all
    return {'x': x, 'ctx_1024': ctx_1024, 'fside_Bx16xSxS2_0': fside_Bx16xSxS2_0, 'mask_BxS2_bf1': mask_BxS2_bf1, 'L0_xattn_W_q': _L0_xattn_in['W_q'], 'L0_xattn_W_k': _L0_xattn_in['W_k'], 'L0_xattn_W_v': _L0_xattn_in['W_v'], 'L0_attn_source_embedding': _L0_attn_in['source_embedding'], 'L0_attn_value_embedding': _L0_attn_in['value_embedding'], 'L0_attn_Wq': _L0_attn_in['Wq'], 'L0_attn_bq': _L0_attn_in['bq'], 'L0_attn_Wk': _L0_attn_in['Wk'], 'L0_attn_bk': _L0_attn_in['bk'], 'L0_attn_Wv': _L0_attn_in['Wv'], 'L0_attn_bv': _L0_attn_in['bv'], 'L0_attn_Wo': _L0_attn_in['Wo'], 'L0_attn_bo': _L0_attn_in['bo'], 'L0_attn_ln_g': _L0_attn_in['ln_g'], 'L0_attn_ln_b': _L0_attn_in['ln_b'], 'L0_ffn_Wr': _L0_ffn_in['Wr'], 'L0_ffn_Wg': _L0_ffn_in['Wg'], 'L0_ffn_Wu': _L0_ffn_in['Wu'], 'L0_ffn_Wd': _L0_ffn_in['Wd'], 'L0_ffn_Sg': _L0_ffn_in['Sg'], 'L0_ffn_Su': _L0_ffn_in['Su'], 'L0_ffn_Sd': _L0_ffn_in['Sd'], 'L1_xattn_Wq': _L1_xattn_in['Wq'], 'L1_xattn_bq': _L1_xattn_in['bq'], 'L1_xattn_Wk': _L1_xattn_in['Wk'], 'L1_xattn_bk': _L1_xattn_in['bk'], 'L1_xattn_Wv': _L1_xattn_in['Wv'], 'L1_xattn_bv': _L1_xattn_in['bv'], 'L1_xattn_Wo': _L1_xattn_in['Wo'], 'L1_xattn_bo': _L1_xattn_in['bo'], 'L1_attn_Win': _L1_attn_in['Win'], 'L1_attn_bin_': _L1_attn_in['bin_'], 'L1_attn_A_log': _L1_attn_in['A_log'], 'L1_attn_B': _L1_attn_in['B'], 'L1_attn_C': _L1_attn_in['C'], 'L1_attn_Dp': _L1_attn_in['Dp'], 'L1_attn_dt': _L1_attn_in['dt'], 'L1_attn_Wout': _L1_attn_in['Wout'], 'L1_attn_bout': _L1_attn_in['bout'], 'L1_ffn_Wg': _L1_ffn_in['Wg'], 'L1_ffn_bg': _L1_ffn_in['bg'], 'L1_ffn_We': _L1_ffn_in['We'], 'L1_ffn_be': _L1_ffn_in['be'], 'L2_xattn_Wq': _L2_xattn_in['Wq'], 'L2_xattn_Wk': _L2_xattn_in['Wk'], 'L2_xattn_Wv': _L2_xattn_in['Wv'], 'L2_xattn_Wo': _L2_xattn_in['Wo'], 'L2_attn_Wq': _L2_attn_in['Wq'], 'L2_attn_Wkv_down': _L2_attn_in['Wkv_down'], 'L2_attn_Wk_up': _L2_attn_in['Wk_up'], 'L2_attn_Wv_up': _L2_attn_in['Wv_up'], 'L2_attn_Wout': _L2_attn_in['Wout'], 'L2_ffn_router_w': _L2_ffn_in['router_w'], 'L2_ffn_router_b': _L2_ffn_in['router_b'], 'L2_ffn_w1': _L2_ffn_in['w1'], 'L2_ffn_b1': _L2_ffn_in['b1'], 'L2_ffn_w2': _L2_ffn_in['w2'], 'L2_ffn_b2': _L2_ffn_in['b2'], 'L3_xattn_Wq': _L3_xattn_in['Wq'], 'L3_xattn_bq': _L3_xattn_in['bq'], 'L3_xattn_Wk': _L3_xattn_in['Wk'], 'L3_xattn_bk': _L3_xattn_in['bk'], 'L3_xattn_Wv': _L3_xattn_in['Wv'], 'L3_xattn_bv': _L3_xattn_in['bv'], 'L3_xattn_Wo': _L3_xattn_in['Wo'], 'L3_xattn_bo': _L3_xattn_in['bo'], 'L3_attn_Wq': _L3_attn_in['Wq'], 'L3_attn_bq': _L3_attn_in['bq'], 'L3_attn_Wk': _L3_attn_in['Wk'], 'L3_attn_bk': _L3_attn_in['bk'], 'L3_attn_Wv': _L3_attn_in['Wv'], 'L3_attn_bv': _L3_attn_in['bv'], 'L3_attn_Wo': _L3_attn_in['Wo'], 'L3_attn_bo': _L3_attn_in['bo'], 'L3_ffn_Ws1': _L3_ffn_in['Ws1'], 'L3_ffn_bs1': _L3_ffn_in['bs1'], 'L3_ffn_Ws2': _L3_ffn_in['Ws2'], 'L3_ffn_bs2': _L3_ffn_in['bs2'], 'L3_ffn_We1': _L3_ffn_in['We1'], 'L3_ffn_be1': _L3_ffn_in['be1'], 'L3_ffn_We2': _L3_ffn_in['We2'], 'L3_ffn_be2': _L3_ffn_in['be2'], 'L3_ffn_Wr': _L3_ffn_in['Wr'], 'L3_ffn_br': _L3_ffn_in['br']}

def reference(x, ctx_1024, fside_Bx16xSxS2_0, mask_BxS2_bf1, L0_xattn_W_q, L0_xattn_W_k, L0_xattn_W_v, L0_attn_source_embedding, L0_attn_value_embedding, L0_attn_Wq, L0_attn_bq, L0_attn_Wk, L0_attn_bk, L0_attn_Wv, L0_attn_bv, L0_attn_Wo, L0_attn_bo, L0_attn_ln_g, L0_attn_ln_b, L0_ffn_Wr, L0_ffn_Wg, L0_ffn_Wu, L0_ffn_Wd, L0_ffn_Sg, L0_ffn_Su, L0_ffn_Sd, L1_xattn_Wq, L1_xattn_bq, L1_xattn_Wk, L1_xattn_bk, L1_xattn_Wv, L1_xattn_bv, L1_xattn_Wo, L1_xattn_bo, L1_attn_Win, L1_attn_bin_, L1_attn_A_log, L1_attn_B, L1_attn_C, L1_attn_Dp, L1_attn_dt, L1_attn_Wout, L1_attn_bout, L1_ffn_Wg, L1_ffn_bg, L1_ffn_We, L1_ffn_be, L2_xattn_Wq, L2_xattn_Wk, L2_xattn_Wv, L2_xattn_Wo, L2_attn_Wq, L2_attn_Wkv_down, L2_attn_Wk_up, L2_attn_Wv_up, L2_attn_Wout, L2_ffn_router_w, L2_ffn_router_b, L2_ffn_w1, L2_ffn_b1, L2_ffn_w2, L2_ffn_b2, L3_xattn_Wq, L3_xattn_bq, L3_xattn_Wk, L3_xattn_bk, L3_xattn_Wv, L3_xattn_bv, L3_xattn_Wo, L3_xattn_bo, L3_attn_Wq, L3_attn_bq, L3_attn_Wk, L3_attn_bk, L3_attn_Wv, L3_attn_bv, L3_attn_Wo, L3_attn_bo, L3_ffn_Ws1, L3_ffn_bs1, L3_ffn_Ws2, L3_ffn_bs2, L3_ffn_We1, L3_ffn_be1, L3_ffn_We2, L3_ffn_be2, L3_ffn_Wr, L3_ffn_br):
    import jax
    import jax.numpy as jnp

    def _L0_xattn_ref(q, k, v, W_q, W_k, W_v):
        import jax, jax.numpy as jnp
        import numpy as np
        INPUT_DIM = 256
        EMBED_DIM = 256
        Q = jnp.einsum('bsd,de->bse', q, W_q)
        K = jnp.einsum('bsd,de->bse', k, W_k)
        V = jnp.einsum('bsd,de->bse', v, W_v)
        scores = jnp.einsum('bqe,bke->bqk', Q, K) / jnp.sqrt(jnp.float32(EMBED_DIM))
        attn = jax.nn.softmax(scores, axis=-1)
        return jnp.einsum('bqk,bke->bqe', attn, V)

    def _L0_attn_ref(target_embedding, source_embedding, value_embedding, Wq, bq, Wk, bk, Wv, bv, Wo, bo, ln_g, ln_b):
        import jax, jax.numpy as jnp
        import numpy as np
        D_MODEL = 256
        N_HEADS = 16
        D_KEYS = 64
        D_LLM = 256
        LN_EPS = 1e-12
        B, L, _ = target_embedding.shape
        S = source_embedding.shape[0]
        H, E = (N_HEADS, D_KEYS)
        q = (target_embedding @ Wq + bq).reshape(B, L, H, E)
        k = (source_embedding @ Wk + bk).reshape(S, H, E)
        v = (value_embedding @ Wv + bv).reshape(S, H, E)
        eq = jax.nn.elu(q)
        ek = jax.nn.elu(k)
        qn = eq / jnp.linalg.norm(eq, axis=-1, keepdims=True)
        kn = ek / jnp.linalg.norm(ek, axis=-1, keepdims=True)
        scores = jnp.einsum('blhe,she->bhls', qn, kn)
        scale = 1.0 / np.sqrt(E).astype(np.float32)
        A = jax.nn.softmax(scale * scores, axis=-1)
        ctx = jnp.einsum('bhls,she->blhe', A, v).reshape(B, L, H * E)
        h = ctx @ Wo + bo
        x = h + target_embedding
        mu = jnp.mean(x, axis=-1, keepdims=True)
        var = jnp.mean(jnp.square(x - mu), axis=-1, keepdims=True)
        return (x - mu) / jnp.sqrt(var + LN_EPS) * ln_g + ln_b

    def _L0_ffn_ref(x, Wr, Wg, Wu, Wd, Sg, Su, Sd):
        import jax, jax.numpy as jnp
        import numpy as np
        TOP_K = 2
        EPS = 1e-20
        B, S, H = x.shape
        T = B * S
        xt = x.reshape(T, H)
        scores = jax.nn.softmax(xt @ Wr, axis=-1)
        topk_w, topk_idx = jax.lax.top_k(scores, TOP_K)
        topk_w = topk_w / (topk_w.sum(axis=-1, keepdims=True) + EPS)
        g = jax.nn.silu(jnp.einsum('th,ehd->etd', xt, Wg))
        u = jnp.einsum('th,ehd->etd', xt, Wu)
        out_all = jnp.einsum('etd,edh->eth', g * u, Wd)
        tok = jnp.arange(T)[:, None]
        gathered = out_all[topk_idx, tok, :]
        out = jnp.sum(gathered * topk_w[..., None], axis=1).reshape(B, S, H)
        shared = jax.nn.silu(x @ Sg) * (x @ Su) @ Sd
        return out + shared

    def _L1_xattn_ref(hidden_states, key_value_states, bias, Wq, bq, Wk, bk, Wv, bv, Wo, bo):
        import jax, jax.numpy as jnp
        import numpy as np
        EMBED_DIM = 256
        NUM_HEADS = 16
        HEAD_DIM = EMBED_DIM // NUM_HEADS
        BSZ, TGT, SRC = (4, 256, 512)
        B, T, E = hidden_states.shape
        S = key_value_states.shape[1]
        H, hd = (NUM_HEADS, HEAD_DIM)
        scaling = hd ** (-0.5)
        q = (hidden_states @ Wq.T + bq) * scaling
        k = key_value_states @ Wk.T + bk
        v = key_value_states @ Wv.T + bv
        q = q.reshape(B, T, H, hd).transpose(0, 2, 1, 3)
        k = k.reshape(B, S, H, hd).transpose(0, 2, 1, 3)
        v = v.reshape(B, S, H, hd).transpose(0, 2, 1, 3)
        scores = jnp.einsum('bhtd,bhsd->bhts', q, k) + bias
        probs = jax.nn.softmax(scores, axis=-1)
        attn = jnp.einsum('bhts,bhsd->bhtd', probs, v)
        attn = attn.reshape(B, T, E)
        return attn @ Wo.T + bo

    def _L1_attn_ref(x, Win, bin_, A_log, B, C, Dp, dt, Wout, bout):
        import jax, jax.numpy as jnp
        import numpy as np
        import math
        D_MODEL = 256
        D_STATE = 64
        DT_MIN, DT_MAX = (0.001, 0.1)
        b, L, d = x.shape
        x = x @ Win.T + bin_
        u = jnp.transpose(x, (0, 2, 1))
        A = -jnp.exp(-A_log)
        logdA = A * dt[:, None]
        dB = B * dt[:, None]
        t = jnp.arange(L, dtype=x.dtype)
        powers = jnp.exp(logdA[:, :, None] * t)
        k = jnp.einsum('dn,dnl->dl', C * dB, powers)
        n_fft = 2 * L
        k_f = jnp.fft.rfft(k, n=n_fft)
        u_f = jnp.fft.rfft(u, n=n_fft)
        y = jnp.fft.irfft(u_f * k_f[None], n=n_fft)[..., :L]
        y = y + u * Dp[:, None]
        y = jnp.transpose(y, (0, 2, 1))
        return y @ Wout.T + bout

    def _L1_ffn_ref(x, Wg, bg, We, be):
        import jax, jax.numpy as jnp
        import numpy as np
        IN_DIM = 256
        OUT_DIM = 256
        NUM_EXPERTS = 8
        TOP_K = 2
        gate = jax.nn.softmax(x @ Wg + bg, axis=-1)
        topk_vals, topk_idx = jax.lax.top_k(gate, TOP_K)
        onehot = jax.nn.one_hot(topk_idx, NUM_EXPERTS, dtype=gate.dtype)
        gate_sparse = jnp.einsum('bsk,bske->bse', topk_vals, onehot)
        gate_sparse = gate_sparse / jnp.sum(gate_sparse, axis=-1, keepdims=True)
        y = jnp.einsum('bsi,eoi->bseo', x, We) + be[None, None, :, :].transpose(0, 1, 2, 3)
        out = jnp.einsum('bseo,bse->bso', y, gate_sparse)
        return out

    def _L2_xattn_ref(x, context, Wq, Wk, Wv, Wo):
        import jax, jax.numpy as jnp
        import numpy as np
        HEADS = 16
        DIM_HEAD = 64
        QUERY_DIM = 256
        INNER = HEADS * DIM_HEAD
        SCALE = DIM_HEAD ** (-0.5)
        B, N, _ = x.shape
        M = context.shape[1]
        q = (x @ Wq).reshape(B, N, HEADS, DIM_HEAD)
        k = (context @ Wk).reshape(B, M, HEADS, DIM_HEAD)
        v = (context @ Wv).reshape(B, M, HEADS, DIM_HEAD)
        sim = jnp.einsum('bihd,bjhd->bhij', q, k) * SCALE
        attn = jax.nn.softmax(sim, axis=-1)
        out = jnp.einsum('bhij,bjhd->bihd', attn, v)
        out = out.reshape(B, N, INNER)
        return out @ Wo

    def _L2_attn_ref(x_bld, Wq, Wkv_down, Wk_up, Wv_up, Wout):
        import jax, jax.numpy as jnp
        import numpy as np
        B, L, D = (2, 512, 256)
        H, HD = (16, 64)
        LD = 64
        q_blhd = jnp.einsum('bld,dhk->blhk', x_bld, Wq)
        latent_bll = jnp.einsum('bld,dc->blc', x_bld, Wkv_down)
        k_blhd = jnp.einsum('blc,chk->blhk', latent_bll, Wk_up)
        v_blhd = jnp.einsum('blc,chk->blhk', latent_bll, Wv_up)
        attn = jnp.einsum('bqhd,bkhd->bhqk', q_blhd, k_blhd) / jnp.sqrt(jnp.asarray(HD, dtype=x_bld.dtype))
        l = x_bld.shape[1]
        mask = (jnp.arange(l)[None, :] <= jnp.arange(l)[:, None])[None, None]
        neg_inf = jnp.finfo(attn.dtype).min
        attn = jax.nn.softmax(jnp.where(mask, attn, neg_inf), axis=-1)
        y_blhd = jnp.einsum('bhqk,bkhd->bqhd', attn, v_blhd)
        return jnp.einsum('bqhd,hdo->bqo', y_blhd, Wout)

    def _L2_ffn_ref(hidden_states, router_w, router_b, w1, b1, w2, b2):
        import jax, jax.numpy as jnp
        import numpy as np
        E = 16
        K = 4
        B, S, H, I = (4, 256, 256, 512)
        b, s, h = hidden_states.shape
        logits = hidden_states @ router_w + router_b
        probs = jax.nn.softmax(logits, axis=-1)
        topw, topi = jax.lax.top_k(probs, K)
        topw = topw / jnp.sum(topw, axis=-1, keepdims=True)
        combine = jnp.sum(jax.nn.one_hot(topi, E, dtype=hidden_states.dtype) * topw[..., None], axis=2)
        x = hidden_states.reshape(b * s, h)
        c = combine.reshape(b * s, E)

        def body(acc, expert):
            w1e, b1e, w2e, b2e, ce = expert
            hmid = jax.nn.gelu(x @ w1e + b1e, approximate=False)
            return (acc + (hmid @ w2e + b2e) * ce[:, None], None)
        out, _ = jax.lax.scan(body, jnp.zeros_like(x), (w1, b1, w2, b2, c.T))
        return out.reshape(b, s, h)

    def _L3_xattn_ref(q, k, v, attention_mask, Wq, bq, Wk, bk, Wv, bv, Wo, bo):
        import jax, jax.numpy as jnp
        import numpy as np
        N_HEADS = 16
        D_MODEL = 256
        HEAD_DIM = D_MODEL // N_HEADS
        MASK_FILL = -100000000.0

        def _split_heads(x):
            B, S, _ = x.shape
            return x.reshape(B, S, N_HEADS, HEAD_DIM).transpose(0, 2, 1, 3)
        qm = _split_heads(q @ Wq.T + bq)
        km = _split_heads(k @ Wk.T + bk)
        vm = _split_heads(v @ Wv.T + bv)
        scores = jnp.einsum('bnlh,bnph->bnlp', qm, km) / np.sqrt(HEAD_DIM).astype(np.float32)
        mask = attention_mask[:, None, None, :]
        scores = jnp.where(mask, scores, MASK_FILL)
        attn = jax.nn.softmax(scores, axis=-1)
        out = jnp.einsum('bnlp,bnph->bnlh', attn, vm)
        B, _, L, _ = out.shape
        out = out.transpose(0, 2, 1, 3).reshape(B, L, D_MODEL)
        return out @ Wo.T + bo

    def _L3_attn_ref(x, Wq, bq, Wk, bk, Wv, bv, Wo, bo):
        import jax, jax.numpy as jnp
        import numpy as np
        D_MODEL = 256
        N_HEADS = 16
        WINDOW = 64
        SEQ = 1024
        BATCH = 1
        NEG_INF = -1e+30
        B, S, D = x.shape
        H = N_HEADS
        hd = D // H
        q = (x @ Wq + bq).reshape(B, S, H, hd).transpose(0, 2, 1, 3)
        k = (x @ Wk + bk).reshape(B, S, H, hd).transpose(0, 2, 1, 3)
        v = (x @ Wv + bv).reshape(B, S, H, hd).transpose(0, 2, 1, 3)
        scale = 1.0 / jnp.sqrt(jnp.asarray(hd, x.dtype))
        scores = jnp.einsum('bhqd,bhkd->bhqk', q, k) * scale
        i = jnp.arange(S)[:, None]
        j = jnp.arange(S)[None, :]
        allowed = (j <= i) & (i - j < WINDOW)
        scores = jnp.where(allowed, scores, NEG_INF)
        attn = jax.nn.softmax(scores, axis=-1)
        out = jnp.einsum('bhqk,bhkd->bhqd', attn, v)
        out = out.transpose(0, 2, 1, 3).reshape(B, S, D)
        return out @ Wo + bo

    def _L3_ffn_ref(x, Ws1, bs1, Ws2, bs2, We1, be1, We2, be2, Wr, br):
        import jax, jax.numpy as jnp
        import numpy as np
        D = 256
        E = 12
        HS = 2 * D
        HR = 3 * D
        TAU = 1.5

        def _geglu(h):
            a, g = jnp.split(h, 2, axis=-1)
            return a * jax.nn.gelu(g, approximate=False)
        B, T, Dm = x.shape
        xf = x.reshape(-1, Dm)
        ys = _geglu(xf @ Ws1 + bs1) @ Ws2 + bs2
        logits = (xf @ Wr + br) / TAU
        top_val, top_idx = jax.lax.top_k(logits, 2)
        top_w = jax.nn.softmax(top_val, axis=-1)
        onehot = jax.nn.one_hot(top_idx, E, dtype=x.dtype)
        w = jnp.einsum('nke,nk->ne', onehot, top_w)
        h = jnp.einsum('nd,edh->enh', xf, We1) + be1[:, None, :]
        act = _geglu(h)
        yE = jnp.einsum('enh,ehd->end', act, We2) + be2[:, None, :]
        yr = jnp.einsum('end,ne->nd', yE, w)
        return (ys + yr).reshape(B, T, Dm)
    x = x + _L0_xattn_ref(_layernorm(x, axis=-1), ctx_1024, ctx_1024, L0_xattn_W_q, L0_xattn_W_k, L0_xattn_W_v)
    x = x + _L0_attn_ref(_layernorm(x, axis=-1), L0_attn_source_embedding, L0_attn_value_embedding, L0_attn_Wq, L0_attn_bq, L0_attn_Wk, L0_attn_bk, L0_attn_Wv, L0_attn_bv, L0_attn_Wo, L0_attn_bo, L0_attn_ln_g, L0_attn_ln_b)
    x = x + _L0_ffn_ref(_layernorm(x, axis=-1), L0_ffn_Wr, L0_ffn_Wg, L0_ffn_Wu, L0_ffn_Wd, L0_ffn_Sg, L0_ffn_Su, L0_ffn_Sd)
    x = x + _L1_xattn_ref(_layernorm(x, axis=-1), ctx_1024, fside_Bx16xSxS2_0, L1_xattn_Wq, L1_xattn_bq, L1_xattn_Wk, L1_xattn_bk, L1_xattn_Wv, L1_xattn_bv, L1_xattn_Wo, L1_xattn_bo)
    x = x + _L1_attn_ref(_layernorm(x, axis=-1), L1_attn_Win, L1_attn_bin_, L1_attn_A_log, L1_attn_B, L1_attn_C, L1_attn_Dp, L1_attn_dt, L1_attn_Wout, L1_attn_bout)
    x = x + _L1_ffn_ref(_layernorm(x, axis=-1), L1_ffn_Wg, L1_ffn_bg, L1_ffn_We, L1_ffn_be)
    x = x + _L2_xattn_ref(_layernorm(x, axis=-1), ctx_1024, L2_xattn_Wq, L2_xattn_Wk, L2_xattn_Wv, L2_xattn_Wo)
    x = x + _L2_attn_ref(_layernorm(x, axis=-1), L2_attn_Wq, L2_attn_Wkv_down, L2_attn_Wk_up, L2_attn_Wv_up, L2_attn_Wout)
    x = x + _L2_ffn_ref(_layernorm(x, axis=-1), L2_ffn_router_w, L2_ffn_router_b, L2_ffn_w1, L2_ffn_b1, L2_ffn_w2, L2_ffn_b2)
    x = x + _L3_xattn_ref(_layernorm(x, axis=-1), ctx_1024, ctx_1024, mask_BxS2_bf1, L3_xattn_Wq, L3_xattn_bq, L3_xattn_Wk, L3_xattn_bk, L3_xattn_Wv, L3_xattn_bv, L3_xattn_Wo, L3_xattn_bo)
    x = x + _L3_attn_ref(_layernorm(x, axis=-1), L3_attn_Wq, L3_attn_bq, L3_attn_Wk, L3_attn_bk, L3_attn_Wv, L3_attn_bv, L3_attn_Wo, L3_attn_bo)
    x = x + _L3_ffn_ref(_layernorm(x, axis=-1), L3_ffn_Ws1, L3_ffn_bs1, L3_ffn_Ws2, L3_ffn_bs2, L3_ffn_We1, L3_ffn_be1, L3_ffn_We2, L3_ffn_be2, L3_ffn_Wr, L3_ffn_br)
    return x

_drawn_inputs = setup_inputs


def setup_inputs(seed=0):
    import zlib

    import numpy as np

    out = dict(_drawn_inputs(seed))
    spreads = {'L0_attn_bq': (0.0, 2.0),
     'L0_attn_bk': (0.0, 2.0),
     'L0_attn_bv': (0.0, 0.1),
     'L0_attn_bo': (0.0, 0.1),
     'L0_attn_ln_g': (1.0, 0.2),
     'L0_attn_ln_b': (0.0, 0.1),
     'L1_attn_Dp': (1.0, 0.549),
     'L1_ffn_bg': (0.0, 0.1),
     'L2_ffn_router_b': (0.0, 0.672),
     'L2_ffn_b1': (0.0, 0.8),
     'L2_ffn_b2': (0.0, 0.369),
     'L3_xattn_bq': (0.0, 0.8),
     'L3_xattn_bk': (0.0, 2.0),
     'L3_xattn_bv': (0.0, 0.357),
     'L3_xattn_bo': (0.0, 0.306),
     'L3_attn_bq': (0.0, 2.0),
     'L3_attn_bk': (0.0, 2.0),
     'L3_attn_bv': (0.0, 0.573),
     'L3_attn_bo': (0.0, 0.304),
     'L3_ffn_bs1': (0.0, 0.302),
     'L3_ffn_bs2': (0.0, 0.363),
     'L3_ffn_be1': (0.0, 0.489),
     'L3_ffn_be2': (0.0, 0.267),
     'L3_ffn_br': (0.0, 0.551)}
    factors = {'fside_Bx16xSxS2_0': 6.497,
     'L0_attn_source_embedding': 64.0,
     'L0_attn_value_embedding': 5.096,
     'L0_attn_Wq': 64.0,
     'L0_attn_Wk': 64.0,
     'L0_attn_Wv': 5.173,
     'L0_ffn_Wr': 4.679,
     'L0_ffn_Wg': 4.269,
     'L0_ffn_Wu': 7.371,
     'L0_ffn_Wd': 4.16,
     'L0_ffn_Sg': 2.817,
     'L0_ffn_Su': 3.459,
     'L0_ffn_Sd': 3.229,
     'L1_xattn_bq': 4.959,
     'L1_xattn_bk': 64.0,
     'L1_attn_bin_': 3.424,
     'L1_attn_A_log': 8.0,
     'L1_attn_B': 3.375,
     'L1_attn_C': 6.575,
     'L1_attn_dt': 3.605,
     'L1_ffn_be': 4.791,
     'L2_ffn_w1': 3.37,
     'L2_ffn_w2': 3.118,
     'L3_attn_Wq': 24.159,
     'L3_attn_Wk': 24.693,
     'L1_attn_bout': 4.076}
    for name, (base, spread) in spreads.items():
        noise = np.random.default_rng([zlib.crc32(name.encode()), seed]).standard_normal(out[name].shape)
        drawn = base * np.exp(spread * noise) if base else spread * noise
        out[name] = jnp.asarray(drawn.astype(out[name].dtype))
    for name, factor in factors.items():
        out[name] = (out[name] * factor).astype(out[name].dtype)
    return out
```

```python
from contextlib import ExitStack, contextmanager

import numpy as np
import concourse.bass as bass
from concourse import mybir

F32 = mybir.dt.float32
BF16 = mybir.dt.bfloat16
U8 = mybir.dt.uint8
I32 = mybir.dt.int32
ALU = mybir.AluOpType
ACT = mybir.ActivationFunctionType
AX = mybir.AxisListType.X

P = 128
D = 256
KT = D // P
SK = 12544
HEADS = 16
CH = SK // P
GRP = 14
GC = CH // GRP
GW = GC * P
HB = GW // 2
LN_EPS = 1e-5


def hold(sp, held, sem, value):
    sp.wait_ge(sem, value)
    sp.sem_inc(held, 1)


class Phase:

    def __init__(self, nc, ctx, name):
        self.nc, self.ctx, self.name, self.sems = nc, ctx, name, []

    def sb(self, name, shape, dt=F32):
        return self.ctx.enter_context(self.nc.sbuf_tensor(f"{self.name}_{name}", list(shape), dt))

    def ps(self, name, shape, dt=F32):
        return self.ctx.enter_context(self.nc.psum_tensor(f"{self.name}_{name}", list(shape), dt))

    def sem(self, name):
        s = self.nc.alloc_semaphore(f"{self.name}_{name}")
        self.sems.append(s)
        return s


@contextmanager
def phase(nc, name):
    with ExitStack() as ctx:
        ph = Phase(nc, ctx, name)
        yield ph
    nc.clear_and_free_semaphores(ph.sems)
    nc.all_engine_barrier()


def token_norm(nc, ph, com, xnT_ps):
    stats, mv, rstd = ph.sb("stats", [P, 6]), ph.sb("mv", [P, 2]), ph.sb("rstd", [P, 1])
    norm_step, root_ready, xn_ready, xnT_in_psum, xnT_ready = (
        ph.sem(s) for s in ("norm_step", "root_ready", "xn_ready", "xnT_in_psum", "xnT_ready"))

    def on_vector(dve):
        nc.vector.bn_stats(stats[:, :], com.x[:, :]).then_inc(norm_step, 1)
        dve.wait_ge(norm_step, 1)
        nc.vector.bn_aggr(mv[:, :], stats[:, :]).then_inc(norm_step, 1)
        dve.wait_ge(norm_step, 2)
        nc.vector.tensor_scalar(rstd[:, :], mv[:, 1:2], LN_EPS, None, ALU.add).then_inc(norm_step, 1)
        dve.wait_ge(root_ready, 1)
        nc.vector.reciprocal(rstd[:, :], rstd[:, :]).then_inc(norm_step, 1)
        dve.wait_ge(norm_step, 4)
        nc.vector.tensor_scalar(com.xn[:, :], com.x[:, :], mv[:, 0:1], rstd[:, 0:1],
                                ALU.subtract, ALU.mult).then_inc(xn_ready, 1)
        dve.wait_ge(xnT_in_psum, 1)
        nc.vector.tensor_copy(com.xnT[:, :, :], xnT_ps[:, :, :]).then_inc(xnT_ready, 1)
        dve.wait_ge(xnT_ready, 1)

    def on_scalar(act):
        act.wait_ge(norm_step, 3)
        nc.scalar.activation(rstd[:, :], rstd[:, :], ACT.Sqrt).then_inc(root_ready, 1)

    def on_tensor(pe):
        pe.wait_ge(xn_ready, 1)
        for k in range(KT):
            last = nc.tensor.transpose(xnT_ps[:, k, :], com.xn[:, k * P:(k + 1) * P], com.ident[:, :])
        last.then_inc(xnT_in_psum, 1)
        pe.wait_ge(xnT_ready, 1)

    return on_vector, on_scalar, on_tensor


TURNS = 4


def setup(nc, com, a):
    with phase(nc, "init") as ph:
        x_loaded, made = ph.sem("x_loaded"), ph.sem("made")
        with nc.Block() as block:
            @block.sync
            def _(sp):
                sp.dma_start(com.x[:, :], a["x"][0]).then_inc(x_loaded, 16)
                sp.wait_ge(x_loaded, 16)

            @block.gpsimd
            def _(pool):
                nc.gpsimd.memset(com.ident[:, :], 0.0).then_inc(made, 1)
                nc.gpsimd.memset(com.identb[:, :], 0.0).then_inc(made, 1)
                pool.wait_ge(made, 2)
                for m in (com.ident, com.identb):
                    nc.gpsimd.affine_select(out=m[:, :], in_=m[:, :], compare_op=ALU.not_equal, fill=1.0,
                                            base=0, pattern=[[-1, P]], channel_multiplier=1).then_inc(made, 1)
                pool.wait_ge(made, 4)



def prepare_context(nc, com, a, scr):
    with phase(nc, "prep") as ph:
        wq0 = ph.sb("wq0", [P, KT, D])
        nat_w = {n: ph.sb("nat_" + n, [P, KT, D]) for n in ("k0", "k1", "v1", "k3", "v3")}
        wT = {n: ph.sb("T_" + n, [P, KT, D]) for n in nat_w}
        wv2 = ph.sb("wv2", [P, KT, HEADS * 64])
        bk = {n: ph.sb("b" + n, [P, KT]) for n in ("k1", "k3")}
        q0T = ph.sb("q0T", [P, KT, P])
        qfT = ph.sb("qfT", [P, KT, P])
        mask_u8 = ph.sb("mask_u8", [P, GW], U8)
        mask = ph.sb("mask", [P, GW])
        fill_row = ph.sb("fill_row", [1, GW])
        fill_parts = ph.sb("fill_parts", [1, 3, GW], BF16)
        ctx_nat = ph.sb("ctx_nat", [P, GC, D])
        ctxT = ph.sb("ctxT", [P, KT, GW])
        kf = [ph.sb(f"kf{i}", [P, GW]) for i in range(2)]
        kparts = [ph.sb(f"kparts{i}", [P, 3, GW], BF16) for i in range(2)]
        vst = {n: ph.sb("st_" + n, [P, HEADS, GC, 16]) for n in ("v1", "v3")}
        v2st = ph.sb("st_v2", [P, HEADS, GC, 64])
        turn = ph.ps("turn", [P, TURNS, 512])
        work = ph.ps("work", [P, 2, 2, 512])
        norm_vector, norm_scalar, norm_tensor = token_norm(
            nc, ph, com, turn[:, 0, 0:D].rearrange("p (k n) -> p k n", k=KT))
        S = ph.sem
        weights_loaded, wT_in_psum, wT_ready, q0T_in_psum, q0T_ready, qfT_in_psum, qfT_ready = (
            S(s) for s in ("weights_loaded", "wT_in_psum", "wT_ready", "q0T_in_psum", "q0T_ready", "qfT_in_psum",
                           "qfT_ready"))
        ctx_loaded, turn_in_psum, ctxT_stored = (
            S(s) for s in ("ctx_loaded", "turn_in_psum", "ctxT_stored"))
        turn_copied = {"v": S("turn_copied_by_vector"), "s": S("turn_copied_by_scalar")}
        mask_loaded, mask_ready = S("mask_loaded"), S("mask_ready")
        work_full = S("work_full")
        freed = {"v": S("freed_by_vector"), "s": S("freed_by_scalar")}
        hi_ready, rest_ready, mid_ready, parts_ready = (
            S(s) for s in ("hi_ready", "rest_ready", "mid_ready", "parts_ready"))
        parts_stored = [S(f"parts_stored{i}") for i in range(2)]
        narrow_stored, wide_stored, held = S("narrow_values_stored"), S("wide_values_stored"), S("held")
        fill_step, fill_ready, fill_stored = S("fill_step"), S("fill_ready"), S("fill_stored")

        plan = [("s0", 0, "v"), ("k1", 0, "v"), ("v1", 0, "s"), ("k1", 1, "v"), ("v1", 4, "s"),
                ("k3", 0, "v"), ("v3", 0, "s"), ("k3", 1, "v"), ("v3", 4, "s")]
        plan += [("v2", c, "vs"[c % 2]) for c in range(GC)]
        assert len(plan) == 16
        n_by = {e: sum(p[2] == e for p in plan) for e in "vs"}

        def rank(i):
            return sum(p[2] == plan[i][2] for p in plan[:i + 1])

        turns = [(c, k) for c in range(GC) for k in range(KT)]

        with nc.Block() as block:
            @block.sync
            def _(sp):
                loads = [(wq0, a["L0_xattn_W_q"]), (nat_w["k0"], a["L0_xattn_W_k"]), (nat_w["k1"], a["L1_xattn_Wk"]),
                         (nat_w["v1"], a["L1_xattn_Wv"]), (nat_w["k3"], a["L3_xattn_Wk"]),
                         (nat_w["v3"], a["L3_xattn_Wv"]), (wv2, a["L2_xattn_Wv"])]
                for t, src in loads:
                    sp.dma_start(t[:, :, :], src.rearrange("(k p) n -> p k n", p=P)).then_inc(weights_loaded, 16)
                for n, src in (("k1", a["L1_xattn_bk"]), ("k3", a["L3_xattn_bk"])):
                    sp.dma_start(bk[n][:, :], src.rearrange("(k p) -> p k", p=P),
                                 allow_slow_non_contiguous=True).then_inc(weights_loaded, 16)
                sp.sem_inc(turn_in_psum, 1)
                sp.sem_inc(work_full, 1)
                sp.sem_inc(mask_ready, 1)
                sp.sem_inc(turn_copied["v"], 2)
                sp.sem_inc(turn_copied["s"], 2)
                for e in "vs":
                    sp.sem_inc(freed[e], n_by[e])
                sp.sem_inc(parts_ready, 2)
                for s in (parts_stored[0], parts_stored[1], ctxT_stored, fill_stored):
                    sp.sem_inc(s, 16)
                sp.sem_inc(narrow_stored, 32)
                sp.sem_inc(wide_stored, 16)

                def load(g):
                    hold(sp, held, turn_in_psum, g * TURNS + 1)
                    sp.dma_start(ctx_nat[:, :, :], a["ctx_1024"][0, bass.ds(g * GW, GW), :]
                                 .rearrange("(c p) d -> p c d", p=P)).then_inc(ctx_loaded, 16)
                    hold(sp, held, mask_ready, g + 1)
                    sp.dma_start(mask_u8[:, :], a["mask_BxS2_bf1"][0:1, bass.ds(g * GW, GW)]
                                 .to_broadcast([P, GW])).then_inc(mask_loaded, 16)

                def store(g):
                    for e in "vs":
                        hold(sp, held, turn_copied[e], g * 2 + 4)
                    sp.dma_start(scr.ctxT[:, :, bass.ds(g * GW, GW)], ctxT[:, :, :]).then_inc(ctxT_stored, 16)
                    hold(sp, held, fill_ready, g + 1)
                    sp.dma_start(scr.fill[:, :, bass.ds(g * GW, GW)], fill_parts[:, :, :]).then_inc(fill_stored, 16)
                    for i, (n, t) in enumerate((("k1", 0), ("k1", 1), ("k3", 0), ("k3", 1))):
                        hold(sp, held, parts_ready, g * 4 + i + 1 + 2)
                        sp.dma_start(scr.kparts[n][:, t * P:(t + 1) * P, bass.ds(g * GW, GW)]
                                     .rearrange("a p s -> p a s"), kparts[i % 2][:, :, :]).then_inc(parts_stored[i % 2], 16)
                    hold(sp, held, freed["s"], (g + 1) * n_by["s"] + rank(8))
                    for n in ("v1", "v3"):
                        sp.dma_start(scr.v[n][:, :, bass.ds(g * GC, GC), :].rearrange("h p c e -> p h c e"),
                                     vst[n][:, :, :, :]).then_inc(narrow_stored, 16)
                    for e in "vs":
                        hold(sp, held, freed[e], (g + 2) * n_by[e])
                    sp.dma_start(scr.v["v2"][:, :, bass.ds(g * GC, GC), :].rearrange("h p c e -> p h c e"),
                                 v2st[:, :, :, :]).then_inc(wide_stored, 16)

                load(0)
                with sp.Fori(0, GRP - 1) as g:
                    load(g + 1)
                    store(g)
                store(GRP - 1)
                sp.wait_ge(ctxT_stored, 16 * GRP + 16)
                sp.wait_ge(fill_stored, 16 * GRP + 16)
                sp.wait_ge(parts_stored[0], 16 * 2 * GRP + 16)
                sp.wait_ge(parts_stored[1], 16 * 2 * GRP + 16)
                sp.wait_ge(narrow_stored, 32 * GRP + 32)
                sp.wait_ge(wide_stored, 16 * GRP + 16)

            @block.tensor
            def _(pe):
                norm_tensor(pe)
                pe.wait_ge(weights_loaded, 16 * 9)
                for n_i, n in enumerate(nat_w):
                    if n_i:
                        pe.wait_ge(wT_ready, n_i)
                    for k in range(KT):
                        for o in range(KT):
                            last = nc.tensor.transpose(turn[:, 0, (k * KT + o) * P:(k * KT + o + 1) * P],
                                                       nat_w[n][:, o, k * P:(k + 1) * P], com.ident[:, :])
                    last.then_inc(wT_in_psum, 1)
                for e in range(KT):
                    for k in range(KT):
                        last = nc.tensor.matmul(work[:, 0, 0, e * P:(e + 1) * P], wq0[:, k, e * P:(e + 1) * P],
                                                com.xnT[:, k, :], start=(k == 0), stop=(k == KT - 1))
                last.then_inc(q0T_in_psum, 1)
                pe.wait_ge(q0T_ready, 1)
                pe.wait_ge(wT_ready, 5)
                for e in range(KT):
                    for k in range(KT):
                        last = nc.tensor.matmul(work[:, 0, 1, e * P:(e + 1) * P], wT["k0"][:, k, e * P:(e + 1) * P],
                                                q0T[:, k, :], start=(k == 0), stop=(k == KT - 1))
                last.then_inc(qfT_in_psum, 1)
                pe.wait_ge(qfT_ready, 1)
                with pe.Fori(0, GRP) as g:
                    pe.wait_ge(ctx_loaded, g * 16 + 16)
                    for t in range(TURNS):
                        pe.wait_ge(turn_copied["vs"[t % 2]], g * 2 + t // 2 + 1)
                        for j, (c, k) in enumerate(turns[4 * t:4 * t + 4]):
                            last = nc.tensor.transpose(turn[:, t, j * P:(j + 1) * P],
                                                       ctx_nat[:, c, k * P:(k + 1) * P], com.ident[:, :])
                        last.then_inc(turn_in_psum, 1)
                    for e in "vs":
                        pe.wait_ge(turn_copied[e], g * 2 + 4)
                    for i, (what, j, _e) in enumerate(plan):
                        w = work[:, i % 2]
                        b = i - 2 if i >= 2 else len(plan) + i - 2
                        e = plan[b][2]
                        pe.wait_ge(freed[e], (g + 1 if i >= 2 else g) * n_by[e] + rank(b))
                        if what in ("s0", "k1", "k3"):
                            for h in range(2):
                                for k in range(KT):
                                    lhs = qfT[:, k, :] if what == "s0" else wT[what][:, k, j * P:(j + 1) * P]
                                    last = nc.tensor.matmul(w[:, h, 0:HB], lhs, ctxT[:, k, h * HB:(h + 1) * HB],
                                                            start=(k == 0), stop=(k == KT - 1))
                        elif what == "v2":
                            for h in range(2):
                                for k in range(KT):
                                    last = nc.tensor.matmul(w[:, h, :], ctxT[:, k, j * P:(j + 1) * P],
                                                            wv2[:, k, h * 512:(h + 1) * 512],
                                                            start=(k == 0), stop=(k == KT - 1))
                        else:
                            for c in range(j, min(j + 4, GC)):
                                for k in range(KT):
                                    last = nc.tensor.matmul(w[:, (c - j) // 2, (c - j) % 2 * D:(c - j) % 2 * D + D],
                                                            ctxT[:, k, c * P:(c + 1) * P], wT[what][:, k, :],
                                                            start=(k == 0), stop=(k == KT - 1))
                        last.then_inc(work_full, 1)

            def take_turned(eng, copy, g, ts):
                for t in ts:
                    eng.wait_ge(turn_in_psum, g * TURNS + t + 2)
                    if t == ts[0]:
                        eng.wait_ge(ctxT_stored, g * 16 + 16)
                        eng.wait_ge(work_full, g * len(plan) + 1)
                    n = 2 if t < 3 else 1
                    copy(ctxT[:, :, 2 * t * P:(2 * t + n) * P].rearrange("p k (c q) -> p c k q", q=P),
                         turn[:, t, 0:n * 2 * P].rearrange("p (c k q) -> p c k q", k=KT, q=P)
                         ).then_inc(turn_copied["vs"[t % 2]], 1)

            def take_values(eng, copy, g, what, j, i):
                w = work[:, i % 2]
                if what == "v2":
                    eng.wait_ge(wide_stored, g * 16 + 16)
                else:
                    eng.wait_ge(narrow_stored, g * 32 + 32)
                eng.wait_ge(work_full, g * len(plan) + i + 2)
                if what == "v2":
                    return copy(v2st[:, :, j, :], w[:, :, :].rearrange("p b (h e) -> p (b h) e", e=64))
                n = min(4, GC - j)
                out = vst[what][:, :, j:j + n, :].rearrange("p h c e -> p c h e")
                for c in range(n):
                    last = copy(out[:, c], w[:, c // 2, c % 2 * D:c % 2 * D + D].rearrange("p (h e) -> p h e", e=16))
                return last

            @block.vector
            def _(dve):
                norm_vector(dve)
                for n_i, n in enumerate(nat_w):
                    dve.wait_ge(wT_in_psum, n_i + 1)
                    nc.vector.tensor_copy(wT[n][:, :, :].rearrange("p k n -> p (k n)"), turn[:, 0, :]).then_inc(wT_ready, 1)
                dve.wait_ge(q0T_in_psum, 1)
                nc.vector.tensor_copy(q0T[:, :, :].rearrange("p k n -> p (k n)"), work[:, 0, 0, 0:D]).then_inc(q0T_ready, 1)
                dve.wait_ge(qfT_in_psum, 1)
                nc.vector.tensor_scalar(qfT[:, :, :].rearrange("p k n -> p (k n)"), work[:, 0, 1, 0:D], 1.0 / 16, None,
                                        ALU.mult).then_inc(qfT_ready, 1)
                with dve.Fori(0, GRP) as g:
                    take_turned(dve, nc.vector.tensor_copy, g, (0, 2))
                    dve.wait_ge(mask_loaded, g * 16 + 16)
                    nc.vector.tensor_copy(mask[:, :], mask_u8[:, :]).then_inc(mask_ready, 1)
                    dve.wait_ge(mask_ready, g + 2)
                    nc.vector.tensor_scalar(fill_row[:, :], mask[0:1, :], 1.0, 1e8, ALU.subtract,
                                            ALU.mult).then_inc(fill_step, 1)
                    dve.wait_ge(fill_stored, g * 16 + 16)
                    dve.wait_ge(fill_step, g * 5 + 1)
                    for k in range(2):
                        nc.vector.tensor_copy(fill_parts[:, k, :], fill_row[:, :]).then_inc(fill_step, 1)
                        dve.wait_ge(fill_step, g * 5 + 2 * k + 2)
                        nc.vector.tensor_tensor(fill_row[:, :], fill_row[:, :], fill_parts[:, k, :],
                                                ALU.subtract).then_inc(fill_step, 1)
                        dve.wait_ge(fill_step, g * 5 + 2 * k + 3)
                    nc.vector.tensor_copy(fill_parts[:, 2, :], fill_row[:, :]).then_inc(fill_ready, 1)
                    nk = 0
                    for i, (what, j, e) in enumerate(plan):
                        if e != "v":
                            continue
                        if what in ("v1", "v2", "v3"):
                            take_values(dve, nc.vector.tensor_copy, g, what, j, i).then_inc(freed["v"], 1)
                            continue
                        dve.wait_ge(work_full, g * len(plan) + i + 2)
                        w = work[:, i % 2, :, 0:HB]
                        if what == "s0":
                            nc.vector.tensor_reduce(com.mx0[:, bass.ds(g, 1)], w, mybir.AxisListType.XY, ALU.max)
                            nc.vector.tensor_copy(com.S[:, bass.ds(g * GW, GW)].rearrange("p (b s) -> p b s", b=2),
                                                  w).then_inc(freed["v"], 1)
                            continue
                        dve.wait_ge(parts_ready, g * 4 + nk + 1)
                        out = kf[nk % 2][:, :].rearrange("p (b s) -> p b s", b=2)
                        if what == "k1":
                            ins = nc.vector.tensor_scalar(out, w, bk["k1"][:, j:j + 1], None, ALU.add)
                        else:
                            ins = nc.vector.scalar_tensor_tensor(
                                out=out, in0=w, scalar=bk["k3"][:, j:j + 1],
                                in1=mask[:, :].rearrange("p (b s) -> p b s", b=2), op0=ALU.add, op1=ALU.mult)
                        ins.then_inc(freed["v"], 1)
                        nk += 1

            @block.scalar
            def _(act):
                norm_scalar(act)
                act.wait_ge(qfT_ready, 1)
                with act.Fori(0, GRP) as g:
                    take_turned(act, nc.scalar.copy, g, (1, 3))
                    nk = 0
                    for i, (what, j, e) in enumerate(plan):
                        if e == "s":
                            take_values(act, nc.scalar.copy, g, what, j, i).then_inc(freed["s"], 1)
                        elif what in ("k1", "k3"):
                            parts = kparts[nk % 2]
                            act.wait_ge(parts_stored[nk % 2], g * 32 + nk // 2 * 16 + 16)
                            act.wait_ge(freed["v"], (g + 1) * n_by["v"] + rank(i))
                            nc.scalar.copy(parts[:, 0, :], kf[nk % 2][:, :]).then_inc(hi_ready, 1)
                            act.wait_ge(rest_ready, g * 4 + nk + 1)
                            nc.scalar.copy(parts[:, 1, :], kf[nk % 2][:, :]).then_inc(mid_ready, 1)
                            nk += 1

            @block.gpsimd
            def _(pool):
                with pool.Fori(0, GRP) as g:
                    for nk in range(4):
                        k, parts = kf[nk % 2], kparts[nk % 2]
                        pool.wait_ge(hi_ready, g * 4 + nk + 1)
                        nc.gpsimd.tensor_tensor(k[:, :], k[:, :], parts[:, 0, :], ALU.subtract).then_inc(rest_ready, 1)
                        pool.wait_ge(mid_ready, g * 4 + nk + 1)
                        nc.gpsimd.tensor_tensor(parts[:, 2, :], k[:, :], parts[:, 1, :],
                                                ALU.subtract).then_inc(parts_ready, 1)


def common(nc, ctx):
    class Shared:
        pass
    com, scr = Shared(), Shared()
    def sb(name, shape, dt=F32):
        return ctx.enter_context(nc.sbuf_tensor("all_" + name, shape, dt))
    com.x, com.xn, com.xnT = sb("x", [P, D]), sb("xn", [P, D]), sb("xnT", [P, KT, P])
    com.ident, com.identb = sb("ident", [P, P]), sb("identb", [P, P], BF16)
    com.S, com.mx0 = sb("S", [P, SK]), sb("mx0", [P, GRP])
    scr.ctxT = nc.dram_tensor("scratch_ctxT", [P, KT, SK], F32).ap()
    scr.fill = nc.dram_tensor("scratch_fill", [1, 3, SK], BF16).ap()
    scr.kparts = {n: nc.dram_tensor("scratch_" + n, [3, D, SK], BF16).ap() for n in ("k1", "k3")}
    scr.att1 = nc.dram_tensor("scratch_att1", [HEADS, P, 16], F32).ap()
    scr.v = {n: nc.dram_tensor("scratch_" + n, [HEADS, P, CH, w], F32).ap()
             for n, w in (("v1", 16), ("v2", 64), ("v3", 16))}
    return com, scr



R = 7
LAG = 3
PIECES = (0, 1, 2, 0, 1, 0)
QPIECES = (0, 0, 0, 1, 1, 2)
STACK = 16 * len(PIECES)


def head_stream(nc, ph, com, heads, vw, att, v_src, q=None, k_half=None, k_loads=None, bias=None, ring=R, lag=LAG,
                by_vector=(1, 3, 5, 8, 10, 12), q_cur=None,
                ctxT=None, ctx_loaded=None, sum_ps=None):
    v_half = [ph.sb(f"v_half{j}", [P, CH // 2, vw]) for j in range(2)]
    pT = [ph.sb(f"pT{i}", [P, GW]) for i in range(ring)]
    rowmax, negmax = ph.sb("rowmax", [P, 2 * GRP]), ph.sb("negmax", [P, 1])
    rowsum, total, inverse = ph.sb("rowsum", [P, GRP]), ph.sb("total", [P, 1]), ph.sb("inverse", [P, 1])
    turned_ps = [ph.ps(f"turned{i}", [P, 1024]) for i in range(2)]
    scores_ps = [ph.ps(f"scores{i}", [P, 512]) for i in range(2)] if q is not None or ctxT is not None else None
    out_ps = ph.ps("out", [P, 512])
    tiles = P // vw // 2 if vw < 64 else P // vw if vw < P else 1
    if tiles > 1:
        out_parts, select = ph.sb("out_parts", [P, P]), ph.sb("select", [P, vw])
        parts_ready, summed, cleared = ph.sem("parts_ready"), ph.sem("summed"), ph.sem("cleared")
    if bias is not None:
        bias_tile = [ph.sb(f"bias{i}", [P, 2 * GW]) for i in range(GRP // 2)]
        bias_loaded = [ph.sem(f"bias_loaded{i}") for i in range(GRP // 2)]
    S = ph.sem
    scores_full, scores_taken, negmax_ready, max_step = (
        S("scores_full"), S("scores_taken"), S("negmax_ready"), S("max_step"))
    exp_done, turned, weighed, rowsum_taken, out_step, out_taken = (
        S(s) for s in ("exp_done", "turned", "weighed", "rowsum_taken", "out_step", "out_taken"))
    copied = {"v": S("copied_by_vector"), "s": S("copied_by_scalar")}
    k_loaded = [S(f"k_loaded{j}") for j in range(2)]
    v_loaded = [S(f"v_loaded{j}") for j in range(2)]
    held, held_by_vector = S("held"), S("held_by_vector")
    by = ["v" if c in by_vector else "s" for c in range(GRP)]
    n_by = {e: by.count(e) for e in "vs"}
    rank = [by[:c + 1].count(by[c]) for c in range(GRP)]
    more_scores = scores_ps is not None

    class Run:
        pass
    run = Run()
    run.turned_ps, run.turned = turned_ps, turned
    run.exp_done, run.out_taken, run.scores_full, run.negmax = exp_done, out_taken, scores_full, negmax
    run.rowmax, run.negmax_ready, run.max_step = rowmax, negmax_ready, max_step

    def load_keys(sp, h, j, first):
        if k_loads is not None:
            if not first:
                hold(sp, held, scores_full, (h - 1) * 2 * GRP + GRP * (j + 1))
            for dst, src in k_loads(h, j):
                sp.dma_start(dst, src).then_inc(k_loaded[j], 16)

    def load_bias(sp, h, i, first):
        if bias is not None:
            if not first:
                hold(sp, held, scores_taken, (h - 1) * 2 * GRP + 4 * (i + 1) + 2)
            sp.dma_start(bias_tile[i][:, :], bias(h, i)).then_inc(bias_loaded[i], 16)

    def load_values(sp, h, j, first):
        if not first:
            hold(sp, held, weighed, (h - 1) * GRP + GRP // 2 * (j + 1) + ring)
        sp.dma_start(v_half[j][:, :, :], v_src(h, j)).then_inc(v_loaded[j], 16)

    def load_head(sp, k, v, first=False):
        for i in range(GRP // 2):
            if k is not None:
                load_bias(sp, k, i, first)
                if i == 2:
                    load_keys(sp, k, 0, first)
                if i == 6:
                    load_keys(sp, k, 1, first)
            if v is not None:
                if i == 3:
                    load_values(sp, v, 0, first)
                if i == 6:
                    load_values(sp, v, 1, first)

    def on_sync(sp):
        sp.sem_inc(scores_taken, 2)
        sp.sem_inc(weighed, ring)
        sp.sem_inc(rowsum_taken, 1)
        sp.sem_inc(out_taken, 1)
        for e in "vs":
            sp.sem_inc(copied[e], n_by[e])
        load_head(sp, 0, 0, True)
        if heads > 1:
            load_head(sp, 1, None)
            with sp.Fori(0, heads - 2) as h:
                load_head(sp, h + 2, h + 1)
            load_head(sp, None, heads - 1)

    n_k = len(k_loads(0, 0)) if k_loads is not None else 0

    def scores(pe, h, c):
        if k_loads is not None and c % (GRP // 2) == 0:
            j = c // (GRP // 2)
            pe.wait_ge(k_loaded[j], (h + 1) * 16 * n_k)
        for b in (2 * c, 2 * c + 1):
            pe.wait_ge(scores_taken, h * 2 * GRP + b + 1)
            if ctxT is None:
                j, at = b // GRP, b % GRP
                nc.tensor.matmul(scores_ps[b % 2][:, 0:HB], q[:, bass.ds(h * P, P)],
                                 k_half[j][:, at * HB:(at + 1) * HB], start=True, stop=True).then_inc(scores_full, 1)
            else:
                for k in range(KT):
                    last = nc.tensor.matmul(scores_ps[b % 2][:, 0:HB], q_cur[:, k, :],
                                            ctxT[:, k, b * HB:(b + 1) * HB], start=(k == 0), stop=(k == KT - 1))
                last.then_inc(scores_full, 1)

    def turn(pe, h, c):
        pe.wait_ge(exp_done, h * GRP + c + 1)
        b = c - 2 if c >= 2 else c - 2 + GRP
        pe.wait_ge(copied[by[b]], (h + 1 if c >= 2 else h) * n_by[by[b]] + rank[b])
        for i in range(GC):
            last = nc.tensor.transpose(turned_ps[c % 2][:, i * P:(i + 1) * P],
                                       com.S[:, (c * GC + i) * P:(c * GC + i + 1) * P], com.ident[:, :])
        last.then_inc(turned, 1)

    def weigh(pe, h, c):
        if c % (GRP // 2) == 0:
            pe.wait_ge(v_loaded[c // (GRP // 2)], h * 16 + 16)
        if c == 0:
            pe.wait_ge(out_taken, h + 1)
        pe.wait_ge(copied[by[c]], (h + 1) * n_by[by[c]] + rank[c])
        for i in range(GC):
            k = c * GC + i
            v = v_half[k // (CH // 2)][:, k % (CH // 2), :]
            if tiles > 1:
                at = k % tiles * (P // tiles)
                last = nc.tensor.matmul(out_ps[at:at + vw, 0:P], v, pT[c % ring][:, i * P:(i + 1) * P],
                                        start=(k < tiles), stop=(k >= CH - tiles))
                continue
            last = nc.tensor.matmul(out_ps[:, 0:vw], pT[c % ring][:, i * P:(i + 1) * P],
                                    v, start=(k == 0), stop=(k == CH - 1))
        last.then_inc(weighed, 1)

    def sum_tiles(pe, h):
        pe.wait_ge(parts_ready, h + 1)
        nc.tensor.matmul(sum_ps[:, 0:vw], out_parts[:, :], select[:, :], start=True, stop=True).then_inc(summed, 1)

    def tensor_head(pe, h, following):
        for c in range(GRP + lag):
            if c < GRP:
                turn(pe, h, c)
                if following:
                    scores(pe, h + 1, c)
            if c >= lag:
                weigh(pe, h, c - lag)
        if tiles > 1:
            sum_tiles(pe, h)

    def on_tensor(pe, before_scores=lambda pe, h: None):
        if tiles > 1:
            pe.wait_ge(cleared, 1)
        if more_scores:
            before_scores(pe, 0)
            for c in range(GRP):
                if ctx_loaded is not None and c % 2 == 0:
                    pe.wait_ge(ctx_loaded[c // 2], 16)
                scores(pe, 0, c)
        if heads > 1:
            with pe.Fori(0, heads - 1) as h:
                before_scores(pe, h + 1)
                tensor_head(pe, h, True)
        tensor_head(pe, heads - 1, False)

    def copy_turned(eng, copy, h, c):
        eng.wait_ge(turned, h * GRP + c + 1)
        eng.wait_ge(weighed, h * GRP + c + 1)
        copy(pT[c % ring][:, :], turned_ps[c % 2][:, 0:GW]).then_inc(copied[by[c]], 1)

    def take_scores(dve, h, c):
        if bias is not None and c % 2 == 0:
            dve.wait_ge(bias_loaded[c // 2], h * 16 + 16)
        for b in (2 * c, 2 * c + 1):
            if bias is not None:
                hold(dve, held_by_vector, scores_full, h * 2 * GRP + b + 1)
            else:
                dve.wait_ge(scores_full, h * 2 * GRP + b + 1)
            out, s = com.S[:, b * HB:(b + 1) * HB], scores_ps[b % 2][:, 0:HB]
            if bias is not None:
                nc.vector.tensor_tensor_reduce(out, s, bias_tile[b // 4][:, b % 4 * HB:(b % 4 + 1) * HB], 1.0, -3.4e38,
                                               ALU.add, ALU.max, rowmax[:, b:b + 1]).then_inc(scores_taken, 1)
            else:
                nc.vector.tensor_scalar(out, s, 1.0, -3.4e38, ALU.mult, ALU.max,
                                        accum_out=rowmax[:, b:b + 1]).then_inc(scores_taken, 1)

    def max_of(dve, h, rowmax_ap=None):
        if rowmax_ap is None:
            dve.wait_ge(scores_taken, (h + 1) * 2 * GRP + 2)
            rowmax_ap = rowmax[:, :]
        nc.vector.reduce_max(negmax[:, :], rowmax_ap, AX).then_inc(max_step, 1)
        dve.wait_ge(max_step, h + 1)
        nc.vector.tensor_scalar(negmax[:, :], negmax[:, :], -1.0, None, ALU.mult).then_inc(negmax_ready, 1)

    def leave(dve, h):
        dve.wait_ge(exp_done, h * GRP + GRP)
        nc.vector.reduce_sum(total[:, :], rowsum[:, :], AX).then_inc(rowsum_taken, 1)
        dve.wait_ge(rowsum_taken, h + 2)
        nc.vector.reciprocal(inverse[:, :], total[:, :]).then_inc(out_step, 1)
        dve.wait_ge(out_step, h + 1)
        dve.wait_ge(weighed, h * GRP + GRP + ring)
        product = out_ps
        if tiles > 1:
            product = sum_ps
            nc.vector.tensor_copy(out_parts[:, :], out_ps[:, 0:P]).then_inc(parts_ready, 1)
            dve.wait_ge(summed, h + 1)
        nc.vector.tensor_scalar(att[:, bass.ds(h * vw, vw)], product[:, 0:vw], inverse[:, 0:1], None,
                                ALU.mult).then_inc(out_taken, 1)

    def vector_head(dve, h, following):
        for c in range(GRP):
            if by[c] == "v":
                copy_turned(dve, nc.vector.tensor_copy, h, c)
            if following:
                take_scores(dve, h + 1, c)
        if following:
            max_of(dve, h + 1)
        leave(dve, h)

    def on_vector(dve):
        if tiles > 1:
            nc.vector.memset(out_ps[:, 0:P], 0.0)
            nc.vector.reduce_sum(select[:, :], com.ident[:, :].rearrange("p (a e) -> p e a", a=tiles)[:, 0:vw, :],
                                 AX).then_inc(cleared, 1)
        if more_scores:
            for c in range(GRP):
                take_scores(dve, 0, c)
            max_of(dve, 0)
        else:
            max_of(dve, 0, com.mx0[:, :])
        if heads > 1:
            with dve.Fori(0, heads - 1) as h:
                vector_head(dve, h, True)
        vector_head(dve, heads - 1, False)
        dve.wait_ge(out_taken, heads + 1)

    def scalar_head(act, h):
        for c in range(GRP + 2):
            if c < GRP:
                if c == 0:
                    act.wait_ge(negmax_ready, h + 1)
                    act.wait_ge(rowsum_taken, h + 1)
                s = com.S[:, c * GW:(c + 1) * GW]
                nc.scalar.activation(s, s, ACT.Exp, bias=negmax[:, 0:1], scale=1.0,
                                     accum_out=rowsum[:, c:c + 1]).then_inc(exp_done, 1)
            if c >= 2 and by[c - 2] == "s":
                copy_turned(act, nc.scalar.copy, h, c - 2)

    def on_scalar(act):
        if heads > 1:
            with act.Fori(0, heads) as h:
                scalar_head(act, h)
        else:
            scalar_head(act, 0)

    run.on_sync, run.on_tensor, run.on_vector, run.on_scalar = on_sync, on_tensor, on_vector, on_scalar
    return run


def l0_cross_attention(nc, com, a, scr):
    with phase(nc, "l0x") as ph:
        att = ph.sb("att", [P, D])
        attT = ph.sb("attT", [P, KT, P])
        wv = ph.sb("wv", [P, KT, D])
        run = head_stream(nc, ph, com, 1, D, att,
                          lambda h, j: a["ctx_1024"][0, j * (SK // 2):(j + 1) * (SK // 2), :]
                          .rearrange("(c p) d -> p c d", p=P))
        last_ps = ph.ps("last", [P, 512])
        wv_loaded, attT_in_psum, attT_ready, y_in_psum, x_ready = (
            ph.sem(s) for s in ("wv_loaded", "attT_in_psum", "attT_ready", "y_in_psum", "x_ready"))
        with nc.Block() as block:
            @block.sync
            def _(sp):
                run.on_sync(sp)
                sp.dma_start(wv[:, :, :], a["L0_xattn_W_v"].rearrange("(k p) n -> p k n", p=P)).then_inc(wv_loaded, 16)

            @block.tensor
            def _(pe):
                run.on_tensor(pe)
                pe.wait_ge(run.out_taken, 2)
                for k in range(KT):
                    last = nc.tensor.transpose(last_ps[:, k * P:(k + 1) * P], att[:, k * P:(k + 1) * P], com.ident[:, :])
                last.then_inc(attT_in_psum, 1)
                pe.wait_ge(attT_ready, 1)
                pe.wait_ge(wv_loaded, 16)
                for k in range(KT):
                    last = nc.tensor.matmul(last_ps[:, D:2 * D], attT[:, k, :], wv[:, k, :],
                                            start=(k == 0), stop=(k == KT - 1))
                last.then_inc(y_in_psum, 1)

            @block.vector
            def _(dve):
                run.on_vector(dve)
                dve.wait_ge(attT_in_psum, 1)
                nc.vector.tensor_copy(attT[:, :, :].rearrange("p k n -> p (k n)"), last_ps[:, 0:D]).then_inc(attT_ready, 1)
                dve.wait_ge(y_in_psum, 1)
                nc.vector.tensor_tensor(com.x[:, :], last_ps[:, D:2 * D], com.x[:, :], ALU.add).then_inc(x_ready, 1)
                dve.wait_ge(x_ready, 1)

            @block.scalar
            def _(act):
                run.on_scalar(act)


def cross_attention_16(nc, com, a, scr, layer):
    n = layer.lower()
    w = {k: a[f"{layer}_xattn_{k}"] for k in ("Wq", "bq", "bv", "Wo", "bo")}
    masked = layer == "L3"
    rows = STACK + 3 if masked else STACK
    k_dram, v_dram = scr.kparts["k" + n[1]], scr.v["v" + n[1]]
    with phase(nc, n + "x") as ph:
        att = ph.sb("att", [P, D])
        attT = ph.sb("attT", [P, KT, P])
        nat = {k: ph.sb("nat" + k, [P, KT, D]) for k in ("Wq", "Wo")}
        wT = {k: ph.sb("T" + k, [P, KT, D]) for k in nat}
        bb = {k: ph.sb("b_" + k, [P, D]) for k in ("bq", "bv", "bo")}
        qf, qp = ph.sb("qf", [P, D]), [ph.sb(f"qp{i}", [P, D], BF16) for i in range(3)]
        q_nat = ph.sb("q_nat", [P, HEADS, STACK], BF16)
        q_stack = ph.sb("q_stack", [rows, HEADS * P], BF16)
        k_half = [ph.sb(f"k_half{j}", [rows, SK // 2], BF16) for j in range(2)]

        def k_loads(h, j):
            cols = slice(j * (SK // 2), (j + 1) * (SK // 2))
            out, at = [], 0
            for piece in PIECES:
                out.append((k_half[j][at:at + 16, :], k_dram[piece, bass.ds(h * 16, 16), cols]))
                at += 16
            if masked:
                out.append((k_half[j][STACK:STACK + 3, :], scr.fill[0, :, cols]))
            return out

        fside = a["fside_Bx16xSxS2_0"]
        last_ps = ph.ps("last", [P, 512])
        run = head_stream(nc, ph, com, HEADS, 16, att,
                          lambda h, j: v_dram[bass.ds(h, 1), :, j * (CH // 2):(j + 1) * (CH // 2), :]
                          .rearrange("a p c e -> (a p) c e"),
                          q=q_stack, k_half=k_half, k_loads=k_loads,
                          bias=None if masked else lambda h, i: fside[0, bass.ds(h, 1), :, i * 2 * GW:(i + 1) * 2 * GW]
                          .rearrange("a p s -> (a p) s"), sum_ps=last_ps)
        qT_ps = last_ps[:, :].bitcast(BF16)
        norm_vector, norm_scalar, norm_tensor = token_norm(
            nc, ph, com, last_ps[:, 0:D].rearrange("p (k n) -> p k n", k=KT))
        loaded, wT_in_psum, wT_ready, q_in_psum, q_step, q_nat_ready, qT_in_psum, q_ready = (
            ph.sem(s) for s in ("loaded", "wT_in_psum", "wT_ready", "q_in_psum", "q_step", "q_nat_ready",
                                "qT_in_psum", "q_ready"))
        att_stored, att_read, att_ready, attT_in_psum, attT_ready, y_in_psum, x_step = (
            ph.sem(s) for s in ("att_stored", "att_read", "att_ready", "attT_in_psum", "attT_ready", "y_in_psum", "x_step"))
        with nc.Block() as block:
            @block.sync
            def _(sp):
                for k in nat:
                    sp.dma_start(nat[k][:, :, :], w[k].rearrange("(k p) n -> p k n", p=P)).then_inc(loaded, 16)
                for k in bb:
                    sp.dma_start(bb[k][:, :], w[k].partition_broadcast(P)).then_inc(loaded, 16)
                run.on_sync(sp)
                if not masked:
                    sp.wait_ge(att_ready, 1)
                    sp.dma_start(scr.att1.rearrange("h t e -> t h e"),
                                 att[:, :].rearrange("t (h e) -> t h e", e=16)).then_inc(att_stored, 16)
                    sp.wait_ge(att_stored, 16)
                    sp.dma_start(att[:, :], scr.att1.rearrange("h (a b) e -> (h a) (b e)", b=16)).then_inc(att_read, 16)

            @block.tensor
            def _(pe):
                norm_tensor(pe)
                pe.wait_ge(loaded, 16 * 5)
                for i, k_ in enumerate(nat):
                    if i:
                        pe.wait_ge(wT_ready, i)
                    for k in range(KT):
                        for o in range(KT):
                            last = nc.tensor.transpose(last_ps[:, (k * KT + o) * P:(k * KT + o + 1) * P],
                                                       nat[k_][:, o, k * P:(k + 1) * P], com.ident[:, :])
                    last.then_inc(wT_in_psum, 1)
                pe.wait_ge(wT_ready, 2)
                for k in range(KT):
                    last = nc.tensor.matmul(last_ps[:, 0:D], com.xnT[:, k, :], wT["Wq"][:, k, :],
                                            start=(k == 0), stop=(k == KT - 1))
                last.then_inc(q_in_psum, 1)
                pe.wait_ge(q_nat_ready, 1)
                for half in range(2):
                    if half:
                        pe.wait_ge(q_ready, 1)
                    for h in range(8):
                        last = nc.tensor.transpose(qT_ps[0:STACK, h * P:(h + 1) * P], q_nat[:, half * 8 + h, :],
                                                   com.identb[:, :])
                    last.then_inc(qT_in_psum, 1)
                pe.wait_ge(q_ready, 2)
                run.on_tensor(pe)
                pe.wait_ge(att_ready, 1)
                if not masked:
                    pe.wait_ge(att_read, 16)
                for k in range(KT):
                    last = nc.tensor.transpose(last_ps[:, k * P:(k + 1) * P], att[:, k * P:(k + 1) * P], com.ident[:, :])
                last.then_inc(attT_in_psum, 1)
                pe.wait_ge(attT_ready, 1)
                for k in range(KT):
                    last = nc.tensor.matmul(last_ps[:, D:2 * D], attT[:, k, :], wT["Wo"][:, k, :],
                                            start=(k == 0), stop=(k == KT - 1))
                last.then_inc(y_in_psum, 1)

            @block.vector
            def _(dve):
                norm_vector(dve)
                if masked:
                    nc.vector.memset(q_stack[STACK:STACK + 3, :], 1.0)
                for i, k in enumerate(nat):
                    dve.wait_ge(wT_in_psum, i + 1)
                    nc.vector.tensor_copy(wT[k][:, :, :].rearrange("p k n -> p (k n)"), last_ps[:, :]).then_inc(wT_ready, 1)
                dve.wait_ge(q_in_psum, 1)
                dve.wait_ge(loaded, 16 * 5)
                nc.vector.tensor_tensor(qf[:, :], last_ps[:, 0:D], bb["bq"][:, :], ALU.add).then_inc(q_step, 1)
                dve.wait_ge(q_step, 1)
                nc.vector.tensor_scalar(qf[:, :], qf[:, :], 0.25, None, ALU.mult).then_inc(q_step, 1)
                dve.wait_ge(q_step, 2)
                for i in range(3):
                    nc.vector.tensor_copy(qp[i][:, :], qf[:, :]).then_inc(q_step, 1)
                    dve.wait_ge(q_step, 2 * i + 3)
                    if i < 2:
                        nc.vector.tensor_tensor(qf[:, :], qf[:, :], qp[i][:, :], ALU.subtract).then_inc(q_step, 1)
                        dve.wait_ge(q_step, 2 * i + 4)
                for i, piece in enumerate(QPIECES):
                    last = nc.vector.tensor_copy(q_nat[:, :, i * 16:(i + 1) * 16],
                                                 qp[piece][:, :].rearrange("p (h e) -> p h e", e=16))
                last.then_inc(q_nat_ready, 1)
                for half in range(2):
                    dve.wait_ge(qT_in_psum, half + 1)
                    nc.vector.tensor_copy(q_stack[0:STACK, half * 8 * P:(half + 1) * 8 * P],
                                          qT_ps[0:STACK, :]).then_inc(q_ready, 1)
                run.on_vector(dve)
                nc.vector.tensor_tensor(att[:, :], att[:, :], bb["bv"][:, :], ALU.add).then_inc(att_ready, 1)
                dve.wait_ge(attT_in_psum, 1)
                nc.vector.tensor_copy(attT[:, :, :].rearrange("p k n -> p (k n)"), last_ps[:, 0:D]).then_inc(attT_ready, 1)
                nc.vector.tensor_tensor(com.x[:, :], com.x[:, :], bb["bo"][:, :], ALU.add).then_inc(x_step, 1)
                dve.wait_ge(x_step, 1)
                dve.wait_ge(y_in_psum, 1)
                nc.vector.tensor_tensor(com.x[:, :], last_ps[:, D:2 * D], com.x[:, :], ALU.add).then_inc(x_step, 1)
                dve.wait_ge(x_step, 2)

            @block.scalar
            def _(act):
                norm_scalar(act)
                run.on_scalar(act)


def l2_cross_attention(nc, com, a, scr):
    with phase(nc, "l2x") as ph:
        VW = 64
        W = HEADS * VW
        att = ph.sb("att", [P, W])
        ctxT = ph.sb("ctxT", [P, KT, SK])
        q_fold = ph.sb("q_fold", [P, HEADS * KT * P])
        q_cur = ph.sb("q_cur", [P, KT, P])
        last_ps = ph.ps("last", [P, 512])
        at = [0]

        def scratch(*shape):
            n = int(np.prod(shape))
            v = com.S[:, at[0]:at[0] + n]
            at[0] += n
            return v.rearrange("p (a b) -> p a b", a=shape[0])
        wq, wk, wkT, qT = scratch(KT, W), scratch(KT, W), scratch(8, D), scratch(8, P)
        at[0] = 0
        wo, attT = scratch(8, D), scratch(8, P)
        ctx_loaded = [ph.sem(f"ctx_loaded{i}") for i in range(GRP // 2)]
        run = head_stream(nc, ph, com, HEADS, VW, att,
                          lambda h, j: scr.v["v2"][bass.ds(h, 1), :, j * (CH // 2):(j + 1) * (CH // 2), :]
                          .rearrange("a p c e -> (a p) c e"),
                          ring=2, lag=1, q_cur=q_cur, ctxT=ctxT, ctx_loaded=ctx_loaded, sum_ps=last_ps)
        norm_vector, norm_scalar, norm_tensor = token_norm(
            nc, ph, com, last_ps[:, 0:D].rearrange("p (k n) -> p k n", k=KT))
        loaded, front_in_psum, front_ready, q_cur_ready = (
            ph.sem(s) for s in ("loaded", "front_in_psum", "front_ready", "q_cur_ready"))
        wo_loaded, attT_in_psum, attT_ready, y_in_psum, x_ready = (
            ph.sem(s) for s in ("wo_loaded", "attT_in_psum", "attT_ready", "y_in_psum", "x_ready"))
        banks = run.turned_ps
        with nc.Block() as block:
            @block.sync
            def _(sp):
                for t, src in ((wq, a["L2_xattn_Wq"]), (wk, a["L2_xattn_Wk"])):
                    sp.dma_start(t, src.rearrange("(k p) n -> p k n", p=P)).then_inc(loaded, 16)
                for i in range(GRP // 2):
                    cols = slice(i * 2 * GW, (i + 1) * 2 * GW)
                    sp.dma_start(ctxT[:, :, cols], scr.ctxT[:, :, cols]).then_inc(ctx_loaded[i], 16)
                run.on_sync(sp)
                sp.wait_ge(run.turned, HEADS * GRP)
                sp.dma_start(wo, a["L2_xattn_Wo"].rearrange("(k p) n -> p k n", p=P)).then_inc(wo_loaded, 16)

            @block.tensor
            def _(pe):
                norm_tensor(pe)
                pe.wait_ge(loaded, 32)
                for r in range(2):
                    for t in range(8):
                        e, k = r * 4 + t // 2, t % 2
                        last = nc.tensor.transpose(banks[r][:, t * P:(t + 1) * P], wk[:, k, e * P:(e + 1) * P],
                                                   com.ident[:, :])
                    last.then_inc(front_in_psum, 1)
                pe.wait_ge(front_ready, 1)
                for e in range(8):
                    for k in range(KT):
                        last = nc.tensor.matmul(banks[0][:, e * P:(e + 1) * P], wq[:, k, e * P:(e + 1) * P],
                                                com.xnT[:, k, :], start=(k == 0), stop=(k == KT - 1))
                last.then_inc(front_in_psum, 1)
                pe.wait_ge(front_ready, 3)
                for r in range(4):
                    if r:
                        pe.wait_ge(front_ready, r + 2)
                    for t in range(8):
                        h, k = r * 4 + t // 2, t % 2
                        rows = slice(h % 2 * VW, h % 2 * VW + VW)
                        at_col = h % 2 * 512 + t // 4 * KT * P + k * P
                        last = nc.tensor.matmul(banks[(r + 1) % 2][:, at_col:at_col + P],
                                                wkT[rows, h // 2, k * P:(k + 1) * P], qT[rows, h // 2, :],
                                                start=True, stop=True)
                    last.then_inc(front_in_psum, 1)
                pe.wait_ge(front_ready, 7)
                run.on_tensor(pe, before_scores=lambda pe, h: pe.wait_ge(q_cur_ready, h + 1))
                pe.wait_ge(run.out_taken, HEADS + 1)
                for e in range(8):
                    last = nc.tensor.transpose(banks[0][:, e * P:(e + 1) * P], att[:, e * P:(e + 1) * P], com.ident[:, :])
                last.then_inc(attT_in_psum, 1)
                pe.wait_ge(attT_ready, 1)
                pe.wait_ge(wo_loaded, 16)
                for e in range(8):
                    last = nc.tensor.matmul(last_ps[:, 0:D], attT[:, e, :], wo[:, e, :], start=(e == 0), stop=(e == 7))
                last.then_inc(y_in_psum, 1)

            @block.gpsimd
            def _(pool):
                def take_query(h):
                    nc.gpsimd.tensor_copy(q_cur[:, :, :].rearrange("p k n -> p (k n)"),
                                          q_fold[:, bass.ds(h * KT * P, KT * P)]).then_inc(q_cur_ready, 1)
                pool.wait_ge(front_ready, 7)
                take_query(0)
                with pool.Fori(1, HEADS) as h:
                    pool.wait_ge(run.scores_full, h * 2 * GRP)
                    take_query(h)

            @block.vector
            def _(dve):
                norm_vector(dve)
                for r in range(2):
                    dve.wait_ge(front_in_psum, r + 1)
                    nc.vector.tensor_copy(wkT[:, r * 4:(r + 1) * 4, :].rearrange("p a b -> p (a b)"),
                                          banks[r][:, :]).then_inc(front_ready, 1)
                dve.wait_ge(front_in_psum, 3)
                nc.vector.tensor_copy(qT.rearrange("p a b -> p (a b)"), banks[0][:, :]).then_inc(front_ready, 1)
                for r in range(4):
                    dve.wait_ge(front_in_psum, r + 4)
                    nc.vector.tensor_scalar(q_fold[:, r * 1024:(r + 1) * 1024]
                                            .rearrange("p (pair odd n) -> p odd pair n", odd=2, n=KT * P),
                                            banks[(r + 1) % 2][:, :]
                                            .rearrange("p (odd pair n) -> p odd pair n", odd=2, n=KT * P), 0.125, None,
                                            ALU.mult).then_inc(front_ready, 1)
                run.on_vector(dve)
                dve.wait_ge(attT_in_psum, 1)
                nc.vector.tensor_copy(attT.rearrange("p a b -> p (a b)"), banks[0][:, :]).then_inc(attT_ready, 1)
                dve.wait_ge(y_in_psum, 1)
                nc.vector.tensor_tensor(com.x[:, :], last_ps[:, 0:D], com.x[:, :], ALU.add).then_inc(x_ready, 1)
                dve.wait_ge(x_ready, 1)

            @block.scalar
            def _(act):
                norm_scalar(act)
                run.on_scalar(act)



EU = 4
FILL = -3.0e38
MARK = 3.0e38


def gate_steps(nc, ph, com, E, top, eps=0.0, tau=None):
    lg, top8 = ph.sb("logits", [P, E + 8]), ph.sb("top8", [P, 8])
    marked, gates = ph.sb("marked", [P, E + 8]), ph.sb("gates", [P, E])
    prob, one = ph.sb("prob", [P, E + 8]), [ph.sb(f"gate_col{i}", [P, 1]) for i in range(4)]
    big, total, inverse, wsum = one
    gate_step, gate_exp, gates_ready = ph.sem("gate_step"), ph.sem("gate_exp"), ph.sem("gates_ready")

    def on_vector(dve, logits_ps, bias=None):
        n = [0]

        def then(ins):
            n[0] += 1
            ins.then_inc(gate_step, 1)
            dve.wait_ge(gate_step, n[0])
        nc.vector.memset(lg[:, E:E + 8], FILL)
        nc.vector.memset(prob[:, E:E + 8], FILL)
        if bias is None:
            then(nc.vector.tensor_copy(lg[:, 0:E], logits_ps))
        else:
            then(nc.vector.tensor_tensor(lg[:, 0:E], logits_ps, bias, ALU.add))
        if tau is not None:
            then(nc.vector.tensor_scalar(lg[:, 0:E], lg[:, 0:E], 1.0 / tau, None, ALU.mult))
        then(nc.vector.reduce_max(big[:, :], lg[:, 0:E], AX))
        then(nc.vector.tensor_scalar(big[:, :], big[:, :], -1.0, None, ALU.mult))
        dve.wait_ge(gate_exp, 1)
        if tau is None:
            then(nc.vector.reciprocal(inverse[:, :], total[:, :]))
            then(nc.vector.tensor_scalar(prob[:, 0:E], prob[:, 0:E], inverse[:, 0:1], None, ALU.mult))
        ranked = lg if tau is not None else prob
        then(nc.vector.max(top8[:, :], ranked[:, :]))
        then(nc.vector.memset(top8[:, top:8], FILL))
        then(nc.vector.match_replace(marked[:, :], top8[:, :], ranked[:, :], MARK))
        then(nc.vector.tensor_scalar(marked[:, 0:E], marked[:, 0:E], MARK, None, ALU.is_equal))
        then(nc.vector.tensor_tensor(marked[:, 0:E], marked[:, 0:E], prob[:, 0:E], ALU.mult))
        then(nc.vector.reduce_sum(wsum[:, :], marked[:, 0:E], AX))
        if eps:
            then(nc.vector.tensor_scalar(wsum[:, :], wsum[:, :], eps, None, ALU.add))
        then(nc.vector.reciprocal(wsum[:, :], wsum[:, :]))
        nc.vector.tensor_scalar(gates[:, :], marked[:, 0:E], wsum[:, 0:1], None, ALU.mult).then_inc(gates_ready, 1)
        dve.wait_ge(gates_ready, 1)

    def on_scalar(act):
        act.wait_ge(gate_step, 3 if tau is None else 4)
        nc.scalar.activation(prob[:, 0:E], lg[:, 0:E], ACT.Exp, bias=big[:, 0:1], scale=1.0,
                             accum_out=total[:, 0:1]).then_inc(gate_exp, 1)

    return on_vector, on_scalar, gates, gates_ready


def experts(nc, com, a, name, E, top, router, ups, down, hid, act_func, act_at, lin_at=None, U=1, T=4, eps=0.0,
            tau=None, router_bias=None, up_bias=None, down_bias=None, shared=None):
    two = lin_at is not None
    cols = sum(u.shape[-1] for u in ups)
    n_bias = cols // P
    HT = hid // P
    with phase(nc, name) as ph:
        S = ph.sem
        up_w = [ph.sb(f"up{j}", [P, KT, cols]) for j in range(EU)]
        down_w = [ph.sb(f"down{j}", [P, HT, D]) for j in range(EU)]
        h_act = [ph.sb(f"h_act{i}", [P, 512]) for i in range(2)] if two else None
        h = [ph.sb(f"h{i}", [P, 512]) for i in range(2)]
        acc = ph.sb("acc", [P, D])
        wr = ph.sb("wr", [P, KT, E])
        act_ps = [ph.ps(f"act{i}", [P, 512]) for i in range(2)]
        lin_ps = [ph.ps(f"lin{i}", [P, 512]) for i in range(2)] if two else None
        out_ps = [ph.ps(f"out{i}", [P, 512]) for i in range(2)]
        misc_ps = ph.ps("misc", [P, 512])
        rb = ph.sb("rb", [P, E]) if router_bias is not None else None
        n_rows = E * n_bias
        if up_bias is not None:
            blocks = [(r, min(n_rows, r + P) - r) for r in range(0, n_rows, P)]
            bias_nat = ph.sb("bias_nat", [P, len(blocks), P])
            biasT = ph.sb("biasT", [P, n_rows])
        if down_bias is not None:
            db, gatesT = ph.sb("db", [E, D]), ph.sb("gatesT", [E, P])
        n_shared = 0
        if shared is not None:
            n_shared = 1
            s_hid, s_ups, s_down, s_bias, s_down_bias, s_lin = shared
            s_cols = sum(u.shape[-1] for u in s_ups)
            s_up, s_dn = ph.sb("s_up", [P, KT, s_cols]), ph.sb("s_down", [P, s_hid // P, D])
            if s_bias is not None:
                sb_nat, sbT = ph.sb("sb_nat", [8, P]), ph.sb("sbT", [P, 8])
                sdb = ph.sb("sdb", [P, D])
        gate_vector, gate_scalar, gates, gates_ready = gate_steps(nc, ph, com, E, top, eps, tau)
        norm_vector, norm_scalar, norm_tensor = token_norm(
            nc, ph, com, misc_ps[:, 0:D].rearrange("p (k n) -> p k n", k=KT))
        small_loaded, shared_loaded, held = S("small_loaded"), S("shared_loaded"), S("held")
        w_loaded = [S(f"w_loaded{j}") for j in range(EU)]
        logits_full, bias_in_psum, bias_ready, gatesT_in_psum, gatesT_ready, start_in_psum, acc_started = (
            S(s) for s in ("logits_full", "bias_in_psum", "bias_ready", "gatesT_in_psum", "gatesT_ready",
                           "start_in_psum", "acc_started"))
        up_full, act_done, h_ready, down_done, acc_done = (
            S(s) for s in ("up_full", "act_done", "h_ready", "down_done", "acc_done"))
        x_ready = S("x_ready")
        n_dma = len(ups) + 1
        n_small = 1 + (router_bias is not None) + (down_bias is not None)
        if up_bias is not None:
            n_small += len(blocks)
        if shared is not None and s_bias is not None:
            n_small += 2

        with nc.Block() as block:
            @block.sync
            def _(sp):
                for s in (h_ready, down_done, acc_done):
                    sp.sem_inc(s, 2)
                sp.dma_start(wr[:, :, :], router.rearrange("(k p) n -> p k n", p=P)).then_inc(small_loaded, 16)
                if router_bias is not None:
                    sp.dma_start(rb[:, :], router_bias.partition_broadcast(P)).then_inc(small_loaded, 16)
                if down_bias is not None:
                    sp.dma_start(db[:, :], down_bias).then_inc(small_loaded, 16)
                if up_bias is not None:
                    rows = up_bias.rearrange("e (t p) -> (e t) p", p=P)
                    for i, (r, n) in enumerate(blocks):
                        sp.dma_start(bias_nat[0:n, i, :], rows[r:r + n, :]).then_inc(small_loaded, 16)
                if shared is not None:
                    if s_bias is not None:
                        sp.dma_start(sb_nat[:, :], s_bias.rearrange("(t p) -> t p", p=P)).then_inc(small_loaded, 16)
                        sp.dma_start(sdb[:, :], s_down_bias.partition_broadcast(P)).then_inc(small_loaded, 16)
                    c0 = 0
                    for u in s_ups:
                        sp.dma_start(s_up[:, :, c0:c0 + u.shape[-1]],
                                     u.rearrange("(k p) n -> p k n", p=P)).then_inc(shared_loaded, 16)
                        c0 += u.shape[-1]
                    sp.dma_start(s_dn[:, :, :], s_down.rearrange("(k p) n -> p k n", p=P)).then_inc(shared_loaded, 16)

                def load(e, j):
                    c0 = 0
                    for u in ups:
                        n = u.shape[-1]
                        sp.dma_start(up_w[j][:, :, c0:c0 + n], u[bass.ds(e, 1)]
                                     .rearrange("a (k p) n -> p (a k) n", p=P)).then_inc(w_loaded[j], 16)
                        c0 += n
                    sp.dma_start(down_w[j][:, :, :], down[bass.ds(e, 1)]
                                 .rearrange("a (k p) n -> p (a k) n", p=P)).then_inc(w_loaded[j], 16)
                for j in range(EU):
                    load(j, j)
                with sp.Fori(1, E // EU) as g:
                    for j in range(EU):
                        hold(sp, held, down_done, n_shared + ((g - 1) * EU + j + 1) * U + 2)
                        load(g * EU + j, j)

            def up(pe, n, r, w, u, t_n, act0, lin0, loaded, count):
                if loaded is not None:
                    pe.wait_ge(loaded, count)
                pe.wait_ge(h_ready, n + 1)
                for bank, first in ((act_ps, act0),) + (((lin_ps, lin0),) if two else ()):
                    for t in range(t_n):
                        c = first + (u * t_n + t) * P
                        for k in range(KT):
                            last = nc.tensor.matmul(bank[r][:, t * P:(t + 1) * P], w[:, k, c:c + P], com.xnT[:, k, :],
                                                    start=(k == 0), stop=(k == KT - 1))
                last.then_inc(up_full, 1)

            def down_product(pe, n, r, w, m, o, u, u_n, t_n):
                if u == 0:
                    pe.wait_ge(acc_done, m + 1)
                pe.wait_ge(h_ready, n + 1 + 2)
                for t in range(t_n):
                    last = nc.tensor.matmul(out_ps[o][:, 0:D], h[r][:, t * P:(t + 1) * P], w[:, u * t_n + t, :],
                                            start=(u == 0 and t == 0), stop=(u == u_n - 1 and t == t_n - 1))
                last.then_inc(down_done, 1)

            local = [(j, u) for j in range(EU) for u in range(U)]

            @block.tensor
            def _(pe):
                norm_tensor(pe)
                pe.wait_ge(small_loaded, 16 * n_small)
                for k in range(KT):
                    last = nc.tensor.matmul(misc_ps[:, 256:256 + E], com.xnT[:, k, :], wr[:, k, :],
                                            start=(k == 0), stop=(k == KT - 1))
                last.then_inc(logits_full, 1)
                if up_bias is not None:
                    pe.wait_ge(acc_started, 1)
                    for i, (r, n) in enumerate(blocks):
                        last = nc.tensor.transpose(out_ps[0][:, r:r + n], bias_nat[0:n, i, :], com.ident[0:n, 0:n])
                    if shared is not None:
                        last = nc.tensor.transpose(out_ps[0][:, n_rows:n_rows + 8], sb_nat[:, :], com.ident[0:8, 0:8])
                    last.then_inc(bias_in_psum, 1)
                    pe.wait_ge(bias_ready, 1)
                if shared is not None:
                    up(pe, 0, 0, s_up, 0, s_hid // P, s_lin[0], s_lin[1], shared_loaded, 16 * (len(s_ups) + 1))
                    down_product(pe, 0, 0, s_dn, 0, 0, 0, 1, s_hid // P)
                with pe.Fori(0, E // EU) as g:
                    for i, (j, u) in enumerate(local):
                        n = n_shared + g * EU * U + i
                        up(pe, n, (n_shared + i) % 2, up_w[j], u, T, act_at, lin_at,
                           w_loaded[j] if u == 0 else None, (g + 1) * 16 * n_dma)
                        if i:
                            pj, pu = local[i - 1]
                            down_product(pe, n - 1, (n_shared + i - 1) % 2, down_w[pj], n_shared + g * EU + pj,
                                         (n_shared + pj) % 2, pu, U, T)
                    down_product(pe, n, (n_shared + i) % 2, down_w[j], n_shared + g * EU + j,
                                 (n_shared + j) % 2, u, U, T)
                if down_bias is not None:
                    pe.wait_ge(gates_ready, 1)
                    nc.tensor.transpose(misc_ps[0:E, 0:P], gates[:, :], com.ident[:, :]).then_inc(gatesT_in_psum, 1)
                    pe.wait_ge(gatesT_ready, 1)
                    nc.tensor.matmul(misc_ps[:, 256:512], gatesT[:, :], db[:, :], start=True,
                                     stop=True).then_inc(start_in_psum, 1)

            def activate(act, n, r, t_n, bias_at):
                act.wait_ge(up_full, n + 1)
                if two:
                    act.wait_ge(h_ready, n + 1)
                else:
                    act.wait_ge(down_done, n + 1)
                dst = h_act[r] if two else h[r]
                if bias_at is None:
                    last = nc.scalar.activation(dst[:, 0:t_n * P], act_ps[r][:, 0:t_n * P], act_func)
                else:
                    for t in range(t_n):
                        last = nc.scalar.activation(dst[:, t * P:(t + 1) * P], act_ps[r][:, t * P:(t + 1) * P], act_func,
                                                    bias=bias_at(t), scale=1.0)
                last.then_inc(act_done if two else h_ready, 1)

            def bias_col(g, j, u, first):
                if up_bias is None:
                    return None
                return lambda t: biasT[:, bass.ds((g * EU + j) * n_bias + first // P + u * T + t, 1)]

            @block.scalar
            def _(act):
                norm_scalar(act)
                gate_scalar(act)
                if up_bias is not None:
                    act.wait_ge(bias_ready, 1)
                if shared is not None:
                    activate(act, 0, 0, s_hid // P, None if s_bias is None else
                             (lambda t: sbT[:, s_lin[0] // P + t:s_lin[0] // P + t + 1]))
                with act.Fori(0, E // EU) as g:
                    for i, (j, u) in enumerate(local):
                        activate(act, n_shared + g * EU * U + i, (n_shared + i) % 2, T, bias_col(g, j, u, act_at))

            def hidden(dve, n, r, t_n, bias_at):
                if not two:
                    return
                dve.wait_ge(act_done, n + 1)
                dve.wait_ge(down_done, n + 1)
                if bias_at is None:
                    last = nc.vector.tensor_tensor(h[r][:, 0:t_n * P], lin_ps[r][:, 0:t_n * P], h_act[r][:, 0:t_n * P],
                                                   ALU.mult)
                else:
                    for t in range(t_n):
                        c = slice(t * P, (t + 1) * P)
                        last = nc.vector.scalar_tensor_tensor(out=h[r][:, c], in0=lin_ps[r][:, c], scalar=bias_at(t),
                                                              in1=h_act[r][:, c], op0=ALU.add, op1=ALU.mult)
                last.then_inc(h_ready, 1)

            def accumulate(dve, m, o, last_unit, gate):
                dve.wait_ge(down_done, last_unit + 1 + 2)
                dve.wait_ge(acc_done, m + 2)
                dve.wait_ge(acc_started, 1)
                if gate is None:
                    nc.vector.tensor_tensor(acc[:, :], out_ps[o][:, 0:D], acc[:, :], ALU.add).then_inc(acc_done, 1)
                else:
                    nc.vector.scalar_tensor_tensor(out=acc[:, :], in0=out_ps[o][:, 0:D], scalar=gate, in1=acc[:, :],
                                                   op0=ALU.mult, op1=ALU.add).then_inc(acc_done, 1)

            @block.vector
            def _(dve):
                norm_vector(dve)
                dve.wait_ge(small_loaded, 16 * n_small)
                if shared is not None and s_bias is not None:
                    nc.vector.tensor_tensor(acc[:, :], com.x[:, :], sdb[:, :], ALU.add).then_inc(acc_started, 1)
                else:
                    nc.vector.tensor_copy(acc[:, :], com.x[:, :]).then_inc(acc_started, 1)
                dve.wait_ge(logits_full, 1)
                gate_vector(dve, misc_ps[:, 256:256 + E], rb[:, :] if router_bias is not None else None)
                if up_bias is not None:
                    dve.wait_ge(bias_in_psum, 1)
                    if shared is not None:
                        nc.vector.tensor_copy(sbT[:, :], out_ps[0][:, n_rows:n_rows + 8])
                    nc.vector.tensor_copy(biasT[:, :], out_ps[0][:, 0:n_rows]).then_inc(bias_ready, 1)
                    dve.wait_ge(bias_ready, 1)
                if shared is not None:
                    hidden(dve, 0, 0, s_hid // P, None if s_bias is None else
                           (lambda t: sbT[:, s_lin[1] // P + t:s_lin[1] // P + t + 1]))
                    accumulate(dve, 0, 0, 0, None)
                with dve.Fori(0, E // EU) as g:
                    def weighed(j):
                        accumulate(dve, n_shared + g * EU + j, (n_shared + j) % 2, n_shared + (g * EU + j + 1) * U - 1,
                                   gates[:, bass.ds(g * EU + j, 1)])
                    for i, (j, u) in enumerate(local):
                        hidden(dve, n_shared + g * EU * U + i, (n_shared + i) % 2, T,
                               bias_col(g, j, u, lin_at) if two else None)
                        if u == 0 and j:
                            weighed(j - 1)
                    weighed(EU - 1)
                dve.wait_ge(acc_done, 2 + n_shared + E)
                if down_bias is not None:
                    dve.wait_ge(gatesT_in_psum, 1)
                    nc.vector.tensor_copy(gatesT[:, :], misc_ps[0:E, 0:P]).then_inc(gatesT_ready, 1)
                    dve.wait_ge(start_in_psum, 1)
                    nc.vector.tensor_tensor(com.x[:, :], misc_ps[:, 256:512], acc[:, :], ALU.add).then_inc(x_ready, 1)
                else:
                    nc.vector.tensor_copy(com.x[:, :], acc[:, :]).then_inc(x_ready, 1)
                dve.wait_ge(x_ready, 1)


def l0_experts(nc, com, a):
    experts(nc, com, a, "l0f", 8, 2, a["L0_ffn_Wr"], [a["L0_ffn_Wg"], a["L0_ffn_Wu"]], a["L0_ffn_Wd"], 512, ACT.Silu,
            0, 512, eps=1e-20, shared=(512, [a["L0_ffn_Sg"], a["L0_ffn_Su"]], a["L0_ffn_Sd"], None, None, (0, 512)))


def l2_experts(nc, com, a):
    experts(nc, com, a, "l2f", 16, 4, a["L2_ffn_router_w"], [a["L2_ffn_w1"]], a["L2_ffn_w2"], 512, ACT.Gelu, 0,
            router_bias=a["L2_ffn_router_b"], up_bias=a["L2_ffn_b1"], down_bias=a["L2_ffn_b2"])


def l3_experts(nc, com, a):
    experts(nc, com, a, "l3f", 12, 2, a["L3_ffn_Wr"], [a["L3_ffn_We1"]], a["L3_ffn_We2"], 768, ACT.Gelu, 768, 0,
            U=2, T=3, tau=1.5, router_bias=a["L3_ffn_br"], up_bias=a["L3_ffn_be1"], down_bias=a["L3_ffn_be2"],
            shared=(512, [a["L3_ffn_Ws1"]], a["L3_ffn_Ws2"], a["L3_ffn_bs1"], a["L3_ffn_bs2"], (512, 0)))


def l1_experts(nc, com, a):
    E, OT = a["L1_ffn_We"].shape[0], a["L1_ffn_We"].shape[1] // P
    with phase(nc, "l1f") as ph:
        S = ph.sem
        w_nat = ph.sb("w_nat", [P, E, OT, D])
        wT = ph.sb("wT", [P, E, KT * D])
        wg, bg = ph.sb("wg", [P, KT, E]), ph.sb("bg", [P, E])
        be, gatesT = ph.sb("be", [E, D]), ph.sb("gatesT", [E, P])
        turned_ps = [ph.ps(f"turned{i}", [P, 512]) for i in range(2)]
        y_ps = [ph.ps(f"y{i}", [P, 512]) for i in range(2)]
        misc_ps = ph.ps("misc", [P, 512])
        small_loaded = S("small_loaded")
        w_loaded = [S(f"w_loaded{e}") for e in range(E)]
        logits_full, turned, wT_ready, y_full, acc_done = (
            S(s) for s in ("logits_full", "turned", "wT_ready", "y_full", "acc_done"))
        gatesT_in_psum, gatesT_ready, bias_full = (S(s) for s in ("gatesT_in_psum", "gatesT_ready", "bias_full"))
        gate_vector, gate_scalar, gates, gates_ready = gate_steps(nc, ph, com, E, 2)
        norm_vector, norm_scalar, norm_tensor = token_norm(
            nc, ph, com, misc_ps[:, 0:D].rearrange("p (k n) -> p k n", k=KT))
        with nc.Block() as block:
            @block.sync
            def _(sp):
                sp.dma_start(wg[:, :, :], a["L1_ffn_Wg"].rearrange("(k p) n -> p k n", p=P)).then_inc(small_loaded, 16)
                sp.dma_start(bg[:, :], a["L1_ffn_bg"].partition_broadcast(P)).then_inc(small_loaded, 16)
                sp.dma_start(be[:, :], a["L1_ffn_be"]).then_inc(small_loaded, 16)
                for e in range(E):
                    sp.dma_start(w_nat[:, e, :, :],
                                 a["L1_ffn_We"][e].rearrange("(t p) n -> p t n", p=P)).then_inc(w_loaded[e], 16)

            @block.tensor
            def _(pe):
                def turn_weights(e):
                    pe.wait_ge(w_loaded[e], 16)
                    if e >= 2:
                        pe.wait_ge(wT_ready, e - 1)
                    for k in range(KT):
                        for o in range(OT):
                            last = nc.tensor.transpose(turned_ps[e % 2][:, k * D + o * P:k * D + (o + 1) * P],
                                                       w_nat[:, e, o, k * P:(k + 1) * P], com.ident[:, :])
                    last.then_inc(turned, 1)
                turn_weights(0)
                norm_tensor(pe)
                pe.wait_ge(small_loaded, 48)
                for k in range(KT):
                    last = nc.tensor.matmul(misc_ps[:, D:D + E], com.xnT[:, k, :], wg[:, k, :],
                                            start=(k == 0), stop=(k == KT - 1))
                last.then_inc(logits_full, 1)
                for e in range(E):
                    if e + 1 < E:
                        turn_weights(e + 1)
                    pe.wait_ge(wT_ready, e + 1)
                    if e >= 2:
                        pe.wait_ge(acc_done, e - 1)
                    for k in range(KT):
                        last = nc.tensor.matmul(y_ps[e % 2][:, 0:D], com.xnT[:, k, :], wT[:, e, k * D:(k + 1) * D],
                                                start=(k == 0), stop=(k == KT - 1))
                    last.then_inc(y_full, 1)
                pe.wait_ge(gates_ready, 1)
                nc.tensor.transpose(misc_ps[0:E, 0:P], gates[:, :], com.ident[:, :]).then_inc(gatesT_in_psum, 1)
                pe.wait_ge(gatesT_ready, 1)
                nc.tensor.matmul(misc_ps[:, D:2 * D], gatesT[:, :], be[:, :], start=True, stop=True).then_inc(bias_full, 1)

            @block.scalar
            def _(act):
                norm_scalar(act)
                gate_scalar(act)
                for e in range(E):
                    act.wait_ge(turned, e + 1)
                    nc.scalar.copy(wT[:, e, :], turned_ps[e % 2][:, :]).then_inc(wT_ready, 1)

            @block.vector
            def _(dve):
                norm_vector(dve)
                dve.wait_ge(small_loaded, 48)
                dve.wait_ge(logits_full, 1)
                gate_vector(dve, misc_ps[:, D:D + E], bg[:, :])
                for e in range(E):
                    dve.wait_ge(y_full, e + 1)
                    if e:
                        dve.wait_ge(acc_done, e)
                    nc.vector.scalar_tensor_tensor(out=com.x[:, :], in0=y_ps[e % 2][:, 0:D], scalar=gates[:, e:e + 1],
                                                   in1=com.x[:, :], op0=ALU.mult, op1=ALU.add).then_inc(acc_done, 1)
                dve.wait_ge(gatesT_in_psum, 1)
                nc.vector.tensor_copy(gatesT[:, :], misc_ps[0:E, 0:P]).then_inc(gatesT_ready, 1)
                dve.wait_ge(bias_full, 1)
                dve.wait_ge(acc_done, E)
                nc.vector.tensor_tensor(com.x[:, :], misc_ps[:, D:2 * D], com.x[:, :], ALU.add).then_inc(acc_done, 1)
                dve.wait_ge(acc_done, E + 1)



class FewKeys:

    def __init__(self, nc, ph, com, keys, width, qm, kT, v, mask=None, floor=None):
        self.nc, self.ph, self.com, self.keys, self.width = nc, ph, com, keys, width
        self.qm, self.kT, self.v, self.mask, self.floor = qm, kT, v, mask, floor
        self.per = 512 // keys
        self.rounds = HEADS // self.per
        self.tile_heads = P // width
        self.wide = width == 64
        S = ph.sem
        self.s_ps = [ph.ps(f"s{i}", [P, 512]) for i in range(2)]
        self.t_ps = [ph.ps(f"t{i}", [P, 512]) for i in range(2)]
        self.o_ps = [ph.ps(f"o{i}", [P, 512]) for i in range(2)]
        self.e = [ph.sb(f"e{i}", [P, 512]) for i in range(2)]
        self.pT = [ph.sb(f"pT{i}", [P, 512]) for i in range(2)]
        self.big, self.total = ph.sb("big", [P, HEADS]), ph.sb("total", [P, HEADS])
        self.attT = ph.sb("attT", [P, HEADS * width // P, P])
        if not self.wide:
            self.att = ph.sb("att", [P, HEADS * width])
        (self.scores_full, self.masked, self.max_step, self.exp_done, self.inverse_ready, self.probs_ready, self.turned,
         self.pT_ready, self.out_full, self.att_ready, self.att_turned, self.attT_ready) = (S(s) for s in (
             "scores_full", "masked", "max_step", "exp_done", "inverse_ready", "probs_ready", "turned", "pT_ready",
             "out_full", "att_ready", "att_turned", "attT_ready"))

    def on_tensor(self, pe):
        nc = self.nc

        def scores(r):
            if r >= 2:
                pe.wait_ge(self.exp_done, r - 1)
            for j in range(self.per):
                h = r * self.per + j
                last = nc.tensor.matmul(self.s_ps[r % 2][:, j * self.keys:(j + 1) * self.keys], self.qm[:, h, :],
                                        self.kT[:, h // self.tile_heads, :], start=True, stop=True)
            last.then_inc(self.scores_full, 1)

        def turn(r):
            pe.wait_ge(self.probs_ready, r + 1)
            if r >= 2:
                pe.wait_ge(self.pT_ready, r - 1)
            for b in range(4):
                last = nc.tensor.transpose(self.t_ps[r % 2][:, b * P:(b + 1) * P], self.e[r % 2][:, b * P:(b + 1) * P],
                                           self.com.ident[:, :])
            last.then_inc(self.turned, 1)

        def weigh(r):
            pe.wait_ge(self.pT_ready, r + 1)
            kt = self.keys // P
            w = self.width
            for j in range(self.per):
                h = r * self.per + j
                for s in range(kt):
                    probs = self.pT[r % 2][:, (j * kt + s) * P:(j * kt + s + 1) * P]
                    values = self.v[:, s, h * w:(h + 1) * w]
                    if self.wide:
                        last = nc.tensor.matmul(self.o_ps[h // 8][h % 2 * w:(h % 2 + 1) * w, h // 2 % 4 * P:(h // 2 % 4 + 1) * P],
                                                values, probs, start=(s == 0), stop=(s == kt - 1))
                    else:
                        last = nc.tensor.matmul(self.o_ps[0][:, h * w:(h + 1) * w], probs, values,
                                                start=(s == 0), stop=(s == kt - 1))
            last.then_inc(self.out_full, 1)

        scores(0)
        for r in range(self.rounds):
            if r + 1 < self.rounds:
                scores(r + 1)
            turn(r)
            if r:
                weigh(r - 1)
        weigh(self.rounds - 1)
        if not self.wide:
            pe.wait_ge(self.att_ready, 1)
            for t in range(KT):
                last = nc.tensor.transpose(self.o_ps[1][:, t * P:(t + 1) * P], self.att[:, t * P:(t + 1) * P],
                                           self.com.ident[:, :])
            last.then_inc(self.att_turned, 1)
        pe.wait_ge(self.attT_ready, 2 if self.wide else 1)

    def on_vector(self, dve):
        nc, per, keys = self.nc, self.per, self.keys
        steps = 0

        def maximum(r):
            dve.wait_ge(self.scores_full, r + 1)
            cols = slice(r * per, (r + 1) * per)
            src = self.s_ps[r % 2]
            if self.mask is not None:
                if r >= 2:
                    dve.wait_ge(self.turned, r - 1)
                    dve.wait_ge(self.exp_done, r - 1)
                src = self.e[r % 2]
                nc.vector.tensor_tensor(self.e[r % 2][:, :].rearrange("p (h s) -> p h s", h=per),
                                        self.s_ps[r % 2][:, :].rearrange("p (h s) -> p h s", h=per),
                                        self.mask[:, :].unsqueeze(1).to_broadcast([P, per, keys]),
                                        ALU.min).then_inc(self.masked, 1)
                dve.wait_ge(self.masked, r + 1)
            nc.vector.reduce_max(self.big[:, cols], src[:, :].rearrange("p (h s) -> p h s", h=per),
                                 AX).then_inc(self.max_step, 1)
            dve.wait_ge(self.max_step, 2 * r + 1)
            nc.vector.tensor_scalar(self.big[:, cols], self.big[:, cols], -1.0, None, ALU.mult).then_inc(self.max_step, 1)

        def normalise(r):
            cols = slice(r * per, (r + 1) * per)
            dve.wait_ge(self.exp_done, r + 1)
            nc.vector.reciprocal(self.total[:, cols], self.total[:, cols]).then_inc(self.inverse_ready, 1)
            dve.wait_ge(self.inverse_ready, r + 1)
            e = self.e[r % 2][:, :].rearrange("p (h s) -> p h s", h=per)
            nc.vector.tensor_tensor(e, e, self.total[:, cols].unsqueeze(2).to_broadcast([P, per, keys]),
                                    ALU.mult).then_inc(self.probs_ready, 1)

        maximum(0)
        for r in range(self.rounds):
            if r + 1 < self.rounds:
                maximum(r + 1)
            normalise(r)
        if self.wide:
            for i in range(2):
                dve.wait_ge(self.out_full, self.rounds // 2 * (i + 1))
                nc.vector.tensor_copy(self.attT[:, i * 4:(i + 1) * 4, :].rearrange("p t n -> p (t n)"),
                                      self.o_ps[i][:, :]).then_inc(self.attT_ready, 1)
        else:
            dve.wait_ge(self.out_full, self.rounds)
            nc.vector.tensor_copy(self.att[:, :], self.o_ps[0][:, 0:HEADS * self.width]).then_inc(self.att_ready, 1)
            dve.wait_ge(self.att_turned, 1)
            nc.vector.tensor_copy(self.attT[:, :, :].rearrange("p t n -> p (t n)"),
                                  self.o_ps[1][:, 0:D]).then_inc(self.attT_ready, 1)

    def on_scalar(self, act):
        nc, per, keys = self.nc, self.per, self.keys

        def exponents(r):
            act.wait_ge(self.max_step, 2 * r + 2)
            if r >= 2:
                act.wait_ge(self.turned, r - 1)
            src = self.s_ps[r % 2] if self.mask is None else self.e[r % 2]
            for j in range(per):
                h = r * per + j
                last = nc.scalar.activation(self.e[r % 2][:, j * keys:(j + 1) * keys], src[:, j * keys:(j + 1) * keys],
                                            ACT.Exp, bias=self.big[:, h:h + 1], scale=1.0,
                                            accum_out=self.total[:, h:h + 1])
            last.then_inc(self.exp_done, 1)

        def copy(r):
            act.wait_ge(self.turned, r + 1)
            if r >= 2:
                act.wait_ge(self.out_full, r - 1)
            nc.scalar.copy(self.pT[r % 2][:, :], self.t_ps[r % 2][:, :]).then_inc(self.pT_ready, 1)

        exponents(0)
        for r in range(self.rounds):
            if r + 1 < self.rounds:
                exponents(r + 1)
            copy(r)


def make_head_rows(nc, pool, rows, n, width, done):
    nc.gpsimd.memset(rows[:, :], 1.0).then_inc(done, 1)
    pool.wait_ge(done, 1)
    nc.gpsimd.affine_select(out=rows[:, :], in_=rows[:, :], compare_op=ALU.is_ge, fill=0.0, base=0,
                            pattern=[[-width, n]], channel_multiplier=1).then_inc(done, 1)
    pool.wait_ge(done, 2)
    nc.gpsimd.affine_select(out=rows[:, :], in_=rows[:, :], compare_op=ALU.is_ge, fill=0.0, base=width - 1,
                            pattern=[[width, n]], channel_multiplier=-1).then_inc(done, 1)


def l3_attention(nc, com, a):
    W, window, fill, n = 16, 64, -1.0e30, P // 16
    with phase(nc, "l3a") as ph:
        S = ph.sem
        w = {m: ph.sb("w" + m, [P, KT, D]) for m in "qkvo"}
        bq, bk = ph.sb("bq", [P, KT]), ph.sb("bk", [P, KT])
        bv, bo = ph.sb("bv", [P, D]), ph.sb("bo", [P, D])
        rows, mask = ph.sb("rows", [P, n]), ph.sb("mask", [P, P])
        qT, kT = ph.sb("qT", [P, KT, P]), ph.sb("kT", [P, KT, P])
        qm, v = ph.sb("qm", [P, HEADS, P]), ph.sb("v", [P, 1, D])
        fk = FewKeys(nc, ph, com, P, W, qm, kT, v, mask)
        front_ps = [ph.ps(f"front{i}", [P, 512]) for i in range(2)]
        norm_vector, norm_scalar, norm_tensor = token_norm(
            nc, ph, com, front_ps[0][:, 0:D].rearrange("p (k n) -> p k n", k=KT))
        loaded, rows_made, mask_made, front_full, front_step, ready, y_full, x_step = (
            S(s) for s in ("loaded", "rows_made", "mask_made", "front_full", "front_step", "ready", "y_full", "x_step"))
        with nc.Block() as block:
            @block.sync
            def _(sp):
                for m in "qkvo":
                    sp.dma_start(w[m][:, :, :], a["L3_attn_W" + m].rearrange("(k p) n -> p k n", p=P)).then_inc(loaded, 16)
                for t, src in ((bq, a["L3_attn_bq"]), (bk, a["L3_attn_bk"])):
                    sp.dma_start(t[:, :], src.rearrange("(k p) -> p k", p=P),
                                 allow_slow_non_contiguous=True).then_inc(loaded, 16)
                for t, src in ((bv, a["L3_attn_bv"]), (bo, a["L3_attn_bo"])):
                    sp.dma_start(t[:, :], src.partition_broadcast(P)).then_inc(loaded, 16)

            @block.gpsimd
            def _(pool):
                make_head_rows(nc, pool, rows, n, W, rows_made)
                nc.gpsimd.memset(mask[:, :], -FILL).then_inc(mask_made, 1)
                pool.wait_ge(mask_made, 1)
                nc.gpsimd.affine_select(out=mask[:, :], in_=mask[:, :], compare_op=ALU.is_ge, fill=fill, base=0,
                                        pattern=[[-1, P]], channel_multiplier=1).then_inc(mask_made, 1)
                pool.wait_ge(mask_made, 2)
                nc.gpsimd.affine_select(out=mask[:, :], in_=mask[:, :], compare_op=ALU.is_ge, fill=fill,
                                        base=window - 1, pattern=[[1, P]], channel_multiplier=-1).then_inc(mask_made, 1)

            @block.tensor
            def _(pe):
                norm_tensor(pe)
                pe.wait_ge(loaded, 16 * 8)
                for m, at in (("q", 0), ("k", D)):
                    for t in range(KT):
                        for k in range(KT):
                            last = nc.tensor.matmul(front_ps[1][:, at + t * P:at + (t + 1) * P],
                                                    w[m][:, k, t * P:(t + 1) * P], com.xnT[:, k, :],
                                                    start=(k == 0), stop=(k == KT - 1))
                    last.then_inc(front_full, 1)
                for k in range(KT):
                    last = nc.tensor.matmul(front_ps[0][:, D:2 * D], com.xnT[:, k, :], w["v"][:, k, :],
                                            start=(k == 0), stop=(k == KT - 1))
                last.then_inc(front_full, 1)
                pe.wait_ge(ready, 1 + KT + KT)
                fk.on_tensor(pe)
                for k in range(KT):
                    last = nc.tensor.matmul(front_ps[0][:, 0:D], fk.attT[:, k, :], w["o"][:, k, :],
                                            start=(k == 0), stop=(k == KT - 1))
                last.then_inc(y_full, 1)

            @block.vector
            def _(dve):
                norm_vector(dve)
                dve.wait_ge(loaded, 16 * 8)
                dve.wait_ge(front_full, 2)
                for t in range(KT):
                    nc.vector.tensor_scalar(qT[:, t, :], front_ps[1][:, t * P:(t + 1) * P], bq[:, t:t + 1], 0.25,
                                            ALU.add, ALU.mult).then_inc(front_step, 1)
                dve.wait_ge(front_step, KT)
                dve.wait_ge(rows_made, 3)
                for t in range(KT):
                    nc.vector.tensor_tensor(qm[:, t * n:(t + 1) * n, :], qT[:, t, :].unsqueeze(1).to_broadcast([P, n, P]),
                                            rows[:, :].unsqueeze(2).to_broadcast([P, n, P]), ALU.mult).then_inc(ready, 1)
                for t in range(KT):
                    nc.vector.tensor_scalar(kT[:, t, :], front_ps[1][:, D + t * P:D + (t + 1) * P], bk[:, t:t + 1], None,
                                            ALU.add).then_inc(ready, 1)
                dve.wait_ge(front_full, 3)
                nc.vector.tensor_tensor(v[:, 0, :], front_ps[0][:, D:2 * D], bv[:, :], ALU.add).then_inc(ready, 1)
                nc.vector.tensor_tensor(com.x[:, :], com.x[:, :], bo[:, :], ALU.add).then_inc(x_step, 1)
                dve.wait_ge(mask_made, 3)
                fk.on_vector(dve)
                dve.wait_ge(y_full, 1)
                dve.wait_ge(x_step, 1)
                nc.vector.tensor_tensor(com.x[:, :], front_ps[0][:, 0:D], com.x[:, :], ALU.add).then_inc(x_step, 1)
                dve.wait_ge(x_step, 2)

            @block.scalar
            def _(act):
                norm_scalar(act)
                fk.on_scalar(act)


def l2_attention(nc, com, a):
    W, LD = 64, a["L2_attn_Wkv_down"].shape[1]
    AW = HEADS * W
    NT = AW // P
    with phase(nc, "l2a") as ph:
        S = ph.sem
        wq, wd = ph.sb("wq", [P, KT, AW]), ph.sb("wd", [P, KT, LD])
        wk, wv = ph.sb("wk", [LD, AW]), ph.sb("wv", [LD, AW])
        wo = ph.sb("wo", [P, NT, D])
        rows, mask = ph.sb("rows", [P, 2]), ph.sb("mask", [P, P])
        latT = ph.sb("latT", [LD, P])
        kT = ph.sb("kT", [P, NT, P])
        qm, v = ph.sb("qm", [P, HEADS, P]), ph.sb("v", [P, 1, AW])
        fk = FewKeys(nc, ph, com, P, W, qm, kT, v, mask)
        front_ps = [ph.ps(f"front{i}", [P, 512]) for i in range(2)]
        norm_vector, norm_scalar, norm_tensor = token_norm(
            nc, ph, com, front_ps[0][:, 0:D].rearrange("p (k n) -> p k n", k=KT))
        loaded, wo_loaded, rows_made, mask_made, latent_full, latT_ready, q_full, k_full, v_full = (
            S(s) for s in ("loaded", "wo_loaded", "rows_made", "mask_made", "latent_full", "latT_ready", "q_full",
                           "k_full", "v_full"))
        qm_ready, kT_ready, v_ready, y_full, x_ready = (
            S(s) for s in ("qm_ready", "kT_ready", "v_ready", "y_full", "x_ready"))
        q_ps, k_ps, v_ps = fk.s_ps, fk.o_ps, fk.t_ps
        with nc.Block() as block:
            @block.sync
            def _(sp):
                sp.dma_start(wd[:, :, :], a["L2_attn_Wkv_down"].rearrange("(k p) n -> p k n", p=P)).then_inc(loaded, 16)
                for t, name in ((wk, "L2_attn_Wk_up"), (wv, "L2_attn_Wv_up")):
                    sp.dma_start(t[:, :], a[name].rearrange("c h e -> c (h e)")).then_inc(loaded, 16)
                sp.dma_start(wq[:, :, :], a["L2_attn_Wq"].rearrange("(k p) h e -> p k (h e)", p=P)).then_inc(loaded, 16)
                sp.dma_start(wo[:, :, :], a["L2_attn_Wout"].rearrange("h e n -> (h e) n")
                             .rearrange("(k p) n -> p k n", p=P)).then_inc(wo_loaded, 16)

            @block.gpsimd
            def _(pool):
                make_head_rows(nc, pool, rows, 2, W, rows_made)
                nc.gpsimd.memset(mask[:, :], -FILL).then_inc(mask_made, 1)
                pool.wait_ge(mask_made, 1)
                nc.gpsimd.affine_select(out=mask[:, :], in_=mask[:, :], compare_op=ALU.is_ge,
                                        fill=float(np.finfo(np.float32).min), base=0, pattern=[[-1, P]],
                                        channel_multiplier=1).then_inc(mask_made, 1)

            @block.tensor
            def _(pe):
                norm_tensor(pe)
                pe.wait_ge(loaded, 16 * 4)
                for k in range(KT):
                    last = nc.tensor.matmul(front_ps[1][0:LD, 0:P], wd[:, k, :], com.xnT[:, k, :],
                                            start=(k == 0), stop=(k == KT - 1))
                last.then_inc(latent_full, 1)
                for t in range(NT):
                    for k in range(KT):
                        last = nc.tensor.matmul(q_ps[t // 4][:, t % 4 * P:(t % 4 + 1) * P], wq[:, k, t * P:(t + 1) * P],
                                                com.xnT[:, k, :], start=(k == 0), stop=(k == KT - 1))
                    if t % 4 == 3:
                        last.then_inc(q_full, 1)
                pe.wait_ge(latT_ready, 1)
                for t in range(NT):
                    last = nc.tensor.matmul(k_ps[t // 4][:, t % 4 * P:(t % 4 + 1) * P], wk[:, t * P:(t + 1) * P],
                                            latT[:, :], start=True, stop=True)
                last.then_inc(k_full, 1)
                for i in range(2):
                    last = nc.tensor.matmul(v_ps[i][:, :], latT[:, :], wv[:, i * 512:(i + 1) * 512], start=True, stop=True)
                last.then_inc(v_full, 1)
                pe.wait_ge(qm_ready, 2 * 2)
                pe.wait_ge(kT_ready, 2)
                pe.wait_ge(v_ready, 2)
                fk.on_tensor(pe)
                pe.wait_ge(wo_loaded, 16)
                for k in range(NT):
                    last = nc.tensor.matmul(front_ps[0][:, 0:D], fk.attT[:, k, :], wo[:, k, :],
                                            start=(k == 0), stop=(k == NT - 1))
                last.then_inc(y_full, 1)

            @block.vector
            def _(dve):
                norm_vector(dve)
                dve.wait_ge(latent_full, 1)
                nc.vector.tensor_copy(latT[:, :], front_ps[1][0:LD, 0:P]).then_inc(latT_ready, 1)
                dve.wait_ge(rows_made, 3)
                for i in range(2):
                    dve.wait_ge(q_full, i + 1)
                    for j in range(2):
                        nc.vector.tensor_scalar(qm[:, i * 8:(i + 1) * 8, :].rearrange("p (t two) n -> p two t n", two=2)[:, j],
                                                q_ps[i][:, :].rearrange("p (t n) -> p t n", n=P), rows[:, j:j + 1], 0.125,
                                                ALU.mult, ALU.mult).then_inc(qm_ready, 1)
                dve.wait_ge(mask_made, 2)
                fk.on_vector(dve)
                dve.wait_ge(y_full, 1)
                nc.vector.tensor_tensor(com.x[:, :], front_ps[0][:, 0:D], com.x[:, :], ALU.add).then_inc(x_ready, 1)
                dve.wait_ge(x_ready, 1)

            @block.scalar
            def _(act):
                norm_scalar(act)
                act.wait_ge(k_full, 1)
                for i in range(2):
                    nc.scalar.copy(kT[:, i * 4:(i + 1) * 4, :].rearrange("p t n -> p (t n)"), k_ps[i][:, :]).then_inc(kT_ready, 1)
                act.wait_ge(v_full, 1)
                for i in range(2):
                    nc.scalar.copy(v[:, 0, i * 512:(i + 1) * 512], v_ps[i][:, :]).then_inc(v_ready, 1)
                fk.on_scalar(act)


def l1_state_space(nc, com, a):
    N = a["L1_attn_A_log"].shape[1]
    RING = 4
    with phase(nc, "l1a") as ph:
        S = ph.sem
        nat = {m: ph.sb("nat_" + m, [P, KT, D]) for m in ("in", "out")}
        wT = {m: ph.sb("T_" + m, [P, KT, D]) for m in ("in", "out")}
        b_in, skip, dt = (ph.sb(m, [P, KT]) for m in ("b_in", "skip", "dt"))
        b_out = ph.sb("b_out", [P, D])
        a_log, b_st, c_st = (ph.sb(m, [P, KT, N]) for m in ("a_log", "b_st", "c_st"))
        rate, weight = ph.sb("rate", [P, KT, N]), ph.sb("weight", [P, KT, N])
        steps_i, steps = ph.sb("steps_i", [P, P], I32), ph.sb("steps", [P, P])
        powers = [[ph.sb(f"powers{i}{t}", [P, P]) for t in range(KT)] for i in range(2)]
        k_rev = ph.sb("k_rev", [P, KT, P])
        uT, yT = ph.sb("uT", [P, KT, P]), ph.sb("yT", [P, KT, P])
        products = ph.sb("products", [P, RING, KT, P])
        turned_ps = [ph.ps(f"turned{i}", [P, 512]) for i in range(2)]
        u_ps, y_ps, misc_ps = ph.ps("u", [P, 512]), ph.ps("y", [P, 512]), ph.ps("misc", [P, 512])
        norm_vector, norm_scalar, norm_tensor = token_norm(
            nc, ph, com, misc_ps[:, 0:D].rearrange("p (k n) -> p k n", k=KT))
        loaded, state_loaded, turned, wT_ready, u_full, u_ready = (
            S(s) for s in ("loaded", "state_loaded", "turned", "wT_ready", "u_full", "u_ready"))
        decay_ready, weight_step, rate_ready, steps_step, k_step, powers_ready = (
            S(s) for s in ("decay_ready", "weight_step", "rate_ready", "steps_step", "k_step", "powers_ready"))
        conv_done, y_ready, out_full, x_step = (S(s) for s in ("conv_done", "y_ready", "out_full", "x_step"))
        with nc.Block() as block:
            @block.sync
            def _(sp):
                sp.sem_inc(k_step, 2 * KT)
                for t, name in ((a_log, "A_log"), (b_st, "B"), (c_st, "C")):
                    sp.dma_start(t[:, :, :], a["L1_attn_" + name].rearrange("(k p) n -> p k n", p=P)).then_inc(state_loaded, 16)
                for t, name in ((dt, "dt"), (b_in, "bin_"), (skip, "Dp")):
                    sp.dma_start(t[:, :], a["L1_attn_" + name].rearrange("(k p) -> p k", p=P),
                                 allow_slow_non_contiguous=True).then_inc(state_loaded, 16)
                for m in ("in", "out"):
                    sp.dma_start(nat[m][:, :, :], a["L1_attn_W" + m].rearrange("(k p) n -> p k n", p=P)).then_inc(loaded, 16)
                sp.dma_start(b_out[:, :], a["L1_attn_bout"].partition_broadcast(P)).then_inc(loaded, 16)

            @block.gpsimd
            def _(pool):
                nc.gpsimd.iota(steps_i[:, :], pattern=[[-1, P]], base=P - 1, channel_multiplier=0).then_inc(steps_step, 1)
                pool.wait_ge(steps_step, 1)
                nc.gpsimd.tensor_copy(steps[:, :], steps_i[:, :]).then_inc(steps_step, 1)
                nc.gpsimd.memset(k_rev[:, :, :], 0.0).then_inc(steps_step, 1)
                pool.wait_ge(steps_step, 3)

            @block.tensor
            def _(pe):
                pe.wait_ge(loaded, 48)
                for i, m in enumerate(("in", "out")):
                    for k in range(KT):
                        for o in range(KT):
                            last = nc.tensor.transpose(turned_ps[i][:, k * D + o * P:k * D + (o + 1) * P],
                                                       nat[m][:, o, k * P:(k + 1) * P], com.ident[:, :])
                    last.then_inc(turned, 1)
                norm_tensor(pe)
                pe.wait_ge(wT_ready, 1)
                for t in range(KT):
                    for k in range(KT):
                        last = nc.tensor.matmul(u_ps[:, t * P:(t + 1) * P], wT["in"][:, k, t * P:(t + 1) * P],
                                                com.xnT[:, k, :], start=(k == 0), stop=(k == KT - 1))
                last.then_inc(u_full, 1)
                pe.wait_ge(wT_ready, 2)
                pe.wait_ge(y_ready, KT)
                for k in range(KT):
                    last = nc.tensor.matmul(y_ps[:, 0:D], yT[:, k, :], wT["out"][:, k, :],
                                            start=(k == 0), stop=(k == KT - 1))
                last.then_inc(out_full, 1)

            @block.scalar
            def _(act):
                norm_scalar(act)
                for i, m in enumerate(("in", "out")):
                    act.wait_ge(turned, i + 1)
                    nc.scalar.copy(wT[m][:, :, :].rearrange("p k n -> p (k n)"), turned_ps[i][:, :]).then_inc(wT_ready, 1)
                act.wait_ge(state_loaded, 16 * 6)
                nc.scalar.activation(a_log[:, :, :], a_log[:, :, :], ACT.Exp, bias=0.0, scale=-1.0).then_inc(decay_ready, 1)
                act.wait_ge(rate_ready, KT)
                act.wait_ge(steps_step, 3)
                with act.Fori(0, N // 2) as n:
                    for i in range(2):
                        for t in range(KT):
                            act.wait_ge(k_step, n * 2 * KT + i * KT + t + 1)
                            nc.scalar.activation(powers[i][t][:, :], steps[:, :], ACT.Exp, bias=0.0,
                                                 scale=rate[:, t, bass.ds(n * 2 + i, 1)]).then_inc(powers_ready, 1)

            @block.vector
            def _(dve):
                norm_vector(dve)
                dve.wait_ge(state_loaded, 16 * 6)
                dve.wait_ge(decay_ready, 1)
                for t in range(KT):
                    nc.vector.tensor_scalar(rate[:, t, :], a_log[:, t, :], dt[:, t:t + 1], -1.0,
                                            ALU.mult, ALU.mult).then_inc(rate_ready, 1)
                    nc.vector.tensor_scalar(b_st[:, t, :], b_st[:, t, :], dt[:, t:t + 1], None,
                                            ALU.mult).then_inc(weight_step, 1)
                dve.wait_ge(weight_step, KT)
                nc.vector.tensor_tensor(weight[:, :, :], c_st[:, :, :], b_st[:, :, :], ALU.mult).then_inc(weight_step, 1)
                dve.wait_ge(u_full, 1)
                for t in range(KT):
                    nc.vector.tensor_scalar(uT[:, t, :], u_ps[:, t * P:(t + 1) * P], b_in[:, t:t + 1], None,
                                            ALU.add).then_inc(u_ready, 1)
                dve.wait_ge(loaded, 48)
                nc.vector.tensor_tensor(com.x[:, :], com.x[:, :], b_out[:, :], ALU.add).then_inc(x_step, 1)
                dve.wait_ge(weight_step, KT + 1)
                dve.wait_ge(steps_step, 3)
                with dve.Fori(0, N // 2) as n:
                    for i in range(2):
                        for t in range(KT):
                            dve.wait_ge(powers_ready, n * 2 * KT + i * KT + t + 1)
                            dve.wait_ge(k_step, (n * 2 + i) * KT + t + 1 + KT)
                            nc.vector.scalar_tensor_tensor(out=k_rev[:, t, :], in0=powers[i][t][:, :],
                                                           scalar=weight[:, t, bass.ds(n * 2 + i, 1)],
                                                           in1=k_rev[:, t, :], op0=ALU.mult,
                                                           op1=ALU.add).then_inc(k_step, 1)
                dve.wait_ge(k_step, N * KT + 2 * KT)
                dve.wait_ge(u_ready, KT)
                for l in range(P):
                    for t in range(KT):
                        if l >= RING:
                            dve.wait_ge(conv_done, (l - RING) * KT + t + 1)
                        nc.vector.tensor_tensor_reduce(out=products[:, l % RING, t, 0:l + 1],
                                                       in0=k_rev[:, t, P - 1 - l:P], in1=uT[:, t, 0:l + 1],
                                                       op0=ALU.mult, op1=ALU.add, scale=1.0, scalar=0.0,
                                                       accum_out=yT[:, t, l:l + 1]).then_inc(conv_done, 1)
                dve.wait_ge(conv_done, P * KT)
                for t in range(KT):
                    nc.vector.scalar_tensor_tensor(out=yT[:, t, :], in0=uT[:, t, :], scalar=skip[:, t:t + 1],
                                                   in1=yT[:, t, :], op0=ALU.mult, op1=ALU.add).then_inc(y_ready, 1)
                dve.wait_ge(out_full, 1)
                dve.wait_ge(x_step, 1)
                nc.vector.tensor_tensor(com.x[:, :], y_ps[:, 0:D], com.x[:, :], ALU.add).then_inc(x_step, 1)
                dve.wait_ge(x_step, 2)


def l0_attention(nc, com, a):
    W = 64
    AW = HEADS * W
    NT, ST = AW // P, a["L0_attn_source_embedding"].shape[0] // P
    TILES = ST + 1
    Q = ST
    with phase(nc, "l0a") as ph:
        S = ph.sem
        emb = {m: ph.sb("emb_" + m, [P, ST, D]) for m in "kv"}
        embT = {m: ph.sb("embT_" + m, [P, KT, ST * P]) for m in "kv"}
        w = {m: ph.sb("w" + m, [P, KT, AW]) for m in "kqv"}
        wo = ph.sb("wo", [P, NT, D])
        bias = {m: ph.sb("b" + m, [P, AW]) for m in "kqv"}
        bo, ln_g, ln_b = (ph.sb(m, [P, D]) for m in ("bo", "ln_g", "ln_b"))
        rows = ph.sb("rows", [P, 2])
        feature, low = ph.sb("feature", [P, TILES, AW]), [ph.sb(f"low{i}", [P, AW]) for i in range(2)]
        inverse = ph.sb("inverse", [P, TILES, HEADS])
        kT, v = ph.sb("kT", [P, NT, ST * P]), ph.sb("v", [P, ST, AW])
        qm = ph.sb("qm", [P, HEADS, P])
        res, stats, mv, rstd = ph.sb("res", [P, D]), ph.sb("stats2", [P, 6]), ph.sb("mv2", [P, 2]), ph.sb("rstd2", [P, 1])
        fk = FewKeys(nc, ph, com, ST * P, W, qm, kT, v)
        front_ps = [ph.ps(f"front{i}", [P, 512]) for i in range(2)]
        product_ps = [fk.s_ps, front_ps]
        turned_ps = [fk.t_ps, fk.o_ps]
        value_ps = fk.t_ps + fk.o_ps
        norm_vector, norm_scalar, norm_tensor = token_norm(
            nc, ph, com, front_ps[0][:, 0:D].rearrange("p (k n) -> p k n", k=KT))
        emb_loaded = {m: S(f"emb_{m}_loaded") for m in "kv"}
        w_loaded = {m: S(f"w{m}_loaded") for m in "kqv"}
        small_loaded, rows_made, emb_turned, embT_ready, value_full, v_ready = (
            S(s) for s in ("small_loaded", "rows_made", "emb_turned", "embT_ready", "value_full", "v_ready"))
        product_full, z_ready, low_ready, exp_low, high_ready, feature_ready, square_ready, squares_summed = (
            S(s) for s in ("product_full", "z_ready", "low_ready", "exp_low", "high_ready", "feature_ready",
                           "square_ready", "squares_summed"))
        root_taken, inverse_step, unit_ready, unit_turned, unitT_ready, y_full, out_step, out_root = (
            S(s) for s in ("root_taken", "inverse_step", "unit_ready", "unit_turned", "unitT_ready", "y_full",
                           "out_step", "out_root"))
        with nc.Block() as block:
            @block.sync
            def _(sp):
                for m, name in (("k", "source"), ("v", "value")):
                    sp.dma_start(emb[m][:, :, :], a[f"L0_attn_{name}_embedding"]
                                 .rearrange("(t p) n -> p t n", p=P)).then_inc(emb_loaded[m], 16)
                    sp.dma_start(w[m][:, :, :], a["L0_attn_W" + m].rearrange("(k p) n -> p k n", p=P)).then_inc(w_loaded[m], 16)
                    sp.dma_start(bias[m][:, :], a["L0_attn_b" + m].partition_broadcast(P)).then_inc(w_loaded[m], 16)
                sp.dma_start(w["q"][:, :, :], a["L0_attn_Wq"].rearrange("(k p) n -> p k n", p=P)).then_inc(w_loaded["q"], 16)
                sp.dma_start(bias["q"][:, :], a["L0_attn_bq"].partition_broadcast(P)).then_inc(w_loaded["q"], 16)
                for t, name in ((bo, "bo"), (ln_g, "ln_g"), (ln_b, "ln_b")):
                    sp.dma_start(t[:, :], a["L0_attn_" + name].partition_broadcast(P)).then_inc(small_loaded, 16)
                sp.dma_start(wo[:, :, :], a["L0_attn_Wo"].rearrange("(k p) n -> p k n", p=P)).then_inc(small_loaded, 16)

            @block.tensor
            def _(pe):
                for i, m in enumerate("kv"):
                    pe.wait_ge(emb_loaded[m], 16)
                    for k in range(KT):
                        for t in range(ST):
                            last = nc.tensor.transpose(turned_ps[i][k][:, t * P:(t + 1) * P],
                                                       emb[m][:, t, k * P:(k + 1) * P], com.ident[:, :])
                        last.then_inc(emb_turned, 1)
                norm_tensor(pe)
                for i in range(TILES):
                    m = "q" if i == Q else "k"
                    pe.wait_ge(w_loaded[m], 32)
                    if i == 0:
                        pe.wait_ge(embT_ready, KT)
                    if i >= 2:
                        pe.wait_ge(z_ready, 2 * (i - 1))
                    for half in range(2):
                        for k in range(KT):
                            lhs = com.xnT[:, k, :] if i == Q else embT["k"][:, k, i * P:(i + 1) * P]
                            last = nc.tensor.matmul(product_ps[i % 2][half][:, :], lhs,
                                                    w[m][:, k, half * 512:(half + 1) * 512],
                                                    start=(k == 0), stop=(k == KT - 1))
                        last.then_inc(product_full, 1)
                pe.wait_ge(w_loaded["v"], 32)
                pe.wait_ge(embT_ready, 2 * KT)
                for j in range(2 * ST):
                    if j >= 4:
                        pe.wait_ge(v_ready, j - 3)
                    t, half = j // 2, j % 2
                    for k in range(KT):
                        last = nc.tensor.matmul(value_ps[j % 4][:, :], embT["v"][:, k, t * P:(t + 1) * P],
                                                w["v"][:, k, half * 512:(half + 1) * 512],
                                                start=(k == 0), stop=(k == KT - 1))
                    last.then_inc(value_full, 1)
                pe.wait_ge(v_ready, 2 * ST)
                for i in range(TILES):
                    pe.wait_ge(unit_ready, i + 1)
                    if i >= 2:
                        pe.wait_ge(unitT_ready, 2 * (i - 1))
                    for t in range(NT):
                        last = nc.tensor.transpose(turned_ps[i % 2][t // 4][:, t % 4 * P:(t % 4 + 1) * P],
                                                   feature[:, i, t * P:(t + 1) * P], com.ident[:, :])
                        if t % 4 == 3:
                            last.then_inc(unit_turned, 1)
                pe.wait_ge(unitT_ready, 2 * ST + 4)
                fk.on_tensor(pe)
                pe.wait_ge(small_loaded, 64)
                for k in range(NT):
                    last = nc.tensor.matmul(front_ps[0][:, 0:D], fk.attT[:, k, :], wo[:, k, :],
                                            start=(k == 0), stop=(k == NT - 1))
                last.then_inc(y_full, 1)

            def square(pool, i):
                pool.wait_ge(feature_ready, i + 1)
                nc.gpsimd.tensor_tensor(low[i % 2][:, :], feature[:, i, :], feature[:, i, :], ALU.mult).then_inc(square_ready, 1)

            @block.gpsimd
            def _(pool):
                make_head_rows(nc, pool, rows, 2, W, rows_made)
                for i in range(TILES):
                    pool.wait_ge(z_ready, 2 * (i + 1))
                    if i >= 2:
                        pool.wait_ge(squares_summed, i - 1)
                    nc.gpsimd.tensor_scalar(low[i % 2][:, :], feature[:, i, :], 0.0, None, ALU.min).then_inc(low_ready, 1)
                    if i:
                        square(pool, i - 1)
                square(pool, TILES - 1)

            @block.scalar
            def _(act):
                norm_scalar(act)
                for i, m in enumerate("kv"):
                    for k in range(KT):
                        act.wait_ge(emb_turned, i * KT + k + 1)
                        nc.scalar.copy(embT[m][:, k, :], turned_ps[i][k][:, :]).then_inc(embT_ready, 1)
                for i in range(TILES):
                    act.wait_ge(low_ready, i + 1)
                    nc.scalar.activation(low[i % 2][:, :], low[i % 2][:, :], ACT.Exp).then_inc(exp_low, 1)
                act.wait_ge(squares_summed, TILES)
                nc.scalar.activation(inverse[:, :, :], inverse[:, :, :], ACT.Sqrt).then_inc(root_taken, 1)
                for i in range(ST):
                    for half in range(2):
                        act.wait_ge(unit_turned, 2 * i + half + 1)
                        nc.scalar.copy(kT[:, half * 4:(half + 1) * 4, i * P:(i + 1) * P],
                                       turned_ps[i % 2][half][:, :].rearrange("p (t n) -> p t n", n=P)
                                       ).then_inc(unitT_ready, 1)
                fk.on_scalar(act)
                act.wait_ge(out_step, 5)
                nc.scalar.activation(rstd[:, :], rstd[:, :], ACT.Sqrt).then_inc(out_root, 1)

            @block.vector
            def _(dve):
                def shift(i):
                    m = "q" if i == Q else "k"
                    dve.wait_ge(w_loaded[m], 32)
                    for half in range(2):
                        c = slice(half * 512, (half + 1) * 512)
                        dve.wait_ge(product_full, 2 * i + half + 1)
                        nc.vector.tensor_tensor(feature[:, i, c], product_ps[i % 2][half][:, :], bias[m][:, c],
                                                ALU.add).then_inc(z_ready, 1)

                def elu(i):
                    dve.wait_ge(low_ready, i + 1)
                    nc.vector.tensor_scalar(feature[:, i, :], feature[:, i, :], 0.0, -1.0, ALU.max, ALU.add).then_inc(high_ready, 1)
                    dve.wait_ge(high_ready, i + 1)
                    dve.wait_ge(exp_low, i + 1)
                    nc.vector.tensor_tensor(feature[:, i, :], feature[:, i, :], low[i % 2][:, :], ALU.add).then_inc(feature_ready, 1)

                def sum_squares(i):
                    dve.wait_ge(square_ready, i + 1)
                    nc.vector.reduce_sum(inverse[:, i, :], low[i % 2][:, :].rearrange("p (h e) -> p h e", e=W),
                                         AX).then_inc(squares_summed, 1)
                norm_vector(dve)
                for i in range(TILES):
                    if i >= 2:
                        sum_squares(i - 2)
                    shift(i)
                    if i:
                        elu(i - 1)
                elu(TILES - 1)
                sum_squares(TILES - 2)
                sum_squares(TILES - 1)
                dve.wait_ge(root_taken, 1)
                nc.vector.reciprocal(inverse[:, :, :], inverse[:, :, :]).then_inc(inverse_step, 1)
                dve.wait_ge(inverse_step, 1)
                nc.vector.tensor_scalar(inverse[:, Q, :], inverse[:, Q, :], 0.125, None, ALU.mult).then_inc(inverse_step, 1)
                dve.wait_ge(w_loaded["v"], 32)
                for j in range(2 * ST):
                    t, c = j // 2, slice(j % 2 * 512, (j % 2 + 1) * 512)
                    dve.wait_ge(value_full, j + 1)
                    nc.vector.tensor_tensor(v[:, t, c], value_ps[j % 4][:, :], bias["v"][:, c], ALU.add).then_inc(v_ready, 1)
                dve.wait_ge(inverse_step, 2)
                for i in range(TILES):
                    f = feature[:, i, :].rearrange("p (h e) -> p h e", e=W)
                    nc.vector.tensor_tensor(f, f, inverse[:, i, :].unsqueeze(2).to_broadcast([P, HEADS, W]),
                                            ALU.mult).then_inc(unit_ready, 1)
                dve.wait_ge(rows_made, 3)
                for half in range(2):
                    dve.wait_ge(unit_turned, 2 * Q + half + 1)
                    for j in range(2):
                        nc.vector.tensor_scalar(qm[:, half * 8:(half + 1) * 8, :].rearrange("p (t two) n -> p two t n", two=2)[:, j],
                                                turned_ps[Q % 2][half][:, :].rearrange("p (t n) -> p t n", n=P),
                                                rows[:, j:j + 1], None, ALU.mult).then_inc(unitT_ready, 1)
                dve.wait_ge(small_loaded, 64)
                nc.vector.tensor_tensor(res[:, :], com.xn[:, :], bo[:, :], ALU.add).then_inc(out_step, 1)
                fk.on_vector(dve)
                dve.wait_ge(y_full, 1)
                dve.wait_ge(out_step, 1)
                nc.vector.tensor_tensor(res[:, :], front_ps[0][:, 0:D], res[:, :], ALU.add).then_inc(out_step, 1)
                dve.wait_ge(out_step, 2)
                nc.vector.bn_stats(stats[:, :], res[:, :]).then_inc(out_step, 1)
                dve.wait_ge(out_step, 3)
                nc.vector.bn_aggr(mv[:, :], stats[:, :]).then_inc(out_step, 1)
                dve.wait_ge(out_step, 4)
                nc.vector.tensor_scalar(rstd[:, :], mv[:, 1:2], 1e-12, None, ALU.add).then_inc(out_step, 1)
                dve.wait_ge(out_root, 1)
                nc.vector.reciprocal(rstd[:, :], rstd[:, :]).then_inc(out_step, 1)
                dve.wait_ge(out_step, 6)
                nc.vector.tensor_scalar(res[:, :], res[:, :], mv[:, 0:1], rstd[:, 0:1], ALU.subtract,
                                        ALU.mult).then_inc(out_step, 1)
                dve.wait_ge(out_step, 7)
                nc.vector.tensor_tensor(res[:, :], res[:, :], ln_g[:, :], ALU.mult).then_inc(out_step, 1)
                nc.vector.tensor_tensor(com.x[:, :], com.x[:, :], ln_b[:, :], ALU.add).then_inc(out_step, 1)
                dve.wait_ge(out_step, 9)
                nc.vector.tensor_tensor(com.x[:, :], com.x[:, :], res[:, :], ALU.add).then_inc(out_step, 1)
                dve.wait_ge(out_step, 10)



_INS = [
        'x', 'ctx_1024', 'fside_Bx16xSxS2_0', 'mask_BxS2_bf1', 'L0_xattn_W_q', 'L0_xattn_W_k', 'L0_xattn_W_v',
        'L0_attn_source_embedding', 'L0_attn_value_embedding', 'L0_attn_Wq', 'L0_attn_bq', 'L0_attn_Wk',
        'L0_attn_bk', 'L0_attn_Wv', 'L0_attn_bv', 'L0_attn_Wo', 'L0_attn_bo', 'L0_attn_ln_g', 'L0_attn_ln_b',
        'L0_ffn_Wr', 'L0_ffn_Wg', 'L0_ffn_Wu', 'L0_ffn_Wd', 'L0_ffn_Sg', 'L0_ffn_Su', 'L0_ffn_Sd',
        'L1_xattn_Wq', 'L1_xattn_bq', 'L1_xattn_Wk', 'L1_xattn_bk', 'L1_xattn_Wv', 'L1_xattn_bv',
        'L1_xattn_Wo', 'L1_xattn_bo', 'L1_attn_Win', 'L1_attn_bin_', 'L1_attn_A_log', 'L1_attn_B',
        'L1_attn_C', 'L1_attn_Dp', 'L1_attn_dt', 'L1_attn_Wout', 'L1_attn_bout', 'L1_ffn_Wg', 'L1_ffn_bg',
        'L1_ffn_We', 'L1_ffn_be', 'L2_xattn_Wq', 'L2_xattn_Wk', 'L2_xattn_Wv', 'L2_xattn_Wo', 'L2_attn_Wq',
        'L2_attn_Wkv_down', 'L2_attn_Wk_up', 'L2_attn_Wv_up', 'L2_attn_Wout', 'L2_ffn_router_w',
        'L2_ffn_router_b', 'L2_ffn_w1', 'L2_ffn_b1', 'L2_ffn_w2', 'L2_ffn_b2', 'L3_xattn_Wq', 'L3_xattn_bq',
        'L3_xattn_Wk', 'L3_xattn_bk', 'L3_xattn_Wv', 'L3_xattn_bv', 'L3_xattn_Wo', 'L3_xattn_bo',
        'L3_attn_Wq', 'L3_attn_bq', 'L3_attn_Wk', 'L3_attn_bk', 'L3_attn_Wv', 'L3_attn_bv', 'L3_attn_Wo',
        'L3_attn_bo', 'L3_ffn_Ws1', 'L3_ffn_bs1', 'L3_ffn_Ws2', 'L3_ffn_bs2', 'L3_ffn_We1', 'L3_ffn_be1',
        'L3_ffn_We2', 'L3_ffn_be2', 'L3_ffn_Wr', 'L3_ffn_br']
_OUTS = [((1, 128, 256), "float32")]


def latent_decoder(nc, a, out):
    with ExitStack() as ctx:
        com, scr = common(nc, ctx)
        setup(nc, com, a)
        prepare_context(nc, com, a, scr)
        l0_cross_attention(nc, com, a, scr)
        l0_attention(nc, com, a)
        l0_experts(nc, com, a)
        cross_attention_16(nc, com, a, scr, "L1")
        l1_state_space(nc, com, a)
        l1_experts(nc, com, a)
        l2_cross_attention(nc, com, a, scr)
        l2_attention(nc, com, a)
        l2_experts(nc, com, a)
        cross_attention_16(nc, com, a, scr, "L3")
        l3_attention(nc, com, a)
        l3_experts(nc, com, a)
        with phase(nc, "end") as ph:
            stored = ph.sem("stored")
            with nc.Block() as block:
                @block.sync
                def _(sp):
                    sp.dma_start(out[0], com.x[:, :]).then_inc(stored, 16)
                    sp.wait_ge(stored, 16)


def kernel(**inputs):
    import numpy as _np
    import concourse.bacc as _bacc
    from concourse import mybir as _mybir
    from concourse.bass_utils import run_bass_kernel_spmd as _run

    nc = _bacc.Bacc("TRN2", target_bir_lowering=False, num_devices=1)
    arrays, args = {}, {}
    for name in _INS:
        a = _np.ascontiguousarray(inputs[name])
        arrays[f"in_{name}_dram"] = a
        args[name] = nc.dram_tensor(f"in_{name}_dram", a.shape, _mybir.dt.from_np(a.dtype), kind="ExternalInput").ap()
    outs = []
    for i, (shape, dtype) in enumerate(_OUTS):
        dt = _mybir.dt.from_np(_np.dtype(dtype))
        outs.append(nc.dram_tensor(f"out_{i}_dram", shape, dt, kind="ExternalOutput").ap())
    latent_decoder(nc, args, outs[0])
    r = _run(nc, [arrays], core_ids=[0])
    return r.results[0]["out_0_dram"]
```

```python
from contextlib import ExitStack, contextmanager

import numpy as np
import concourse.bass as bass
from concourse import mybir

F32 = mybir.dt.float32
BF16 = mybir.dt.bfloat16
U8 = mybir.dt.uint8
I32 = mybir.dt.int32
ALU = mybir.AluOpType
ACT = mybir.ActivationFunctionType
AX = mybir.AxisListType.X

P = 128
D = 256
KT = D // P
SK = 12544
HEADS = 16
CH = SK // P
GRP = 14
GC = CH // GRP
GW = GC * P
HB = GW // 2
LN_EPS = 1e-5


def hold(sp, held, sem, value):
    sp.wait_ge(sem, value)
    sp.sem_inc(held, 1)


class Phase:

    def __init__(self, nc, ctx, name):
        self.nc, self.ctx, self.name, self.sems = nc, ctx, name, []

    def sb(self, name, shape, dt=F32):
        return self.ctx.enter_context(self.nc.sbuf_tensor(f"{self.name}_{name}", list(shape), dt))

    def ps(self, name, shape, dt=F32):
        return self.ctx.enter_context(self.nc.psum_tensor(f"{self.name}_{name}", list(shape), dt))

    def sem(self, name):
        s = self.nc.alloc_semaphore(f"{self.name}_{name}")
        self.sems.append(s)
        return s


@contextmanager
def phase(nc, name):
    with ExitStack() as ctx:
        ph = Phase(nc, ctx, name)
        yield ph
    nc.clear_and_free_semaphores(ph.sems)
    nc.all_engine_barrier()


def token_norm(nc, ph, com, xnT_ps):
    stats, mv, rstd = ph.sb("stats", [P, 6]), ph.sb("mv", [P, 2]), ph.sb("rstd", [P, 1])
    norm_step, root_ready, xn_ready, xnT_in_psum, xnT_ready = (
        ph.sem(s) for s in ("norm_step", "root_ready", "xn_ready", "xnT_in_psum", "xnT_ready"))

    def on_vector(dve):
        nc.vector.bn_stats(stats[:, :], com.x[:, :]).then_inc(norm_step, 1)
        dve.wait_ge(norm_step, 1)
        nc.vector.bn_aggr(mv[:, :], stats[:, :]).then_inc(norm_step, 1)
        dve.wait_ge(norm_step, 2)
        nc.vector.tensor_scalar(rstd[:, :], mv[:, 1:2], LN_EPS, None, ALU.add).then_inc(norm_step, 1)
        dve.wait_ge(root_ready, 1)
        nc.vector.reciprocal(rstd[:, :], rstd[:, :]).then_inc(norm_step, 1)
        dve.wait_ge(norm_step, 4)
        nc.vector.tensor_scalar(com.xn[:, :], com.x[:, :], mv[:, 0:1], rstd[:, 0:1],
                                ALU.subtract, ALU.mult).then_inc(xn_ready, 1)
        dve.wait_ge(xnT_in_psum, 1)
        nc.vector.tensor_copy(com.xnT[:, :, :], xnT_ps[:, :, :]).then_inc(xnT_ready, 1)
        dve.wait_ge(xnT_ready, 1)

    def on_scalar(act):
        act.wait_ge(norm_step, 3)
        nc.scalar.activation(rstd[:, :], rstd[:, :], ACT.Sqrt).then_inc(root_ready, 1)

    def on_tensor(pe):
        pe.wait_ge(xn_ready, 1)
        for k in range(KT):
            last = nc.tensor.transpose(xnT_ps[:, k, :], com.xn[:, k * P:(k + 1) * P], com.ident[:, :])
        last.then_inc(xnT_in_psum, 1)
        pe.wait_ge(xnT_ready, 1)

    return on_vector, on_scalar, on_tensor


TURNS = 4


def setup(nc, com, a):
    with phase(nc, "init") as ph:
        x_loaded, made = ph.sem("x_loaded"), ph.sem("made")
        with nc.Block() as block:
            @block.sync
            def _(sp):
                sp.dma_start(com.x[:, :], a["x"][0]).then_inc(x_loaded, 16)
                sp.wait_ge(x_loaded, 16)

            @block.gpsimd
            def _(pool):
                nc.gpsimd.memset(com.ident[:, :], 0.0).then_inc(made, 1)
                nc.gpsimd.memset(com.identb[:, :], 0.0).then_inc(made, 1)
                pool.wait_ge(made, 2)
                for m in (com.ident, com.identb):
                    nc.gpsimd.affine_select(out=m[:, :], in_=m[:, :], compare_op=ALU.not_equal, fill=1.0,
                                            base=0, pattern=[[-1, P]], channel_multiplier=1).then_inc(made, 1)
                pool.wait_ge(made, 4)



def high_parts(value):
    parts, rest = [], np.float32(value)
    for _ in range(3):
        high = (rest.reshape(1).view(np.uint32) & np.uint32(0xFFFF0000)).view(np.float32)[0]
        parts.append(float(high))
        rest = np.float32(rest - high)
    assert rest == 0
    return parts


def prepare_context(nc, com, a, scr):
    with phase(nc, "prep") as ph:
        wq0 = ph.sb("wq0", [P, KT, D])
        nat_w = {n: ph.sb("nat_" + n, [P, KT, D]) for n in ("k0", "k1", "v1", "k3", "v3")}
        wT = {n: ph.sb("T_" + n, [P, KT, D]) for n in nat_w}
        wv2 = ph.sb("wv2", [P, KT, HEADS * 64])
        bk = {n: ph.sb("b" + n, [P, KT]) for n in ("k1", "k3")}
        q0T = ph.sb("q0T", [P, KT, P])
        qfT = ph.sb("qfT", [P, KT, P])
        mask_u8 = ph.sb("mask_u8", [P, GW], U8)
        mask = ph.sb("mask", [P, GW])
        fill_value, fill_tile = ph.sb("fill_value", [3, 1]), ph.sb("fill_tile", [3, GW], BF16)
        ctx_nat = ph.sb("ctx_nat", [P, GC, D])
        ctxT = ph.sb("ctxT", [P, KT, GW])
        kf = [ph.sb(f"kf{i}", [P, GW]) for i in range(2)]
        kparts = [ph.sb(f"kparts{i}", [P, 3, GW], BF16) for i in range(2)]
        vst = {n: ph.sb("st_" + n, [P, HEADS, GC, w]) for n, w in (("v1", 16), ("v3", 17))}
        v2st = ph.sb("st_v2", [P, HEADS, GC, 64])
        turn = ph.ps("turn", [P, TURNS, 512])
        work = ph.ps("work", [P, 2, 2, 512])
        norm_vector, norm_scalar, norm_tensor = token_norm(
            nc, ph, com, turn[:, 0, 0:D].rearrange("p (k n) -> p k n", k=KT))
        S = ph.sem
        weights_loaded, wT_in_psum, wT_ready, q0T_in_psum, q0T_ready, qfT_in_psum, qfT_ready = (
            S(s) for s in ("weights_loaded", "wT_in_psum", "wT_ready", "q0T_in_psum", "q0T_ready", "qfT_in_psum",
                           "qfT_ready"))
        ctx_loaded, turn_in_psum, ctxT_stored = (
            S(s) for s in ("ctx_loaded", "turn_in_psum", "ctxT_stored"))
        turn_copied = {"v": S("turn_copied_by_vector"), "s": S("turn_copied_by_scalar")}
        mask_loaded, mask_ready, ones_set = S("mask_loaded"), S("mask_ready"), S("ones_set")
        work_full = S("work_full")
        freed = {"v": S("freed_by_vector"), "s": S("freed_by_scalar")}
        hi_ready, rest_ready, mid_ready, parts_ready = (
            S(s) for s in ("hi_ready", "rest_ready", "mid_ready", "parts_ready"))
        parts_stored = [S(f"parts_stored{i}") for i in range(2)]
        narrow_stored, held = S("narrow_values_stored"), S("held")
        wide_loaded, wide_stored = S("wide_weights_loaded"), [S(f"wide_values_stored{i}") for i in range(2)]
        fill_ready, fill_stored = S("fill_ready"), S("fill_stored")

        plan = [("s0", 0, "v"), ("k1", 0, "v"), ("v1", 0, "s"), ("k1", 1, "v"), ("v1", 4, "s"),
                ("k3", 0, "v"), ("v3", 0, "s"), ("k3", 1, "v"), ("v3", 4, "s")]
        plan += [("v2", c, "vs"[c % 2]) for c in range(GC)]
        assert len(plan) == 16
        WIDE = ((0, 4), (4, GC))
        n_by = {e: sum(p[2] == e for p in plan) for e in "vs"}

        def rank(i):
            return sum(p[2] == plan[i][2] for p in plan[:i + 1])

        turns = [(c, k) for c in range(GC) for k in range(KT)]

        with nc.Block() as block:
            @block.sync
            def _(sp):
                loads = [(wq0, a["L0_xattn_W_q"]), (nat_w["k0"], a["L0_xattn_W_k"]), (nat_w["k1"], a["L1_xattn_Wk"]),
                         (nat_w["v1"], a["L1_xattn_Wv"]), (nat_w["k3"], a["L3_xattn_Wk"]),
                         (nat_w["v3"], a["L3_xattn_Wv"])]
                for t, src in loads:
                    sp.dma_start(t[:, :, :], src.rearrange("(k p) n -> p k n", p=P)).then_inc(weights_loaded, 16)
                for n, src in (("k1", a["L1_xattn_bk"]), ("k3", a["L3_xattn_bk"])):
                    sp.dma_start(bk[n][:, :], src.rearrange("(k p) -> p k", p=P),
                                 allow_slow_non_contiguous=True).then_inc(weights_loaded, 16)
                sp.dma_start(wv2[:, :, :], a["L2_xattn_Wv"].rearrange("(k p) n -> p k n", p=P)).then_inc(wide_loaded, 16)
                sp.sem_inc(turn_in_psum, 1)
                sp.sem_inc(work_full, 1)
                sp.sem_inc(mask_ready, 1)
                sp.sem_inc(turn_copied["v"], 2)
                sp.sem_inc(turn_copied["s"], 2)
                for e in "vs":
                    sp.sem_inc(freed[e], n_by[e])
                sp.sem_inc(parts_ready, 2)
                for s in (parts_stored[0], parts_stored[1], ctxT_stored, fill_stored):
                    sp.sem_inc(s, 16)
                sp.sem_inc(narrow_stored, 32)
                for s in wide_stored:
                    sp.sem_inc(s, 16)

                def load(g):
                    hold(sp, held, turn_in_psum, g * TURNS + 1)
                    sp.dma_start(ctx_nat[:, :, :], a["ctx_1024"][0, bass.ds(g * GW, GW), :]
                                 .rearrange("(c p) d -> p c d", p=P)).then_inc(ctx_loaded, 16)
                    hold(sp, held, mask_ready, g + 1)
                    sp.dma_start(mask_u8[:, :], a["mask_BxS2_bf1"][0:1, bass.ds(g * GW, GW)]
                                 .to_broadcast([P, GW])).then_inc(mask_loaded, 16)

                def store(g):
                    for e in "vs":
                        hold(sp, held, turn_copied[e], g * 2 + 4)
                    sp.dma_start(scr.ctxT[:, :, bass.ds(g * GW, GW)], ctxT[:, :, :]).then_inc(ctxT_stored, 16)
                    hold(sp, held, fill_ready, g + 1)
                    sp.dma_start(scr.fill[0, :, bass.ds(g * GW, GW)], fill_tile[:, :]).then_inc(fill_stored, 16)
                    for i, (n, t) in enumerate((("k1", 0), ("k1", 1), ("k3", 0), ("k3", 1))):
                        hold(sp, held, parts_ready, g * 4 + i + 1 + 2)
                        sp.dma_start(scr.kparts[n][:, t * P:(t + 1) * P, bass.ds(g * GW, GW)]
                                     .rearrange("a p s -> p a s"), kparts[i % 2][:, :, :]).then_inc(parts_stored[i % 2], 16)
                    hold(sp, held, freed["s"], (g + 1) * n_by["s"] + rank(8))
                    for n in ("v1", "v3"):
                        sp.dma_start(scr.v[n][:, :, bass.ds(g * GC, GC), :].rearrange("h p c e -> p h c e"),
                                     vst[n][:, :, :, :]).then_inc(narrow_stored, 16)
                    for i, (c0, c1) in enumerate(WIDE):
                        for c in (c1 - 2, c1 - 1):
                            k = 9 + c
                            hold(sp, held, freed[plan[k][2]], (g + 1) * n_by[plan[k][2]] + rank(k))
                        sp.dma_start(scr.v["v2"][:, :, bass.ds(g * GC + c0, c1 - c0), :].rearrange("h p c e -> p h c e"),
                                     v2st[:, :, c0:c1, :]).then_inc(wide_stored[i], 16)

                sp.wait_ge(ones_set, 4)
                load(0)
                with sp.Fori(0, GRP - 1) as g:
                    load(g + 1)
                    store(g)
                store(GRP - 1)
                sp.wait_ge(ctxT_stored, 16 * GRP + 16)
                sp.wait_ge(fill_stored, 16 * GRP + 16)
                sp.wait_ge(parts_stored[0], 16 * 2 * GRP + 16)
                sp.wait_ge(parts_stored[1], 16 * 2 * GRP + 16)
                sp.wait_ge(narrow_stored, 32 * GRP + 32)
                for s in wide_stored:
                    sp.wait_ge(s, 16 * GRP + 16)

            @block.tensor
            def _(pe):
                norm_tensor(pe)
                pe.wait_ge(weights_loaded, 16 * 8)
                for n_i, n in enumerate(nat_w):
                    if n_i >= TURNS:
                        pe.wait_ge(wT_ready, n_i - TURNS + 1)
                    for k in range(KT):
                        for o in range(KT):
                            last = nc.tensor.transpose(turn[:, n_i % TURNS, (k * KT + o) * P:(k * KT + o + 1) * P],
                                                       nat_w[n][:, o, k * P:(k + 1) * P], com.ident[:, :])
                    last.then_inc(wT_in_psum, 1)
                for e in range(KT):
                    for k in range(KT):
                        last = nc.tensor.matmul(work[:, 0, 0, e * P:(e + 1) * P], wq0[:, k, e * P:(e + 1) * P],
                                                com.xnT[:, k, :], start=(k == 0), stop=(k == KT - 1))
                last.then_inc(q0T_in_psum, 1)
                pe.wait_ge(q0T_ready, 1)
                pe.wait_ge(wT_ready, 5)
                for e in range(KT):
                    for k in range(KT):
                        last = nc.tensor.matmul(work[:, 0, 1, e * P:(e + 1) * P], wT["k0"][:, k, e * P:(e + 1) * P],
                                                q0T[:, k, :], start=(k == 0), stop=(k == KT - 1))
                last.then_inc(qfT_in_psum, 1)
                pe.wait_ge(qfT_ready, 1)
                pe.wait_ge(wide_loaded, 16)
                with pe.Fori(0, GRP) as g:
                    pe.wait_ge(ctx_loaded, g * 16 + 16)
                    for t in range(TURNS):
                        pe.wait_ge(turn_copied["vs"[t % 2]], g * 2 + t // 2 + 1)
                        for j, (c, k) in enumerate(turns[4 * t:4 * t + 4]):
                            last = nc.tensor.transpose(turn[:, t, j * P:(j + 1) * P],
                                                       ctx_nat[:, c, k * P:(k + 1) * P], com.ident[:, :])
                        last.then_inc(turn_in_psum, 1)
                    for e in "vs":
                        pe.wait_ge(turn_copied[e], g * 2 + 4)
                    for i, (what, j, _e) in enumerate(plan):
                        w = work[:, i % 2]
                        b = i - 2 if i >= 2 else len(plan) + i - 2
                        e = plan[b][2]
                        pe.wait_ge(freed[e], (g + 1 if i >= 2 else g) * n_by[e] + rank(b))
                        if what in ("s0", "k1", "k3"):
                            for h in range(2):
                                for k in range(KT):
                                    lhs = qfT[:, k, :] if what == "s0" else wT[what][:, k, j * P:(j + 1) * P]
                                    last = nc.tensor.matmul(w[:, h, 0:HB], lhs, ctxT[:, k, h * HB:(h + 1) * HB],
                                                            start=(k == 0), stop=(k == KT - 1))
                        elif what == "v2":
                            for h in range(2):
                                for k in range(KT):
                                    last = nc.tensor.matmul(w[:, h, :], ctxT[:, k, j * P:(j + 1) * P],
                                                            wv2[:, k, h * 512:(h + 1) * 512],
                                                            start=(k == 0), stop=(k == KT - 1))
                        else:
                            for c in range(j, min(j + 4, GC)):
                                for k in range(KT):
                                    last = nc.tensor.matmul(w[:, (c - j) // 2, (c - j) % 2 * D:(c - j) % 2 * D + D],
                                                            ctxT[:, k, c * P:(c + 1) * P], wT[what][:, k, :],
                                                            start=(k == 0), stop=(k == KT - 1))
                        last.then_inc(work_full, 1)

            def take_turned(eng, copy, g, ts):
                for t in ts:
                    eng.wait_ge(turn_in_psum, g * TURNS + t + 2)
                    if t == ts[0]:
                        eng.wait_ge(ctxT_stored, g * 16 + 16)
                        eng.wait_ge(work_full, g * len(plan) + 1)
                    n = 2 if t < 3 else 1
                    copy(ctxT[:, :, 2 * t * P:(2 * t + n) * P].rearrange("p k (c q) -> p c k q", q=P),
                         turn[:, t, 0:n * 2 * P].rearrange("p (c k q) -> p c k q", k=KT, q=P)
                         ).then_inc(turn_copied["vs"[t % 2]], 1)

            def take_values(eng, copy, g, what, j, i):
                w = work[:, i % 2]
                if what == "v2":
                    eng.wait_ge(wide_stored[0 if j < WIDE[0][1] else 1], g * 16 + 16)
                else:
                    eng.wait_ge(narrow_stored, g * 32 + 32)
                eng.wait_ge(work_full, g * len(plan) + i + 2)
                if what == "v2":
                    return copy(v2st[:, :, j, :], w[:, :, :].rearrange("p b (h e) -> p (b h) e", e=64))
                n = min(4, GC - j)
                out = vst[what][:, :, j:j + n, 0:16].rearrange("p h c e -> p c h e")
                for c in range(n):
                    last = copy(out[:, c], w[:, c // 2, c % 2 * D:c % 2 * D + D].rearrange("p (h e) -> p h e", e=16))
                return last

            @block.vector
            def _(dve):
                norm_vector(dve)
                for n_i, n in enumerate(nat_w):
                    dve.wait_ge(wT_in_psum, n_i + 1)
                    nc.vector.tensor_copy(wT[n][:, :, :].rearrange("p k n -> p (k n)"),
                                          turn[:, n_i % TURNS, :]).then_inc(wT_ready, 1)
                dve.wait_ge(q0T_in_psum, 1)
                nc.vector.tensor_copy(q0T[:, :, :].rearrange("p k n -> p (k n)"), work[:, 0, 0, 0:D]).then_inc(q0T_ready, 1)
                dve.wait_ge(qfT_in_psum, 1)
                nc.vector.tensor_scalar(qfT[:, :, :].rearrange("p k n -> p (k n)"), work[:, 0, 1, 0:D], 1.0 / 16, None,
                                        ALU.mult).then_inc(qfT_ready, 1)
                dve.wait_ge(ones_set, 4)
                with dve.Fori(0, GRP) as g:
                    take_turned(dve, nc.vector.tensor_copy, g, (0, 2))
                    dve.wait_ge(mask_loaded, g * 16 + 16)
                    nc.vector.tensor_copy(mask[:, :], mask_u8[:, :]).then_inc(mask_ready, 1)
                    dve.wait_ge(mask_ready, g + 2)
                    dve.wait_ge(fill_stored, g * 16 + 16)
                    nc.vector.tensor_scalar(fill_tile[:, :], mask[0:3, :], 1.0, fill_value[:, 0:1], ALU.subtract,
                                            ALU.mult).then_inc(fill_ready, 1)
                    nk = 0
                    for i, (what, j, e) in enumerate(plan):
                        if e != "v":
                            continue
                        if what in ("v1", "v2", "v3"):
                            take_values(dve, nc.vector.tensor_copy, g, what, j, i).then_inc(freed["v"], 1)
                            continue
                        dve.wait_ge(work_full, g * len(plan) + i + 2)
                        w = work[:, i % 2, :, 0:HB]
                        if what == "s0":
                            nc.vector.tensor_reduce(com.mx0[:, bass.ds(g, 1)], w, mybir.AxisListType.XY, ALU.max)
                            nc.vector.tensor_copy(com.S[:, bass.ds(g * GW, GW)].rearrange("p (b s) -> p b s", b=2),
                                                  w).then_inc(freed["v"], 1)
                            continue
                        dve.wait_ge(parts_ready, g * 4 + nk + 1)
                        out = kf[nk % 2][:, :].rearrange("p (b s) -> p b s", b=2)
                        if what == "k1":
                            ins = nc.vector.tensor_scalar(out, w, bk["k1"][:, j:j + 1], None, ALU.add)
                        else:
                            ins = nc.vector.scalar_tensor_tensor(
                                out=out, in0=w, scalar=bk["k3"][:, j:j + 1],
                                in1=mask[:, :].rearrange("p (b s) -> p b s", b=2), op0=ALU.add, op1=ALU.mult)
                        ins.then_inc(freed["v"], 1)
                        nk += 1

            @block.scalar
            def _(act):
                norm_scalar(act)
                act.wait_ge(qfT_ready, 1)
                with act.Fori(0, GRP) as g:
                    take_turned(act, nc.scalar.copy, g, (1, 3))
                    nk = 0
                    for i, (what, j, e) in enumerate(plan):
                        if e == "s":
                            take_values(act, nc.scalar.copy, g, what, j, i).then_inc(freed["s"], 1)
                        elif what in ("k1", "k3"):
                            parts = kparts[nk % 2]
                            act.wait_ge(parts_stored[nk % 2], g * 32 + nk // 2 * 16 + 16)
                            act.wait_ge(freed["v"], (g + 1) * n_by["v"] + rank(i))
                            nc.scalar.copy(parts[:, 0, :], kf[nk % 2][:, :]).then_inc(hi_ready, 1)
                            act.wait_ge(rest_ready, g * 4 + nk + 1)
                            nc.scalar.copy(parts[:, 1, :], kf[nk % 2][:, :]).then_inc(mid_ready, 1)
                            nk += 1

            @block.gpsimd
            def _(pool):
                nc.gpsimd.memset(vst["v3"][:, :, :, 16:17], 1.0).then_inc(ones_set, 1)
                nc.gpsimd.memset(fill_value[:, :], high_parts(1e8)[2]).then_inc(ones_set, 1)
                for row in (2, 1):
                    pool.wait_ge(ones_set, 4 - row)
                    nc.gpsimd.affine_select(out=fill_value[:, :], in_=fill_value[:, :], compare_op=ALU.is_ge,
                                            fill=high_parts(1e8)[row - 1], base=-row, pattern=[[0, 1]],
                                            channel_multiplier=1).then_inc(ones_set, 1)
                with pool.Fori(0, GRP) as g:
                    for nk in range(4):
                        k, parts = kf[nk % 2], kparts[nk % 2]
                        pool.wait_ge(hi_ready, g * 4 + nk + 1)
                        nc.gpsimd.tensor_tensor(k[:, :], k[:, :], parts[:, 0, :], ALU.subtract).then_inc(rest_ready, 1)
                        pool.wait_ge(mid_ready, g * 4 + nk + 1)
                        nc.gpsimd.tensor_tensor(parts[:, 2, :], k[:, :], parts[:, 1, :],
                                                ALU.subtract).then_inc(parts_ready, 1)


def common(nc, ctx):
    class Shared:
        pass
    com, scr = Shared(), Shared()
    def sb(name, shape, dt=F32):
        return ctx.enter_context(nc.sbuf_tensor("all_" + name, shape, dt))
    com.x, com.xn, com.xnT = sb("x", [P, D]), sb("xn", [P, D]), sb("xnT", [P, KT, P])
    com.ident, com.identb = sb("ident", [P, P]), sb("identb", [P, P], BF16)
    com.S, com.mx0 = sb("S", [P, SK]), sb("mx0", [P, GRP])
    com.k_rev = sb("k_rev", [P, KT, P])
    scr.ctxT = nc.dram_tensor("scratch_ctxT", [P, KT, SK], F32).ap()
    scr.fill = nc.dram_tensor("scratch_fill", [1, 3, SK], BF16).ap()
    scr.kparts = {n: nc.dram_tensor("scratch_" + n, [3, D, SK], BF16).ap() for n in ("k1", "k3")}
    scr.att1 = nc.dram_tensor("scratch_att1", [HEADS, P, 16], F32).ap()
    scr.v = {n: nc.dram_tensor("scratch_" + n, [HEADS, P, CH, w], F32).ap()
             for n, w in (("v1", 16), ("v2", 64), ("v3", 17))}
    return com, scr



R = 7
LAG = 3
PIECES = (0, 1, 2, 0, 1, 0)
QPIECES = (0, 0, 0, 1, 1, 2)
STACK = 16 * len(PIECES)


def head_stream(nc, ph, com, heads, vw, att, v_src, q=None, k_half=None, k_loads=None, bias=None, ring=R, lag=LAG,
                by_vector=(1, 3, 5, 8, 10, 12), q_cur=None,
                ctxT=None, ctx_loaded=None, sum_ps=None, beside=None):
    v_half = [ph.sb(f"v_half{j}", [P, CH // 2, vw]) for j in range(2)]
    pT = [ph.sb(f"pT{i}", [P, GW]) for i in range(ring)]
    rowmax, negmax = ph.sb("rowmax", [P, 2 * GRP]), ph.sb("negmax", [P, 1])
    rowsum, total, inverse = ph.sb("rowsum", [P, GRP]), ph.sb("total", [P, 1]), ph.sb("inverse", [P, 1])
    turned_ps = [ph.ps(f"turned{i}", [P, 1024]) for i in range(2)]
    scores_ps = [ph.ps(f"scores{i}", [P, 512]) for i in range(2)] if q is not None or ctxT is not None else None
    out_ps = ph.ps("out", [P, 512])
    tiles = P // vw // 2 if vw < 64 else P // vw if vw < P else 1
    if tiles > 1:
        out_parts, select = ph.sb("out_parts", [P, P]), ph.sb("select", [P, vw])
        parts_ready, summed, cleared = ph.sem("parts_ready"), ph.sem("summed"), ph.sem("cleared")
    if bias is not None:
        bias_tile = [ph.sb(f"bias{i}", [P, 2 * GW]) for i in range(GRP // 2)]
        bias_loaded = [ph.sem(f"bias_loaded{i}") for i in range(GRP // 2)]
    S = ph.sem
    scores_full, scores_taken, negmax_ready, max_step = (
        S("scores_full"), S("scores_taken"), S("negmax_ready"), S("max_step"))
    exp_done, turned, weighed, rowsum_taken, out_step, out_taken = (
        S(s) for s in ("exp_done", "turned", "weighed", "rowsum_taken", "out_step", "out_taken"))
    copied = {"v": S("copied_by_vector"), "s": S("copied_by_scalar")}
    k_loaded = [S(f"k_loaded{j}") for j in range(2)]
    v_loaded = [S(f"v_loaded{j}") for j in range(2 if heads > 1 else GRP)]
    held, held_by_vector = S("held"), S("held_by_vector")
    by = ["v" if c in by_vector else "s" for c in range(GRP)]
    n_by = {e: by.count(e) for e in "vs"}
    rank = [by[:c + 1].count(by[c]) for c in range(GRP)]
    more_scores = scores_ps is not None

    class Run:
        pass
    run = Run()
    run.turned_ps, run.turned = turned_ps, turned
    run.exp_done, run.out_taken, run.scores_full, run.negmax = exp_done, out_taken, scores_full, negmax
    run.rowmax, run.negmax_ready, run.max_step = rowmax, negmax_ready, max_step

    def load_keys(sp, h, j, first):
        if k_loads is not None:
            if not first:
                hold(sp, held, scores_full, (h - 1) * 2 * GRP + GRP * (j + 1))
            for dst, src in k_loads(h, j):
                sp.dma_start(dst, src).then_inc(k_loaded[j], 16)

    def load_bias(sp, h, i, first):
        if bias is not None:
            if not first:
                hold(sp, held, scores_taken, (h - 1) * 2 * GRP + 4 * (i + 1) + 2)
            sp.dma_start(bias_tile[i][:, :], bias(h, i)).then_inc(bias_loaded[i], 16)

    def load_values(sp, h, j, first):
        if not first:
            hold(sp, held, weighed, (h - 1) * GRP + GRP // 2 * (j + 1) + ring)
        if heads == 1:
            for at in range(GRP // 2):
                c = j * (GRP // 2) + at
                sp.dma_start(v_half[j][:, at * GC:(at + 1) * GC, :], v_src(h, c)).then_inc(v_loaded[c], 16)
            return
        sp.dma_start(v_half[j][:, :, :], v_src(h, j)).then_inc(v_loaded[j], 16)

    def load_head(sp, k, v, first=False):
        for i in range(GRP // 2):
            if k is not None:
                load_bias(sp, k, i, first)
                if i == 2:
                    load_keys(sp, k, 0, first)
                if i == 6:
                    load_keys(sp, k, 1, first)
            if v is not None:
                if i == 3:
                    load_values(sp, v, 0, first)
                if i == 6:
                    load_values(sp, v, 1, first)

    def on_sync(sp):
        sp.sem_inc(scores_taken, 2)
        sp.sem_inc(weighed, ring)
        sp.sem_inc(rowsum_taken, 1)
        sp.sem_inc(out_taken, 1)
        for e in "vs":
            sp.sem_inc(copied[e], n_by[e])
        load_head(sp, 0, 0, True)
        if heads > 1:
            load_head(sp, 1, None)
            with sp.Fori(0, heads - 2) as h:
                load_head(sp, h + 2, h + 1)
            load_head(sp, None, heads - 1)

    n_k = len(k_loads(0, 0)) if k_loads is not None else 0

    def scores(pe, h, c):
        if k_loads is not None and c % (GRP // 2) == 0:
            j = c // (GRP // 2)
            pe.wait_ge(k_loaded[j], (h + 1) * 16 * n_k)
        for b in (2 * c, 2 * c + 1):
            pe.wait_ge(scores_taken, h * 2 * GRP + b + 1)
            if ctxT is None:
                j, at = b // GRP, b % GRP
                nc.tensor.matmul(scores_ps[b % 2][:, 0:HB], q[:, bass.ds(h * P, P)],
                                 k_half[j][:, at * HB:(at + 1) * HB], start=True, stop=True).then_inc(scores_full, 1)
            else:
                for k in range(KT):
                    last = nc.tensor.matmul(scores_ps[b % 2][:, 0:HB], q_cur[:, k, :],
                                            ctxT[:, k, b * HB:(b + 1) * HB], start=(k == 0), stop=(k == KT - 1))
                last.then_inc(scores_full, 1)

    def turn(pe, h, c):
        pe.wait_ge(exp_done, h * GRP + c + 1)
        b = c - 2 if c >= 2 else c - 2 + GRP
        pe.wait_ge(copied[by[b]], (h + 1 if c >= 2 else h) * n_by[by[b]] + rank[b])
        for i in range(GC):
            last = nc.tensor.transpose(turned_ps[c % 2][:, i * P:(i + 1) * P],
                                       com.S[:, (c * GC + i) * P:(c * GC + i + 1) * P], com.ident[:, :])
        last.then_inc(turned, 1)

    def weigh(pe, h, c):
        if heads == 1:
            pe.wait_ge(v_loaded[c], 16)
        elif c % (GRP // 2) == 0:
            pe.wait_ge(v_loaded[c // (GRP // 2)], h * 16 + 16)
        if c == 0:
            pe.wait_ge(out_taken, h + 1)
        pe.wait_ge(copied[by[c]], (h + 1) * n_by[by[c]] + rank[c])
        for i in range(GC):
            k = c * GC + i
            v = v_half[k // (CH // 2)][:, k % (CH // 2), :]
            if tiles > 1:
                at = k % tiles * (P // tiles)
                last = nc.tensor.matmul(out_ps[at:at + vw, 0:P], v, pT[c % ring][:, i * P:(i + 1) * P],
                                        start=(k < tiles), stop=(k >= CH - tiles))
                continue
            last = nc.tensor.matmul(out_ps[:, 0:vw], pT[c % ring][:, i * P:(i + 1) * P],
                                    v, start=(k == 0), stop=(k == CH - 1))
        last.then_inc(weighed, 1)

    def sum_tiles(pe, h):
        pe.wait_ge(parts_ready, h + 1)
        nc.tensor.matmul(sum_ps[:, 0:vw], out_parts[:, :], select[:, :], start=True, stop=True).then_inc(summed, 1)

    def tensor_head(pe, h, following):
        for c in range(GRP + lag):
            if c < GRP:
                turn(pe, h, c)
                if following:
                    scores(pe, h + 1, c)
            if c >= lag:
                weigh(pe, h, c - lag)
        if tiles > 1:
            sum_tiles(pe, h)

    def on_tensor(pe, before_scores=lambda pe, h: None):
        if tiles > 1:
            pe.wait_ge(cleared, 1)
        if more_scores:
            before_scores(pe, 0)
            for c in range(GRP):
                if ctx_loaded is not None and c % 2 == 0:
                    pe.wait_ge(ctx_loaded[c // 2], 16)
                scores(pe, 0, c)
        if heads > 1:
            with pe.Fori(0, heads - 1) as h:
                before_scores(pe, h + 1)
                tensor_head(pe, h, True)
        tensor_head(pe, heads - 1, False)

    def copy_turned(eng, copy, h, c):
        eng.wait_ge(turned, h * GRP + c + 1)
        eng.wait_ge(weighed, h * GRP + c + 1)
        copy(pT[c % ring][:, :], turned_ps[c % 2][:, 0:GW]).then_inc(copied[by[c]], 1)

    def take_scores(dve, h, c):
        if bias is not None and c % 2 == 0:
            dve.wait_ge(bias_loaded[c // 2], h * 16 + 16)
        for b in (2 * c, 2 * c + 1):
            if bias is not None:
                hold(dve, held_by_vector, scores_full, h * 2 * GRP + b + 1)
            else:
                dve.wait_ge(scores_full, h * 2 * GRP + b + 1)
            out, s = com.S[:, b * HB:(b + 1) * HB], scores_ps[b % 2][:, 0:HB]
            if bias is not None:
                nc.vector.tensor_tensor_reduce(out, s, bias_tile[b // 4][:, b % 4 * HB:(b % 4 + 1) * HB], 1.0, -3.4e38,
                                               ALU.add, ALU.max, rowmax[:, b:b + 1]).then_inc(scores_taken, 1)
            else:
                nc.vector.tensor_scalar(out, s, 1.0, -3.4e38, ALU.mult, ALU.max,
                                        accum_out=rowmax[:, b:b + 1]).then_inc(scores_taken, 1)

    def max_of(dve, h, rowmax_ap=None):
        if rowmax_ap is None:
            dve.wait_ge(scores_taken, (h + 1) * 2 * GRP + 2)
            rowmax_ap = rowmax[:, :]
        nc.vector.reduce_max(negmax[:, :], rowmax_ap, AX).then_inc(max_step, 1)
        dve.wait_ge(max_step, h + 1)
        nc.vector.tensor_scalar(negmax[:, :], negmax[:, :], -1.0, None, ALU.mult).then_inc(negmax_ready, 1)

    def leave(dve, h):
        dve.wait_ge(exp_done, h * GRP + GRP)
        nc.vector.reduce_sum(total[:, :], rowsum[:, :], AX).then_inc(rowsum_taken, 1)
        dve.wait_ge(rowsum_taken, h + 2)
        nc.vector.reciprocal(inverse[:, :], total[:, :]).then_inc(out_step, 1)
        dve.wait_ge(out_step, h + 1)
        dve.wait_ge(weighed, h * GRP + GRP + ring)
        product = out_ps
        if tiles > 1:
            product = sum_ps
            nc.vector.tensor_copy(out_parts[:, :], out_ps[:, 0:P]).then_inc(parts_ready, 1)
            dve.wait_ge(summed, h + 1)
        nc.vector.tensor_scalar(att[:, bass.ds(h * vw, vw)], product[:, 0:vw], inverse[:, 0:1], None,
                                ALU.mult).then_inc(out_taken, 1)

    def vector_head(dve, h, following):
        for c in range(GRP):
            if beside is not None:
                beside.vector_step(dve, h, c)
            if by[c] == "v":
                copy_turned(dve, nc.vector.tensor_copy, h, c)
            if following:
                take_scores(dve, h + 1, c)
        if following:
            max_of(dve, h + 1)
        leave(dve, h)

    def on_vector(dve):
        if tiles > 1:
            nc.vector.memset(out_ps[:, 0:P], 0.0)
            nc.vector.reduce_sum(select[:, :], com.ident[:, :].rearrange("p (a e) -> p e a", a=tiles)[:, 0:vw, :],
                                 AX).then_inc(cleared, 1)
        if more_scores:
            for c in range(GRP):
                take_scores(dve, 0, c)
            max_of(dve, 0)
        else:
            max_of(dve, 0, com.mx0[:, :])
        if heads > 1:
            with dve.Fori(0, heads - 1) as h:
                vector_head(dve, h, True)
        vector_head(dve, heads - 1, False)
        dve.wait_ge(out_taken, heads + 1)

    def scalar_head(act, h):
        for c in range(GRP + 2):
            if c < GRP:
                if c == 0:
                    act.wait_ge(negmax_ready, h + 1)
                    act.wait_ge(rowsum_taken, h + 1)
                s = com.S[:, c * GW:(c + 1) * GW]
                nc.scalar.activation(s, s, ACT.Exp, bias=negmax[:, 0:1], scale=1.0,
                                     accum_out=rowsum[:, c:c + 1]).then_inc(exp_done, 1)
            if c >= 2 and by[c - 2] == "s":
                copy_turned(act, nc.scalar.copy, h, c - 2)
            if beside is not None:
                beside.scalar_step(act, h, c)

    def on_scalar(act):
        if heads > 1:
            turn = 4
            with act.Fori(0, heads // turn) as g:
                for j in range(turn):
                    scalar_head(act, g * turn + j)
        else:
            scalar_head(act, 0)

    run.on_sync, run.on_tensor, run.on_vector, run.on_scalar = on_sync, on_tensor, on_vector, on_scalar
    return run


def head_stream_turned(nc, ph, com, att, v_src, q, k_load, fill, sum_ps):
    ring, lag, VW, rows = 7, 4, 17, STACK + 6
    tiles = 4
    MX = STACK
    kt = [[ph.sb(f"k{s}{j}", [rows, SK // 2], BF16) for j in range(2)] for s in range(2)]
    v_half = [ph.sb(f"v_half{j}", [P, CH // 2, VW]) for j in range(2)]
    pT = [ph.sb(f"pT{i}", [P, GW]) for i in range(ring)]
    rowmax, nm, nm_parts = ph.sb("rowmax", [P, 2 * GRP]), ph.sb("nm", [P, 1]), ph.sb("nm_parts", [P, 3], BF16)
    inverse = ph.sb("inverse", [P, 1])
    out_parts, select = ph.sb("out_parts", [P, P]), ph.sb("select", [P, VW])
    turned_ps = [ph.ps(f"turned{i}", [P, 1024]) for i in range(2)]
    scores_ps = [ph.ps(f"scores{i}", [P, 512]) for i in range(2)]
    out_ps = ph.ps("out", [P, 512])
    nmT_ps = sum_ps[:, 256:512].bitcast(BF16)
    S = ph.sem
    k_loaded = [[S(f"k_loaded{s}{j}") for j in range(2)] for s in range(2)]
    v_loaded, fill_loaded = [S(f"v_loaded{j}") for j in range(2)], S("fill_loaded")
    scores_full, scores_taken, nm_step, nm_ready, nmT_in_psum, q_ready = (
        S(s) for s in ("scores_full", "scores_taken", "nm_step", "nm_ready", "nmT_in_psum", "max_in_q"))
    turned_full, exp_done, weighed, parts_ready, summed, out_step, out_taken, cleared, held = (
        S(s) for s in ("turned_full", "exp_done", "weighed", "parts_ready", "summed", "out_step", "out_taken",
                       "cleared", "held"))
    N_K = len(PIECES)
    NB = 2 * GRP
    EARLY = 4
    per_slot = [2] * 12 + [0, 0]
    assert EARLY + sum(per_slot) == NB
    first_bank = [EARLY + sum(per_slot[:c]) for c in range(GRP)]

    class Run:
        pass
    run = Run()

    def on_sync(sp):
        sp.sem_inc(scores_taken, 2)
        sp.sem_inc(exp_done, 2)
        sp.sem_inc(weighed, ring)
        sp.sem_inc(parts_ready, 1)

        def load_k(h, s, j, first=False):
            if not first:
                hold(sp, held, turned_full, (h - 2) * GRP + GRP // 2 * (j + 1))
            for dst, src in k_load(kt[s][j], h, j):
                sp.dma_start(dst, src).then_inc(k_loaded[s][j], 16)

        def load_v(h, j, first=False):
            if not first:
                hold(sp, held, weighed, (h - 1) * GRP + GRP // 2 * (j + 1) + ring)
            sp.dma_start(v_half[j][:, :, :], v_src(h, j)).then_inc(v_loaded[j], 16)

        for j in range(2):
            load_k(0, 0, j, True)
            for s in range(2):
                sp.dma_start(kt[s][j][MX + 3:MX + 6, :],
                             fill[0, :, j * (SK // 2):(j + 1) * (SK // 2)]).then_inc(fill_loaded, 16)
        for j in range(2):
            load_v(0, j, True)
        for j in range(2):
            load_k(1, 1, j, True)
        with sp.Fori(0, HEADS // 2 - 1) as i:
            for s in range(2):
                for j in range(2):
                    load_k(i * 2 + s + 2, s, j)
                    load_v(i * 2 + s + 1, j)
        for j in range(2):
            load_v(HEADS - 1, j)

    def scores(pe, h, s, b):
        j, at = b // GRP, b % GRP
        if at == 0:
            pe.wait_ge(k_loaded[s][j], (h // 2 + 1 if isinstance(h, int) else h[0] + 1) * 16 * N_K)
        hh = h if isinstance(h, int) else h[0] * 2 + h[1]
        pe.wait_ge(scores_taken, hh * NB + b + 1)
        nc.tensor.matmul(scores_ps[b % 2][:, 0:HB], q[:, bass.ds(hh * P, P)],
                         kt[s][j][:, at * HB:(at + 1) * HB], start=True, stop=True).then_inc(scores_full, 1)

    def turned(pe, h, s, c):
        pe.wait_ge(exp_done, h * GRP + c + 1)
        for i in range(GC):
            k = c % (GRP // 2) * GC + i
            last = nc.tensor.matmul(turned_ps[c % 2][:, i * P:(i + 1) * P],
                                    kt[s][c // (GRP // 2)][:, k * P:(k + 1) * P], q[:, bass.ds(h * P, P)],
                                    start=True, stop=True)
        last.then_inc(turned_full, 1)

    def weigh(pe, h, c):
        if c % (GRP // 2) == 0:
            pe.wait_ge(v_loaded[c // (GRP // 2)], h * 16 + 16)
        if c == 0:
            pe.wait_ge(parts_ready, h + 1)
        pe.wait_ge(exp_done, h * GRP + c + 1 + 2)
        for i in range(GC):
            k = c * GC + i
            at = k % tiles * (P // tiles)
            last = nc.tensor.matmul(out_ps[at:at + VW, 0:P], v_half[k // (CH // 2)][:, k % (CH // 2), :],
                                    pT[c % ring][:, i * P:(i + 1) * P], start=(k < tiles), stop=(k >= CH - tiles))
        last.then_inc(weighed, 1)

    def sum_tiles(pe, h):
        pe.wait_ge(parts_ready, h + 2)
        nc.tensor.matmul(sum_ps[:, 0:VW], out_parts[:, :], select[:, :], start=True, stop=True).then_inc(summed, 1)

    def turn_max(pe, h):
        pe.wait_ge(nm_ready, h + 1)
        nc.tensor.transpose(nmT_ps[0:3, 0:P], nm_parts[:, :], com.identb[:, :]).then_inc(nmT_in_psum, 1)

    def tensor_head(pe, h, s, following, after, first):
        pe.wait_ge(q_ready, h + 1)
        for c in range(GRP + lag):
            banks = list(range(first_bank[c], first_bank[c] + per_slot[c])) if c < GRP and following is not None else []
            for b in banks[:1]:
                scores(pe, following, 1 - s, b)
            if c < GRP:
                turned(pe, h, s, c)
            for b in banks[1:2]:
                scores(pe, following, 1 - s, b)
            if c >= lag:
                weigh(pe, h, c - lag)
            for b in banks[2:]:
                scores(pe, following, 1 - s, b)
            if c == 1 and not first:
                sum_tiles(pe, h - 1)
            if c == GRP - 1 and following is not None:
                turn_max(pe, h + 1)
            if GRP <= c < GRP + EARLY and after is not None:
                scores(pe, after, s, c - GRP)

    def on_tensor(pe):
        pe.wait_ge(cleared, 2)
        pe.wait_ge(fill_loaded, 64)
        for b in range(NB):
            scores(pe, 0, 0, b)
        turn_max(pe, 0)
        for b in range(EARLY):
            scores(pe, 1, 1, b)
        tensor_head(pe, 0, 0, 1, 2, True)
        tensor_head(pe, 1, 1, 2, 3, False)
        with pe.Fori(1, HEADS // 2 - 1) as i:
            tensor_head(pe, i * 2, 0, (i, 1), (i + 1, 0), False)
            tensor_head(pe, i * 2 + 1, 1, (i + 1, 0), (i + 1, 1), False)
        tensor_head(pe, HEADS - 2, 0, HEADS - 1, None, False)
        tensor_head(pe, HEADS - 1, 1, None, None, False)
        sum_tiles(pe, HEADS - 1)

    def take_scores(dve, h, b):
        dve.wait_ge(scores_full, h * NB + b + 1)
        nc.vector.reduce_max(rowmax[:, b:b + 1], scores_ps[b % 2][:, 0:HB], AX).then_inc(scores_taken, 1)

    def maxima(dve, h):
        n = 6
        dve.wait_ge(scores_taken, (h + 1) * NB + 2)
        nc.vector.reduce_max(nm[:, :], rowmax[:, :], AX).then_inc(nm_step, 1)
        dve.wait_ge(nm_step, h * n + 1)
        nc.vector.tensor_scalar(nm[:, :], nm[:, :], -1.0, None, ALU.mult).then_inc(nm_step, 1)
        for i in range(3):
            dve.wait_ge(nm_step, h * n + 2 * i + 2)
            nc.vector.tensor_copy(nm_parts[:, i:i + 1], nm[:, :]).then_inc(nm_ready if i == 2 else nm_step, 1)
            if i < 2:
                dve.wait_ge(nm_step, h * n + 2 * i + 3)
                nc.vector.tensor_tensor(nm[:, :], nm[:, :], nm_parts[:, i:i + 1], ALU.subtract).then_inc(nm_step, 1)

    def place_maxima(dve, h):
        dve.wait_ge(nmT_in_psum, h + 1)
        nc.vector.tensor_copy(q[MX:MX + 3, bass.ds(h * P, P)], nmT_ps[0:3, 0:P]).then_inc(q_ready, 1)

    def leave_bank(dve, h):
        dve.wait_ge(weighed, h * GRP + GRP + ring)
        nc.vector.tensor_copy(out_parts[:, :], out_ps[:, 0:P]).then_inc(parts_ready, 1)

    def divide(dve, h):
        dve.wait_ge(summed, h + 1)
        nc.vector.reciprocal(inverse[:, :], sum_ps[:, VW - 1:VW]).then_inc(out_step, 1)
        dve.wait_ge(out_step, h + 1)
        nc.vector.tensor_scalar(att[:, bass.ds(h * 16, 16)], sum_ps[:, 0:16], inverse[:, 0:1], None,
                                ALU.mult).then_inc(out_taken, 1)

    def vector_head(dve, h, following, after, first):
        for c in range(GRP):
            if following:
                for b in range(first_bank[c], first_bank[c] + per_slot[c]):
                    take_scores(dve, h + 1, b)
            if c == 3 and not first:
                divide(dve, h - 1)
        if following:
            maxima(dve, h + 1)
            place_maxima(dve, h + 1)
        if after:
            for b in range(EARLY):
                take_scores(dve, h + 2, b)
        leave_bank(dve, h)

    def on_vector(dve):
        nc.vector.memset(out_ps[:, 0:P], 0.0)
        nc.vector.reduce_sum(select[:, :], com.ident[:, :].rearrange("p (a e) -> p e a", a=tiles)[:, 0:VW, :],
                             AX).then_inc(cleared, 1)
        for b in range(NB):
            take_scores(dve, 0, b)
        maxima(dve, 0)
        place_maxima(dve, 0)
        for b in range(EARLY):
            take_scores(dve, 1, b)
        vector_head(dve, 0, True, True, True)
        with dve.Fori(1, HEADS - 2) as h:
            vector_head(dve, h, True, True, False)
        vector_head(dve, HEADS - 2, True, False, False)
        vector_head(dve, HEADS - 1, False, False, False)
        divide(dve, HEADS - 1)
        dve.wait_ge(out_taken, HEADS)

    def on_pool(pool):
        for s in range(2):
            for j in range(2):
                last = nc.gpsimd.memset(kt[s][j][MX:MX + 3, :], 1.0)
        last.then_inc(cleared, 1)

    def on_scalar(act):
        turn = 4
        with act.Fori(0, HEADS // turn) as g:
            for c in range(turn * GRP):
                act.wait_ge(turned_full, g * turn * GRP + c + 1)
                act.wait_ge(weighed, g * turn * GRP + c + 1)
                nc.scalar.activation(pT[c % ring][:, :], turned_ps[c % 2][:, 0:GW], ACT.Exp).then_inc(exp_done, 1)

    run.turned_ps = turned_ps
    run.on_sync, run.on_tensor, run.on_vector, run.on_scalar, run.on_pool = (
        on_sync, on_tensor, on_vector, on_scalar, on_pool)
    return run


def l0_cross_attention(nc, com, a, scr):
    with phase(nc, "l0x") as ph:
        att = ph.sb("att", [P, D])
        attT = ph.sb("attT", [P, KT, P])
        wv = ph.sb("wv", [P, KT, D])
        run = head_stream(nc, ph, com, 1, D, att,
                          lambda h, c: a["ctx_1024"][0, c * GW:(c + 1) * GW, :]
                          .rearrange("(c p) d -> p c d", p=P))
        last_ps = ph.ps("last", [P, 512])
        wv_loaded, attT_in_psum, attT_ready, y_in_psum, x_ready = (
            ph.sem(s) for s in ("wv_loaded", "attT_in_psum", "attT_ready", "y_in_psum", "x_ready"))
        with nc.Block() as block:
            @block.sync
            def _(sp):
                run.on_sync(sp)
                sp.dma_start(wv[:, :, :], a["L0_xattn_W_v"].rearrange("(k p) n -> p k n", p=P)).then_inc(wv_loaded, 16)

            @block.tensor
            def _(pe):
                run.on_tensor(pe)
                pe.wait_ge(run.out_taken, 2)
                for k in range(KT):
                    last = nc.tensor.transpose(last_ps[:, k * P:(k + 1) * P], att[:, k * P:(k + 1) * P], com.ident[:, :])
                last.then_inc(attT_in_psum, 1)
                pe.wait_ge(attT_ready, 1)
                pe.wait_ge(wv_loaded, 16)
                for k in range(KT):
                    last = nc.tensor.matmul(last_ps[:, D:2 * D], attT[:, k, :], wv[:, k, :],
                                            start=(k == 0), stop=(k == KT - 1))
                last.then_inc(y_in_psum, 1)

            @block.vector
            def _(dve):
                run.on_vector(dve)
                dve.wait_ge(attT_in_psum, 1)
                nc.vector.tensor_copy(attT[:, :, :].rearrange("p k n -> p (k n)"), last_ps[:, 0:D]).then_inc(attT_ready, 1)
                dve.wait_ge(y_in_psum, 1)
                nc.vector.tensor_tensor(com.x[:, :], last_ps[:, D:2 * D], com.x[:, :], ALU.add).then_inc(x_ready, 1)
                dve.wait_ge(x_ready, 1)

            @block.scalar
            def _(act):
                run.on_scalar(act)


class StateKernel:

    def __init__(self, nc, ph, com, a):
        self.nc, self.com, self.a = nc, com, a
        N = a["L1_attn_A_log"].shape[1]
        S = ph.sem
        self.n = N // HEADS * KT
        self.dt = ph.sb("dt", [P, KT])
        self.a_log, self.b, self.c, self.rate, self.weight = (
            ph.sb(m, [P, KT, N]) for m in ("a_log", "b_st", "c_st", "rate", "weight"))
        self.steps_i, self.steps = ph.sb("steps_i", [P, P], I32), ph.sb("steps", [P, P])
        self.powers = [ph.sb(f"powers{i}", [P, P]) for i in range(self.n)]
        (self.loaded, self.decay_ready, self.weight_step, self.rate_ready, self.steps_step, self.k_step,
         self.powers_ready) = (S(s) for s in ("states_loaded", "decay_ready", "weight_step", "rate_ready", "steps_step",
                                              "k_step", "powers_ready"))

    def on_sync(self, sp):
        sp.sem_inc(self.k_step, self.n)
        for t, name in ((self.a_log, "A_log"), (self.b, "B"), (self.c, "C")):
            sp.dma_start(t[:, :, :], self.a["L1_attn_" + name].rearrange("(k p) n -> p k n", p=P)).then_inc(self.loaded, 16)
        sp.dma_start(self.dt[:, :], self.a["L1_attn_dt"].rearrange("(k p) -> p k", p=P),
                     allow_slow_non_contiguous=True).then_inc(self.loaded, 16)

    def on_pool(self, pool):
        nc = self.nc
        nc.gpsimd.iota(self.steps_i[:, :], pattern=[[-1, P]], base=P - 1, channel_multiplier=0).then_inc(self.steps_step, 1)
        pool.wait_ge(self.steps_step, 1)
        nc.gpsimd.tensor_copy(self.steps[:, :], self.steps_i[:, :]).then_inc(self.steps_step, 1)
        nc.gpsimd.memset(self.com.k_rev[:, :, :], 0.0).then_inc(self.steps_step, 1)
        pool.wait_ge(self.steps_step, 3)

    def scalar_front(self, act):
        act.wait_ge(self.loaded, 64)
        self.nc.scalar.activation(self.a_log[:, :, :], self.a_log[:, :, :], ACT.Exp, bias=0.0,
                                  scale=-1.0).then_inc(self.decay_ready, 1)
        act.wait_ge(self.rate_ready, KT)
        act.wait_ge(self.steps_step, 3)

    def vector_front(self, dve):
        nc = self.nc
        dve.wait_ge(self.loaded, 64)
        dve.wait_ge(self.decay_ready, 1)
        for t in range(KT):
            nc.vector.tensor_scalar(self.rate[:, t, :], self.a_log[:, t, :], self.dt[:, t:t + 1], -1.0,
                                    ALU.mult, ALU.mult).then_inc(self.rate_ready, 1)
            nc.vector.tensor_scalar(self.b[:, t, :], self.b[:, t, :], self.dt[:, t:t + 1], None,
                                    ALU.mult).then_inc(self.weight_step, 1)
        dve.wait_ge(self.weight_step, KT)
        nc.vector.tensor_tensor(self.weight[:, :, :], self.c[:, :, :], self.b[:, :, :], ALU.mult).then_inc(self.weight_step, 1)
        dve.wait_ge(self.weight_step, KT + 1)
        dve.wait_ge(self.steps_step, 3)

    def scalar_step(self, act, h, c):
        if c < self.n:
            act.wait_ge(self.k_step, h * self.n + c + 1)
            self.nc.scalar.activation(self.powers[c][:, :], self.steps[:, :], ACT.Exp, bias=0.0,
                                      scale=self.rate[:, c % KT, bass.ds(h * (self.n // KT) + c // KT, 1)]
                                      ).then_inc(self.powers_ready, 1)

    def vector_step(self, dve, h, c):
        i = c - 3
        if 0 <= i < self.n:
            k = self.com.k_rev[:, i % KT, :]
            dve.wait_ge(self.powers_ready, h * self.n + i + 1)
            dve.wait_ge(self.k_step, h * self.n + i + self.n - 1)
            self.nc.vector.scalar_tensor_tensor(out=k, in0=self.powers[i][:, :],
                                                scalar=self.weight[:, i % KT, bass.ds(h * (self.n // KT) + i // KT, 1)],
                                                in1=k, op0=ALU.mult, op1=ALU.add).then_inc(self.k_step, 1)

    def vector_end(self, dve):
        dve.wait_ge(self.k_step, self.n * (HEADS + 1))


def cross_attention_16(nc, com, a, scr, layer):
    n = layer.lower()
    w = {k: a[f"{layer}_xattn_{k}"] for k in ("Wq", "bq", "bv", "Wo", "bo")}
    masked = layer == "L3"
    rows = STACK + 6 if masked else STACK
    k_dram, v_dram = scr.kparts["k" + n[1]], scr.v["v" + n[1]]
    with phase(nc, n + "x") as ph:
        att = ph.sb("att", [P, D])
        attT = ph.sb("attT", [P, KT, P])
        nat = {k: ph.sb("nat" + k, [P, KT, D]) for k in ("Wq", "Wo")}
        wT = {k: ph.sb("T" + k, [P, KT, D]) for k in nat}
        bb = {k: ph.sb("b_" + k, [P, D]) for k in ("bq", "bv", "bo")}
        qf, qp = ph.sb("qf", [P, D]), [ph.sb(f"qp{i}", [P, D], BF16) for i in range(3)]
        q_nat = ph.sb("q_nat", [P, HEADS, STACK], BF16)
        q_stack = ph.sb("q_stack", [rows, HEADS * P], BF16)
        k_half = None if masked else [ph.sb(f"k_half{j}", [rows, SK // 2], BF16) for j in range(2)]

        def k_load(tile, h, j):
            cols = slice(j * (SK // 2), (j + 1) * (SK // 2))
            return [(tile[i * 16:(i + 1) * 16, :], k_dram[piece, bass.ds(h * 16, 16), cols])
                    for i, piece in enumerate(PIECES)]

        fside = a["fside_Bx16xSxS2_0"]
        last_ps = ph.ps("last", [P, 512])

        def v_src(h, j):
            return v_dram[bass.ds(h, 1), :, j * (CH // 2):(j + 1) * (CH // 2), :].rearrange("a p c e -> (a p) c e")
        states = None if masked else StateKernel(nc, ph, com, a)
        if masked:
            run = head_stream_turned(nc, ph, com, att, v_src, q_stack, k_load, scr.fill, last_ps)
        else:
            run = head_stream(nc, ph, com, HEADS, 16, att, v_src, q=q_stack, k_half=k_half,
                              k_loads=lambda h, j: k_load(k_half[j], h, j),
                              bias=lambda h, i: fside[0, bass.ds(h, 1), :, i * 2 * GW:(i + 1) * 2 * GW]
                              .rearrange("a p s -> (a p) s"), lag=5, by_vector=(3, 6, 9, 12), sum_ps=last_ps,
                              beside=states)
        qT_ps = last_ps[:, :].bitcast(BF16)
        norm_vector, norm_scalar, norm_tensor = token_norm(
            nc, ph, com, last_ps[:, 0:D].rearrange("p (k n) -> p k n", k=KT))
        loaded, wT_in_psum, wT_ready, q_in_psum, q_step, q_nat_ready, qT_in_psum, q_ready = (
            ph.sem(s) for s in ("loaded", "wT_in_psum", "wT_ready", "q_in_psum", "q_step", "q_nat_ready",
                                "qT_in_psum", "q_ready"))
        att_stored, att_read, att_ready, attT_in_psum, attT_ready, y_in_psum, x_step = (
            ph.sem(s) for s in ("att_stored", "att_read", "att_ready", "attT_in_psum", "attT_ready", "y_in_psum", "x_step"))
        rows_set = ph.sem("rows_set")
        with nc.Block() as block:
            @block.sync
            def _(sp):
                for k in nat:
                    sp.dma_start(nat[k][:, :, :], w[k].rearrange("(k p) n -> p k n", p=P)).then_inc(loaded, 16)
                for k in bb:
                    sp.dma_start(bb[k][:, :], w[k].partition_broadcast(P)).then_inc(loaded, 16)
                if not masked:
                    states.on_sync(sp)
                run.on_sync(sp)
                if not masked:
                    sp.wait_ge(att_ready, 1)
                    sp.dma_start(scr.att1.rearrange("h t e -> t h e"),
                                 att[:, :].rearrange("t (h e) -> t h e", e=16)).then_inc(att_stored, 16)
                    sp.wait_ge(att_stored, 16)
                    sp.dma_start(att[:, :], scr.att1.rearrange("h (a b) e -> (h a) (b e)", b=16)).then_inc(att_read, 16)

            @block.tensor
            def _(pe):
                pe.wait_ge(loaded, 16 * 5)
                for i, k_ in enumerate(nat):
                    for k in range(KT):
                        for o in range(KT):
                            last = nc.tensor.transpose(run.turned_ps[i][:, (k * KT + o) * P:(k * KT + o + 1) * P],
                                                       nat[k_][:, o, k * P:(k + 1) * P], com.ident[:, :])
                    last.then_inc(wT_in_psum, 1)
                norm_tensor(pe)
                pe.wait_ge(wT_ready, 2)
                for k in range(KT):
                    last = nc.tensor.matmul(last_ps[:, 0:D], com.xnT[:, k, :], wT["Wq"][:, k, :],
                                            start=(k == 0), stop=(k == KT - 1))
                last.then_inc(q_in_psum, 1)
                pe.wait_ge(q_nat_ready, 1)
                for half in range(2):
                    if half:
                        pe.wait_ge(q_ready, 1)
                    for h in range(8):
                        last = nc.tensor.transpose(qT_ps[0:STACK, h * P:(h + 1) * P], q_nat[:, half * 8 + h, :],
                                                   com.identb[:, :])
                    last.then_inc(qT_in_psum, 1)
                pe.wait_ge(q_ready, 2)
                run.on_tensor(pe)
                pe.wait_ge(att_ready, 1)
                if not masked:
                    pe.wait_ge(att_read, 16)
                for k in range(KT):
                    last = nc.tensor.transpose(last_ps[:, k * P:(k + 1) * P], att[:, k * P:(k + 1) * P], com.ident[:, :])
                last.then_inc(attT_in_psum, 1)
                pe.wait_ge(attT_ready, 1)
                for k in range(KT):
                    last = nc.tensor.matmul(last_ps[:, D:2 * D], attT[:, k, :], wT["Wo"][:, k, :],
                                            start=(k == 0), stop=(k == KT - 1))
                last.then_inc(y_in_psum, 1)

            @block.vector
            def _(dve):
                norm_vector(dve)
                if masked:
                    nc.vector.memset(q_stack[STACK:STACK + 6, :], 1.0).then_inc(rows_set, 1)
                    dve.wait_ge(rows_set, 1)
                    nc.vector.memset(q_stack[STACK:STACK + 3, :], 0.0).then_inc(rows_set, 1)
                    dve.wait_ge(rows_set, 2)
                dve.wait_ge(q_in_psum, 1)
                dve.wait_ge(loaded, 16 * 5)
                nc.vector.tensor_tensor(qf[:, :], last_ps[:, 0:D], bb["bq"][:, :], ALU.add).then_inc(q_step, 1)
                dve.wait_ge(q_step, 1)
                nc.vector.tensor_scalar(qf[:, :], qf[:, :], 0.25, None, ALU.mult).then_inc(q_step, 1)
                dve.wait_ge(q_step, 2)
                for i in range(3):
                    nc.vector.tensor_copy(qp[i][:, :], qf[:, :]).then_inc(q_step, 1)
                    dve.wait_ge(q_step, 2 * i + 3)
                    if i < 2:
                        nc.vector.tensor_tensor(qf[:, :], qf[:, :], qp[i][:, :], ALU.subtract).then_inc(q_step, 1)
                        dve.wait_ge(q_step, 2 * i + 4)
                for i, piece in enumerate(QPIECES):
                    last = nc.vector.tensor_copy(q_nat[:, :, i * 16:(i + 1) * 16],
                                                 qp[piece][:, :].rearrange("p (h e) -> p h e", e=16))
                last.then_inc(q_nat_ready, 1)
                for half in range(2):
                    dve.wait_ge(qT_in_psum, half + 1)
                    nc.vector.tensor_copy(q_stack[0:STACK, half * 8 * P:(half + 1) * 8 * P],
                                          qT_ps[0:STACK, :]).then_inc(q_ready, 1)
                if not masked:
                    states.vector_front(dve)
                run.on_vector(dve)
                if not masked:
                    states.vector_end(dve)
                nc.vector.tensor_tensor(att[:, :], att[:, :], bb["bv"][:, :], ALU.add).then_inc(att_ready, 1)
                dve.wait_ge(attT_in_psum, 1)
                nc.vector.tensor_copy(attT[:, :, :].rearrange("p k n -> p (k n)"), last_ps[:, 0:D]).then_inc(attT_ready, 1)
                nc.vector.tensor_tensor(com.x[:, :], com.x[:, :], bb["bo"][:, :], ALU.add).then_inc(x_step, 1)
                dve.wait_ge(x_step, 1)
                dve.wait_ge(y_in_psum, 1)
                nc.vector.tensor_tensor(com.x[:, :], last_ps[:, D:2 * D], com.x[:, :], ALU.add).then_inc(x_step, 1)
                dve.wait_ge(x_step, 2)

            @block.scalar
            def _(act):
                norm_scalar(act)
                for i, k in enumerate(nat):
                    act.wait_ge(wT_in_psum, i + 1)
                    nc.scalar.copy(wT[k][:, :, :].rearrange("p k n -> p (k n)"),
                                   run.turned_ps[i][:, 0:512]).then_inc(wT_ready, 1)
                if not masked:
                    states.scalar_front(act)
                run.on_scalar(act)

            @block.gpsimd
            def _(pool):
                if masked:
                    run.on_pool(pool)
                else:
                    states.on_pool(pool)


def l2_cross_attention(nc, com, a, scr):
    with phase(nc, "l2x") as ph:
        VW = 64
        W = HEADS * VW
        att = ph.sb("att", [P, W])
        ctxT = ph.sb("ctxT", [P, KT, SK])
        q_fold = ph.sb("q_fold", [P, HEADS * KT * P])
        q_cur = ph.sb("q_cur", [P, KT, P])
        last_ps = ph.ps("last", [P, 512])
        at = [0]

        def scratch(*shape):
            n = int(np.prod(shape))
            v = com.S[:, at[0]:at[0] + n]
            at[0] += n
            return v.rearrange("p (a b) -> p a b", a=shape[0])
        wq, wk, wkT, qT = scratch(KT, W), scratch(KT, W), scratch(8, D), scratch(8, P)
        at[0] = 0
        wo, attT = scratch(8, D), scratch(8, P)
        ctx_loaded = [ph.sem(f"ctx_loaded{i}") for i in range(GRP // 2)]
        run = head_stream(nc, ph, com, HEADS, VW, att,
                          lambda h, j: scr.v["v2"][bass.ds(h, 1), :, j * (CH // 2):(j + 1) * (CH // 2), :]
                          .rearrange("a p c e -> (a p) c e"),
                          ring=2, lag=1, q_cur=q_cur, ctxT=ctxT, ctx_loaded=ctx_loaded, sum_ps=last_ps)
        norm_vector, norm_scalar, norm_tensor = token_norm(
            nc, ph, com, last_ps[:, 0:D].rearrange("p (k n) -> p k n", k=KT))
        loaded, front_in_psum, front_ready, q_cur_ready = (
            ph.sem(s) for s in ("loaded", "front_in_psum", "front_ready", "q_cur_ready"))
        wo_loaded, attT_in_psum, attT_ready, y_in_psum, x_ready = (
            ph.sem(s) for s in ("wo_loaded", "attT_in_psum", "attT_ready", "y_in_psum", "x_ready"))
        banks = run.turned_ps
        with nc.Block() as block:
            @block.sync
            def _(sp):
                for t, src in ((wq, a["L2_xattn_Wq"]), (wk, a["L2_xattn_Wk"])):
                    sp.dma_start(t, src.rearrange("(k p) n -> p k n", p=P)).then_inc(loaded, 16)
                for i in range(GRP // 2):
                    cols = slice(i * 2 * GW, (i + 1) * 2 * GW)
                    sp.dma_start(ctxT[:, :, cols], scr.ctxT[:, :, cols]).then_inc(ctx_loaded[i], 16)
                run.on_sync(sp)
                sp.wait_ge(run.turned, HEADS * GRP)
                sp.dma_start(wo, a["L2_xattn_Wo"].rearrange("(k p) n -> p k n", p=P)).then_inc(wo_loaded, 16)

            @block.tensor
            def _(pe):
                pe.wait_ge(loaded, 32)
                for r in range(2):
                    for t in range(8):
                        e, k = r * 4 + t // 2, t % 2
                        last = nc.tensor.transpose(banks[r][:, t * P:(t + 1) * P], wk[:, k, e * P:(e + 1) * P],
                                                   com.ident[:, :])
                    last.then_inc(front_in_psum, 1)
                norm_tensor(pe)
                pe.wait_ge(front_ready, 1)
                for e in range(8):
                    for k in range(KT):
                        last = nc.tensor.matmul(banks[0][:, e * P:(e + 1) * P], wq[:, k, e * P:(e + 1) * P],
                                                com.xnT[:, k, :], start=(k == 0), stop=(k == KT - 1))
                last.then_inc(front_in_psum, 1)
                pe.wait_ge(front_ready, 3)
                for r in range(4):
                    if r:
                        pe.wait_ge(front_ready, r + 2)
                    for t in range(8):
                        h, k = r * 4 + t // 2, t % 2
                        rows = slice(h % 2 * VW, h % 2 * VW + VW)
                        at_col = h % 2 * 512 + t // 4 * KT * P + k * P
                        last = nc.tensor.matmul(banks[(r + 1) % 2][:, at_col:at_col + P],
                                                wkT[rows, h // 2, k * P:(k + 1) * P], qT[rows, h // 2, :],
                                                start=True, stop=True)
                    last.then_inc(front_in_psum, 1)
                pe.wait_ge(front_ready, 7)
                run.on_tensor(pe, before_scores=lambda pe, h: pe.wait_ge(q_cur_ready, h + 1))
                pe.wait_ge(run.out_taken, HEADS + 1)
                for e in range(8):
                    last = nc.tensor.transpose(banks[0][:, e * P:(e + 1) * P], att[:, e * P:(e + 1) * P], com.ident[:, :])
                last.then_inc(attT_in_psum, 1)
                pe.wait_ge(attT_ready, 1)
                pe.wait_ge(wo_loaded, 16)
                for e in range(8):
                    last = nc.tensor.matmul(last_ps[:, 0:D], attT[:, e, :], wo[:, e, :], start=(e == 0), stop=(e == 7))
                last.then_inc(y_in_psum, 1)

            @block.gpsimd
            def _(pool):
                def take_query(h):
                    nc.gpsimd.tensor_copy(q_cur[:, :, :].rearrange("p k n -> p (k n)"),
                                          q_fold[:, bass.ds(h * KT * P, KT * P)]).then_inc(q_cur_ready, 1)
                pool.wait_ge(front_ready, 7)
                take_query(0)
                with pool.Fori(1, HEADS) as h:
                    pool.wait_ge(run.scores_full, h * 2 * GRP)
                    take_query(h)

            @block.vector
            def _(dve):
                norm_vector(dve)
                for r in range(2):
                    dve.wait_ge(front_in_psum, r + 1)
                    nc.vector.tensor_copy(wkT[:, r * 4:(r + 1) * 4, :].rearrange("p a b -> p (a b)"),
                                          banks[r][:, :]).then_inc(front_ready, 1)
                dve.wait_ge(front_in_psum, 3)
                nc.vector.tensor_copy(qT.rearrange("p a b -> p (a b)"), banks[0][:, :]).then_inc(front_ready, 1)
                for r in range(4):
                    dve.wait_ge(front_in_psum, r + 4)
                    nc.vector.tensor_scalar(q_fold[:, r * 1024:(r + 1) * 1024]
                                            .rearrange("p (pair odd n) -> p odd pair n", odd=2, n=KT * P),
                                            banks[(r + 1) % 2][:, :]
                                            .rearrange("p (odd pair n) -> p odd pair n", odd=2, n=KT * P), 0.125, None,
                                            ALU.mult).then_inc(front_ready, 1)
                run.on_vector(dve)
                dve.wait_ge(attT_in_psum, 1)
                nc.vector.tensor_copy(attT.rearrange("p a b -> p (a b)"), banks[0][:, :]).then_inc(attT_ready, 1)
                dve.wait_ge(y_in_psum, 1)
                nc.vector.tensor_tensor(com.x[:, :], last_ps[:, 0:D], com.x[:, :], ALU.add).then_inc(x_ready, 1)
                dve.wait_ge(x_ready, 1)

            @block.scalar
            def _(act):
                norm_scalar(act)
                run.on_scalar(act)



EU = 4
FILL = -3.0e38
MARK = 3.0e38


def gate_steps(nc, ph, com, E, top, eps=0.0, tau=None):
    lg, top8 = ph.sb("logits", [P, E + 8]), ph.sb("top8", [P, 8])
    marked, gates = ph.sb("marked", [P, E + 8]), ph.sb("gates", [P, E])
    prob, one = ph.sb("prob", [P, E + 8]), [ph.sb(f"gate_col{i}", [P, 1]) for i in range(4)]
    big, total, inverse, wsum = one
    gate_step, gate_exp, gates_ready = ph.sem("gate_step"), ph.sem("gate_exp"), ph.sem("gates_ready")

    def on_vector(dve, logits_ps, bias=None):
        n = [0]

        def then(ins):
            n[0] += 1
            ins.then_inc(gate_step, 1)
            dve.wait_ge(gate_step, n[0])
        nc.vector.memset(lg[:, E:E + 8], FILL)
        nc.vector.memset(prob[:, E:E + 8], FILL)
        if bias is None:
            then(nc.vector.tensor_copy(lg[:, 0:E], logits_ps))
        else:
            then(nc.vector.tensor_tensor(lg[:, 0:E], logits_ps, bias, ALU.add))
        if tau is not None:
            then(nc.vector.tensor_scalar(lg[:, 0:E], lg[:, 0:E], 1.0 / tau, None, ALU.mult))
        then(nc.vector.reduce_max(big[:, :], lg[:, 0:E], AX))
        then(nc.vector.tensor_scalar(big[:, :], big[:, :], -1.0, None, ALU.mult))
        dve.wait_ge(gate_exp, 1)
        if tau is None:
            then(nc.vector.reciprocal(inverse[:, :], total[:, :]))
            then(nc.vector.tensor_scalar(prob[:, 0:E], prob[:, 0:E], inverse[:, 0:1], None, ALU.mult))
        ranked = lg if tau is not None else prob
        then(nc.vector.max(top8[:, :], ranked[:, :]))
        then(nc.vector.memset(top8[:, top:8], FILL))
        then(nc.vector.match_replace(marked[:, :], top8[:, :], ranked[:, :], MARK))
        then(nc.vector.tensor_scalar(marked[:, 0:E], marked[:, 0:E], MARK, None, ALU.is_equal))
        then(nc.vector.tensor_tensor(marked[:, 0:E], marked[:, 0:E], prob[:, 0:E], ALU.mult))
        then(nc.vector.reduce_sum(wsum[:, :], marked[:, 0:E], AX))
        if eps:
            then(nc.vector.tensor_scalar(wsum[:, :], wsum[:, :], eps, None, ALU.add))
        then(nc.vector.reciprocal(wsum[:, :], wsum[:, :]))
        nc.vector.tensor_scalar(gates[:, :], marked[:, 0:E], wsum[:, 0:1], None, ALU.mult).then_inc(gates_ready, 1)
        dve.wait_ge(gates_ready, 1)

    def on_scalar(act):
        act.wait_ge(gate_step, 3 if tau is None else 4)
        nc.scalar.activation(prob[:, 0:E], lg[:, 0:E], ACT.Exp, bias=big[:, 0:1], scale=1.0,
                             accum_out=total[:, 0:1]).then_inc(gate_exp, 1)

    return on_vector, on_scalar, gates, gates_ready


def experts(nc, com, a, name, E, top, router, ups, down, hid, act_func, act_at, lin_at=None, U=1, T=4, eps=0.0,
            tau=None, router_bias=None, up_bias=None, down_bias=None, shared=None):
    two = lin_at is not None
    cols = sum(u.shape[-1] for u in ups)
    n_bias = cols // P
    HT = hid // P
    with phase(nc, name) as ph:
        S = ph.sem
        up_w = [ph.sb(f"up{j}", [P, KT, cols]) for j in range(EU)]
        down_w = [ph.sb(f"down{j}", [P, HT, D]) for j in range(EU)]
        h_act = [ph.sb(f"h_act{i}", [P, 512]) for i in range(2)] if two else None
        h = [ph.sb(f"h{i}", [P, 512]) for i in range(2)]
        acc = ph.sb("acc", [P, D])
        wr = ph.sb("wr", [P, KT, E])
        act_ps = [ph.ps(f"act{i}", [P, 512]) for i in range(2)]
        lin_ps = [ph.ps(f"lin{i}", [P, 512]) for i in range(2)] if two else None
        out_ps = [ph.ps(f"out{i}", [P, 512]) for i in range(2)]
        misc_ps = ph.ps("misc", [P, 512])
        rb = ph.sb("rb", [P, E]) if router_bias is not None else None
        n_rows = E * n_bias
        if up_bias is not None:
            blocks = [(r, min(n_rows, r + P) - r) for r in range(0, n_rows, P)]
            bias_nat = ph.sb("bias_nat", [P, len(blocks), P])
            biasT = ph.sb("biasT", [P, n_rows])
        if down_bias is not None:
            db, gatesT = ph.sb("db", [E, D]), ph.sb("gatesT", [E, P])
        n_shared = 0
        if shared is not None:
            n_shared = 1
            s_hid, s_ups, s_down, s_bias, s_down_bias, s_lin = shared
            s_cols = sum(u.shape[-1] for u in s_ups)
            s_up, s_dn = ph.sb("s_up", [P, KT, s_cols]), ph.sb("s_down", [P, s_hid // P, D])
            if s_bias is not None:
                sb_nat, sbT = ph.sb("sb_nat", [8, P]), ph.sb("sbT", [P, 8])
                sdb = ph.sb("sdb", [P, D])
        gate_vector, gate_scalar, gates, gates_ready = gate_steps(nc, ph, com, E, top, eps, tau)
        norm_vector, norm_scalar, norm_tensor = token_norm(
            nc, ph, com, misc_ps[:, 0:D].rearrange("p (k n) -> p k n", k=KT))
        small_loaded, shared_loaded, held = S("small_loaded"), S("shared_loaded"), S("held")
        w_loaded = [S(f"w_loaded{j}") for j in range(EU)]
        logits_full, bias_in_psum, bias_ready, gatesT_in_psum, gatesT_ready, start_in_psum, acc_started = (
            S(s) for s in ("logits_full", "bias_in_psum", "bias_ready", "gatesT_in_psum", "gatesT_ready",
                           "start_in_psum", "acc_started"))
        up_full, act_done, h_ready, down_done, acc_done = (
            S(s) for s in ("up_full", "act_done", "h_ready", "down_done", "acc_done"))
        x_ready = S("x_ready")
        n_dma = len(ups) + 1
        n_small = 1 + (router_bias is not None) + (down_bias is not None)
        if up_bias is not None:
            n_small += len(blocks)
        if shared is not None and s_bias is not None:
            n_small += 2

        with nc.Block() as block:
            @block.sync
            def _(sp):
                for s in (h_ready, down_done, acc_done):
                    sp.sem_inc(s, 2)
                sp.dma_start(wr[:, :, :], router.rearrange("(k p) n -> p k n", p=P)).then_inc(small_loaded, 16)
                if router_bias is not None:
                    sp.dma_start(rb[:, :], router_bias.partition_broadcast(P)).then_inc(small_loaded, 16)
                if down_bias is not None:
                    sp.dma_start(db[:, :], down_bias).then_inc(small_loaded, 16)
                if up_bias is not None:
                    rows = up_bias.rearrange("e (t p) -> (e t) p", p=P)
                    for i, (r, n) in enumerate(blocks):
                        sp.dma_start(bias_nat[0:n, i, :], rows[r:r + n, :]).then_inc(small_loaded, 16)
                if shared is not None:
                    if s_bias is not None:
                        sp.dma_start(sb_nat[:, :], s_bias.rearrange("(t p) -> t p", p=P)).then_inc(small_loaded, 16)
                        sp.dma_start(sdb[:, :], s_down_bias.partition_broadcast(P)).then_inc(small_loaded, 16)
                    c0 = 0
                    for u in s_ups:
                        sp.dma_start(s_up[:, :, c0:c0 + u.shape[-1]],
                                     u.rearrange("(k p) n -> p k n", p=P)).then_inc(shared_loaded, 16)
                        c0 += u.shape[-1]
                    sp.dma_start(s_dn[:, :, :], s_down.rearrange("(k p) n -> p k n", p=P)).then_inc(shared_loaded, 16)

                def load(e, j):
                    c0 = 0
                    for u in ups:
                        n = u.shape[-1]
                        sp.dma_start(up_w[j][:, :, c0:c0 + n], u[bass.ds(e, 1)]
                                     .rearrange("a (k p) n -> p (a k) n", p=P)).then_inc(w_loaded[j], 16)
                        c0 += n
                    sp.dma_start(down_w[j][:, :, :], down[bass.ds(e, 1)]
                                 .rearrange("a (k p) n -> p (a k) n", p=P)).then_inc(w_loaded[j], 16)
                for j in range(EU):
                    load(j, j)
                with sp.Fori(1, E // EU) as g:
                    for j in range(EU):
                        hold(sp, held, down_done, n_shared + ((g - 1) * EU + j + 1) * U + 2)
                        load(g * EU + j, j)

            def up(pe, n, r, w, u, t_n, act0, lin0, loaded, count):
                if loaded is not None:
                    pe.wait_ge(loaded, count)
                pe.wait_ge(h_ready, n + 1)
                for bank, first in ((act_ps, act0),) + (((lin_ps, lin0),) if two else ()):
                    for t in range(t_n):
                        c = first + (u * t_n + t) * P
                        for k in range(KT):
                            last = nc.tensor.matmul(bank[r][:, t * P:(t + 1) * P], w[:, k, c:c + P], com.xnT[:, k, :],
                                                    start=(k == 0), stop=(k == KT - 1))
                last.then_inc(up_full, 1)

            def down_product(pe, n, r, w, m, o, u, u_n, t_n):
                if u == 0:
                    pe.wait_ge(acc_done, m + 1)
                pe.wait_ge(h_ready, n + 1 + 2)
                for t in range(t_n):
                    last = nc.tensor.matmul(out_ps[o][:, 0:D], h[r][:, t * P:(t + 1) * P], w[:, u * t_n + t, :],
                                            start=(u == 0 and t == 0), stop=(u == u_n - 1 and t == t_n - 1))
                last.then_inc(down_done, 1)

            local = [(j, u) for j in range(EU) for u in range(U)]

            @block.tensor
            def _(pe):
                norm_tensor(pe)
                pe.wait_ge(small_loaded, 16 * n_small)
                for k in range(KT):
                    last = nc.tensor.matmul(misc_ps[:, 256:256 + E], com.xnT[:, k, :], wr[:, k, :],
                                            start=(k == 0), stop=(k == KT - 1))
                last.then_inc(logits_full, 1)
                if up_bias is not None:
                    pe.wait_ge(acc_started, 1)
                    for i, (r, n) in enumerate(blocks):
                        last = nc.tensor.transpose(out_ps[0][:, r:r + n], bias_nat[0:n, i, :], com.ident[0:n, 0:n])
                    if shared is not None:
                        last = nc.tensor.transpose(out_ps[0][:, n_rows:n_rows + 8], sb_nat[:, :], com.ident[0:8, 0:8])
                    last.then_inc(bias_in_psum, 1)
                    pe.wait_ge(bias_ready, 1)
                if shared is not None:
                    up(pe, 0, 0, s_up, 0, s_hid // P, s_lin[0], s_lin[1], shared_loaded, 16 * (len(s_ups) + 1))
                    down_product(pe, 0, 0, s_dn, 0, 0, 0, 1, s_hid // P)
                with pe.Fori(0, E // EU) as g:
                    for i, (j, u) in enumerate(local):
                        n = n_shared + g * EU * U + i
                        up(pe, n, (n_shared + i) % 2, up_w[j], u, T, act_at, lin_at,
                           w_loaded[j] if u == 0 else None, (g + 1) * 16 * n_dma)
                        if i:
                            pj, pu = local[i - 1]
                            down_product(pe, n - 1, (n_shared + i - 1) % 2, down_w[pj], n_shared + g * EU + pj,
                                         (n_shared + pj) % 2, pu, U, T)
                    down_product(pe, n, (n_shared + i) % 2, down_w[j], n_shared + g * EU + j,
                                 (n_shared + j) % 2, u, U, T)
                if down_bias is not None:
                    pe.wait_ge(gates_ready, 1)
                    nc.tensor.transpose(misc_ps[0:E, 0:P], gates[:, :], com.ident[:, :]).then_inc(gatesT_in_psum, 1)
                    pe.wait_ge(gatesT_ready, 1)
                    nc.tensor.matmul(misc_ps[:, 256:512], gatesT[:, :], db[:, :], start=True,
                                     stop=True).then_inc(start_in_psum, 1)

            def activate(act, n, r, t_n, bias_at):
                act.wait_ge(up_full, n + 1)
                if two:
                    act.wait_ge(h_ready, n + 1)
                else:
                    act.wait_ge(down_done, n + 1)
                dst = h_act[r] if two else h[r]
                if bias_at is None:
                    last = nc.scalar.activation(dst[:, 0:t_n * P], act_ps[r][:, 0:t_n * P], act_func)
                else:
                    for t in range(t_n):
                        last = nc.scalar.activation(dst[:, t * P:(t + 1) * P], act_ps[r][:, t * P:(t + 1) * P], act_func,
                                                    bias=bias_at(t), scale=1.0)
                last.then_inc(act_done if two else h_ready, 1)

            def bias_col(g, j, u, first):
                if up_bias is None:
                    return None
                return lambda t: biasT[:, bass.ds((g * EU + j) * n_bias + first // P + u * T + t, 1)]

            @block.scalar
            def _(act):
                norm_scalar(act)
                gate_scalar(act)
                if up_bias is not None:
                    act.wait_ge(bias_ready, 1)
                if shared is not None:
                    activate(act, 0, 0, s_hid // P, None if s_bias is None else
                             (lambda t: sbT[:, s_lin[0] // P + t:s_lin[0] // P + t + 1]))
                with act.Fori(0, E // EU) as g:
                    for i, (j, u) in enumerate(local):
                        activate(act, n_shared + g * EU * U + i, (n_shared + i) % 2, T, bias_col(g, j, u, act_at))

            def hidden(dve, n, r, t_n, bias_at):
                if not two:
                    return
                dve.wait_ge(act_done, n + 1)
                dve.wait_ge(down_done, n + 1)
                if bias_at is None:
                    last = nc.vector.tensor_tensor(h[r][:, 0:t_n * P], lin_ps[r][:, 0:t_n * P], h_act[r][:, 0:t_n * P],
                                                   ALU.mult)
                else:
                    for t in range(t_n):
                        c = slice(t * P, (t + 1) * P)
                        last = nc.vector.scalar_tensor_tensor(out=h[r][:, c], in0=lin_ps[r][:, c], scalar=bias_at(t),
                                                              in1=h_act[r][:, c], op0=ALU.add, op1=ALU.mult)
                last.then_inc(h_ready, 1)

            def accumulate(dve, m, o, last_unit, gate):
                dve.wait_ge(down_done, last_unit + 1 + 2)
                dve.wait_ge(acc_done, m + 2)
                dve.wait_ge(acc_started, 1)
                if gate is None:
                    nc.vector.tensor_tensor(acc[:, :], out_ps[o][:, 0:D], acc[:, :], ALU.add).then_inc(acc_done, 1)
                else:
                    nc.vector.scalar_tensor_tensor(out=acc[:, :], in0=out_ps[o][:, 0:D], scalar=gate, in1=acc[:, :],
                                                   op0=ALU.mult, op1=ALU.add).then_inc(acc_done, 1)

            @block.vector
            def _(dve):
                norm_vector(dve)
                dve.wait_ge(small_loaded, 16 * n_small)
                if shared is not None and s_bias is not None:
                    nc.vector.tensor_tensor(acc[:, :], com.x[:, :], sdb[:, :], ALU.add).then_inc(acc_started, 1)
                else:
                    nc.vector.tensor_copy(acc[:, :], com.x[:, :]).then_inc(acc_started, 1)
                dve.wait_ge(logits_full, 1)
                gate_vector(dve, misc_ps[:, 256:256 + E], rb[:, :] if router_bias is not None else None)
                if up_bias is not None:
                    dve.wait_ge(bias_in_psum, 1)
                    if shared is not None:
                        nc.vector.tensor_copy(sbT[:, :], out_ps[0][:, n_rows:n_rows + 8])
                    nc.vector.tensor_copy(biasT[:, :], out_ps[0][:, 0:n_rows]).then_inc(bias_ready, 1)
                    dve.wait_ge(bias_ready, 1)
                if shared is not None:
                    hidden(dve, 0, 0, s_hid // P, None if s_bias is None else
                           (lambda t: sbT[:, s_lin[1] // P + t:s_lin[1] // P + t + 1]))
                    accumulate(dve, 0, 0, 0, None)
                with dve.Fori(0, E // EU) as g:
                    def weighed(j):
                        accumulate(dve, n_shared + g * EU + j, (n_shared + j) % 2, n_shared + (g * EU + j + 1) * U - 1,
                                   gates[:, bass.ds(g * EU + j, 1)])
                    for i, (j, u) in enumerate(local):
                        hidden(dve, n_shared + g * EU * U + i, (n_shared + i) % 2, T,
                               bias_col(g, j, u, lin_at) if two else None)
                        if u == 0 and j:
                            weighed(j - 1)
                    weighed(EU - 1)
                dve.wait_ge(acc_done, 2 + n_shared + E)
                if down_bias is not None:
                    dve.wait_ge(gatesT_in_psum, 1)
                    nc.vector.tensor_copy(gatesT[:, :], misc_ps[0:E, 0:P]).then_inc(gatesT_ready, 1)
                    dve.wait_ge(start_in_psum, 1)
                    nc.vector.tensor_tensor(com.x[:, :], misc_ps[:, 256:512], acc[:, :], ALU.add).then_inc(x_ready, 1)
                else:
                    nc.vector.tensor_copy(com.x[:, :], acc[:, :]).then_inc(x_ready, 1)
                dve.wait_ge(x_ready, 1)


def l0_experts(nc, com, a):
    experts(nc, com, a, "l0f", 8, 2, a["L0_ffn_Wr"], [a["L0_ffn_Wg"], a["L0_ffn_Wu"]], a["L0_ffn_Wd"], 512, ACT.Silu,
            0, 512, eps=1e-20, shared=(512, [a["L0_ffn_Sg"], a["L0_ffn_Su"]], a["L0_ffn_Sd"], None, None, (0, 512)))


def l2_experts(nc, com, a):
    experts(nc, com, a, "l2f", 16, 4, a["L2_ffn_router_w"], [a["L2_ffn_w1"]], a["L2_ffn_w2"], 512, ACT.Gelu, 0,
            router_bias=a["L2_ffn_router_b"], up_bias=a["L2_ffn_b1"], down_bias=a["L2_ffn_b2"])


def l3_experts(nc, com, a):
    experts(nc, com, a, "l3f", 12, 2, a["L3_ffn_Wr"], [a["L3_ffn_We1"]], a["L3_ffn_We2"], 768, ACT.Gelu, 768, 0,
            U=2, T=3, tau=1.5, router_bias=a["L3_ffn_br"], up_bias=a["L3_ffn_be1"], down_bias=a["L3_ffn_be2"],
            shared=(512, [a["L3_ffn_Ws1"]], a["L3_ffn_Ws2"], a["L3_ffn_bs1"], a["L3_ffn_bs2"], (512, 0)))


def l1_experts(nc, com, a):
    E, OT = a["L1_ffn_We"].shape[0], a["L1_ffn_We"].shape[1] // P
    with phase(nc, "l1f") as ph:
        S = ph.sem
        w_nat = ph.sb("w_nat", [P, E, OT, D])
        wT = ph.sb("wT", [P, E, KT * D])
        wg, bg = ph.sb("wg", [P, KT, E]), ph.sb("bg", [P, E])
        be, gatesT = ph.sb("be", [E, D]), ph.sb("gatesT", [E, P])
        turned_ps = [ph.ps(f"turned{i}", [P, 512]) for i in range(2)]
        y_ps = [ph.ps(f"y{i}", [P, 512]) for i in range(2)]
        misc_ps = ph.ps("misc", [P, 512])
        small_loaded = S("small_loaded")
        w_loaded = [S(f"w_loaded{e}") for e in range(E)]
        logits_full, turned, wT_ready, y_full, acc_done = (
            S(s) for s in ("logits_full", "turned", "wT_ready", "y_full", "acc_done"))
        gatesT_in_psum, gatesT_ready, bias_full = (S(s) for s in ("gatesT_in_psum", "gatesT_ready", "bias_full"))
        gate_vector, gate_scalar, gates, gates_ready = gate_steps(nc, ph, com, E, 2)
        norm_vector, norm_scalar, norm_tensor = token_norm(
            nc, ph, com, misc_ps[:, 0:D].rearrange("p (k n) -> p k n", k=KT))
        with nc.Block() as block:
            @block.sync
            def _(sp):
                sp.dma_start(wg[:, :, :], a["L1_ffn_Wg"].rearrange("(k p) n -> p k n", p=P)).then_inc(small_loaded, 16)
                sp.dma_start(bg[:, :], a["L1_ffn_bg"].partition_broadcast(P)).then_inc(small_loaded, 16)
                sp.dma_start(be[:, :], a["L1_ffn_be"]).then_inc(small_loaded, 16)
                for e in range(E):
                    sp.dma_start(w_nat[:, e, :, :],
                                 a["L1_ffn_We"][e].rearrange("(t p) n -> p t n", p=P)).then_inc(w_loaded[e], 16)

            @block.tensor
            def _(pe):
                def turn_weights(e):
                    pe.wait_ge(w_loaded[e], 16)
                    if e >= 2:
                        pe.wait_ge(wT_ready, e - 1)
                    for k in range(KT):
                        for o in range(OT):
                            last = nc.tensor.transpose(turned_ps[e % 2][:, k * D + o * P:k * D + (o + 1) * P],
                                                       w_nat[:, e, o, k * P:(k + 1) * P], com.ident[:, :])
                    last.then_inc(turned, 1)
                turn_weights(0)
                norm_tensor(pe)
                pe.wait_ge(small_loaded, 48)
                for k in range(KT):
                    last = nc.tensor.matmul(misc_ps[:, D:D + E], com.xnT[:, k, :], wg[:, k, :],
                                            start=(k == 0), stop=(k == KT - 1))
                last.then_inc(logits_full, 1)
                for e in range(E):
                    if e + 1 < E:
                        turn_weights(e + 1)
                    pe.wait_ge(wT_ready, e + 1)
                    if e >= 2:
                        pe.wait_ge(acc_done, e - 1)
                    for k in range(KT):
                        last = nc.tensor.matmul(y_ps[e % 2][:, 0:D], com.xnT[:, k, :], wT[:, e, k * D:(k + 1) * D],
                                                start=(k == 0), stop=(k == KT - 1))
                    last.then_inc(y_full, 1)
                pe.wait_ge(gates_ready, 1)
                nc.tensor.transpose(misc_ps[0:E, 0:P], gates[:, :], com.ident[:, :]).then_inc(gatesT_in_psum, 1)
                pe.wait_ge(gatesT_ready, 1)
                nc.tensor.matmul(misc_ps[:, D:2 * D], gatesT[:, :], be[:, :], start=True, stop=True).then_inc(bias_full, 1)

            @block.scalar
            def _(act):
                norm_scalar(act)
                gate_scalar(act)
                for e in range(E):
                    act.wait_ge(turned, e + 1)
                    nc.scalar.copy(wT[:, e, :], turned_ps[e % 2][:, :]).then_inc(wT_ready, 1)

            @block.vector
            def _(dve):
                norm_vector(dve)
                dve.wait_ge(small_loaded, 48)
                dve.wait_ge(logits_full, 1)
                gate_vector(dve, misc_ps[:, D:D + E], bg[:, :])
                for e in range(E):
                    dve.wait_ge(y_full, e + 1)
                    if e:
                        dve.wait_ge(acc_done, e)
                    nc.vector.scalar_tensor_tensor(out=com.x[:, :], in0=y_ps[e % 2][:, 0:D], scalar=gates[:, e:e + 1],
                                                   in1=com.x[:, :], op0=ALU.mult, op1=ALU.add).then_inc(acc_done, 1)
                dve.wait_ge(gatesT_in_psum, 1)
                nc.vector.tensor_copy(gatesT[:, :], misc_ps[0:E, 0:P]).then_inc(gatesT_ready, 1)
                dve.wait_ge(bias_full, 1)
                dve.wait_ge(acc_done, E)
                nc.vector.tensor_tensor(com.x[:, :], misc_ps[:, D:2 * D], com.x[:, :], ALU.add).then_inc(acc_done, 1)
                dve.wait_ge(acc_done, E + 1)



class FewKeys:

    def __init__(self, nc, ph, com, keys, width, qm, kT, v, mask):
        self.nc, self.ph, self.com, self.keys, self.width = nc, ph, com, keys, width
        self.qm, self.kT, self.v, self.mask = qm, kT, v, mask
        self.per = 512 // keys
        self.rounds = HEADS // self.per
        self.tile_heads = P // width
        self.wide = width == 64
        S = ph.sem
        self.s_ps = [ph.ps(f"s{i}", [P, 512]) for i in range(2)]
        self.t_ps = [ph.ps(f"t{i}", [P, 512]) for i in range(2)]
        self.o_ps = [ph.ps(f"o{i}", [P, 512]) for i in range(2)]
        self.e = [ph.sb(f"e{i}", [P, 512]) for i in range(self.rounds)]
        self.pT = [ph.sb(f"pT{i}", [P, 512]) for i in range(2)]
        self.big, self.total = ph.sb("big", [P, HEADS]), ph.sb("total", [P, HEADS])
        self.attT = ph.sb("attT", [P, HEADS * width // P, P])
        if not self.wide:
            self.att = ph.sb("att", [P, HEADS * width])
        (self.scores_full, self.masked, self.max_step, self.exp_done, self.inverse_ready, self.probs_ready, self.turned,
         self.pT_ready, self.out_full, self.att_ready, self.att_turned, self.attT_ready) = (S(s) for s in (
             "scores_full", "masked", "max_step", "exp_done", "inverse_ready", "probs_ready", "turned", "pT_ready",
             "out_full", "att_ready", "att_turned", "attT_ready"))

    def on_tensor(self, pe):
        nc = self.nc

        def scores(r):
            if r >= 2:
                pe.wait_ge(self.masked, r - 1)
            for j in range(self.per):
                h = r * self.per + j
                last = nc.tensor.matmul(self.s_ps[r % 2][:, j * self.keys:(j + 1) * self.keys], self.qm[:, h, :],
                                        self.kT[:, h // self.tile_heads, :], start=True, stop=True)
            last.then_inc(self.scores_full, 1)

        def turn(r):
            pe.wait_ge(self.probs_ready, r + 1)
            if r >= 2:
                pe.wait_ge(self.pT_ready, r - 1)
            for b in range(4):
                last = nc.tensor.transpose(self.t_ps[r % 2][:, b * P:(b + 1) * P], self.e[r][:, b * P:(b + 1) * P],
                                           self.com.ident[:, :])
            last.then_inc(self.turned, 1)

        def weigh(r):
            pe.wait_ge(self.pT_ready, r + 1)
            kt = self.keys // P
            w = self.width
            for j in range(self.per):
                h = r * self.per + j
                for s in range(kt):
                    probs = self.pT[r % 2][:, (j * kt + s) * P:(j * kt + s + 1) * P]
                    values = self.v[:, s, h * w:(h + 1) * w]
                    if self.wide:
                        last = nc.tensor.matmul(self.o_ps[h // 8][h % 2 * w:(h % 2 + 1) * w, h // 2 % 4 * P:(h // 2 % 4 + 1) * P],
                                                values, probs, start=(s == 0), stop=(s == kt - 1))
                    else:
                        last = nc.tensor.matmul(self.o_ps[0][:, h * w:(h + 1) * w], probs, values,
                                                start=(s == 0), stop=(s == kt - 1))
            last.then_inc(self.out_full, 1)

        for r in range(self.rounds):
            scores(r)
        for r in range(self.rounds):
            turn(r)
            if r:
                weigh(r - 1)
        weigh(self.rounds - 1)
        if not self.wide:
            pe.wait_ge(self.att_ready, 1)
            for t in range(KT):
                last = nc.tensor.transpose(self.o_ps[1][:, t * P:(t + 1) * P], self.att[:, t * P:(t + 1) * P],
                                           self.com.ident[:, :])
            last.then_inc(self.att_turned, 1)
        pe.wait_ge(self.attT_ready, 2 if self.wide else 1)

    def on_vector(self, dve):
        nc, per, keys = self.nc, self.per, self.keys
        steps = 0

        def maximum(r):
            dve.wait_ge(self.scores_full, r + 1)
            cols = slice(r * per, (r + 1) * per)
            nc.vector.tensor_tensor(self.e[r][:, :].rearrange("p (h s) -> p h s", h=per),
                                    self.s_ps[r % 2][:, :].rearrange("p (h s) -> p h s", h=per),
                                    self.mask[:, :].unsqueeze(1).to_broadcast([P, per, keys]),
                                    ALU.min).then_inc(self.masked, 1)
            dve.wait_ge(self.masked, r + 1)
            nc.vector.reduce_max(self.big[:, cols], self.e[r][:, :].rearrange("p (h s) -> p h s", h=per),
                                 AX).then_inc(self.max_step, 1)
            dve.wait_ge(self.max_step, 2 * r + 1)
            nc.vector.tensor_scalar(self.big[:, cols], self.big[:, cols], -1.0, None, ALU.mult).then_inc(self.max_step, 1)

        def normalise(r):
            cols = slice(r * per, (r + 1) * per)
            dve.wait_ge(self.exp_done, r + 1)
            nc.vector.reciprocal(self.total[:, cols], self.total[:, cols]).then_inc(self.inverse_ready, 1)
            dve.wait_ge(self.inverse_ready, r + 1)
            e = self.e[r][:, :].rearrange("p (h s) -> p h s", h=per)
            nc.vector.tensor_tensor(e, e, self.total[:, cols].unsqueeze(2).to_broadcast([P, per, keys]),
                                    ALU.mult).then_inc(self.probs_ready, 1)

        for r in range(self.rounds):
            maximum(r)
        for r in range(self.rounds):
            normalise(r)
        if self.wide:
            for i in range(2):
                dve.wait_ge(self.out_full, self.rounds // 2 * (i + 1))
                nc.vector.tensor_copy(self.attT[:, i * 4:(i + 1) * 4, :].rearrange("p t n -> p (t n)"),
                                      self.o_ps[i][:, :]).then_inc(self.attT_ready, 1)
        else:
            dve.wait_ge(self.out_full, self.rounds)
            nc.vector.tensor_copy(self.att[:, :], self.o_ps[0][:, 0:HEADS * self.width]).then_inc(self.att_ready, 1)
            dve.wait_ge(self.att_turned, 1)
            nc.vector.tensor_copy(self.attT[:, :, :].rearrange("p t n -> p (t n)"),
                                  self.o_ps[1][:, 0:D]).then_inc(self.attT_ready, 1)

    def on_scalar(self, act):
        nc, per, keys = self.nc, self.per, self.keys

        def exponents(r):
            act.wait_ge(self.max_step, 2 * r + 2)
            for j in range(per):
                h = r * per + j
                last = nc.scalar.activation(self.e[r][:, j * keys:(j + 1) * keys], self.e[r][:, j * keys:(j + 1) * keys],
                                            ACT.Exp, bias=self.big[:, h:h + 1], scale=1.0,
                                            accum_out=self.total[:, h:h + 1])
            last.then_inc(self.exp_done, 1)

        def copy(r):
            act.wait_ge(self.turned, r + 1)
            if r >= 2:
                act.wait_ge(self.out_full, r - 1)
            nc.scalar.copy(self.pT[r % 2][:, :], self.t_ps[r % 2][:, :]).then_inc(self.pT_ready, 1)

        exponents(0)
        exponents(1)
        for r in range(self.rounds):
            if r + 2 < self.rounds:
                exponents(r + 2)
            copy(r)


def make_head_rows(nc, pool, rows, n, width, done):
    nc.gpsimd.memset(rows[:, :], 1.0).then_inc(done, 1)
    pool.wait_ge(done, 1)
    nc.gpsimd.affine_select(out=rows[:, :], in_=rows[:, :], compare_op=ALU.is_ge, fill=0.0, base=0,
                            pattern=[[-width, n]], channel_multiplier=1).then_inc(done, 1)
    pool.wait_ge(done, 2)
    nc.gpsimd.affine_select(out=rows[:, :], in_=rows[:, :], compare_op=ALU.is_ge, fill=0.0, base=width - 1,
                            pattern=[[width, n]], channel_multiplier=-1).then_inc(done, 1)


def l3_attention(nc, com, a):
    W, window, fill, n = 16, 64, -1.0e30, P // 16
    with phase(nc, "l3a") as ph:
        S = ph.sem
        w = {m: ph.sb("w" + m, [P, KT, D]) for m in "qkvo"}
        bq, bk = ph.sb("bq", [P, KT]), ph.sb("bk", [P, KT])
        bv, bo = ph.sb("bv", [P, D]), ph.sb("bo", [P, D])
        rows, mask = ph.sb("rows", [P, n]), ph.sb("mask", [P, P])
        qT, kT = ph.sb("qT", [P, KT, P]), ph.sb("kT", [P, KT, P])
        qm, v = ph.sb("qm", [P, HEADS, P]), ph.sb("v", [P, 1, D])
        fk = FewKeys(nc, ph, com, P, W, qm, kT, v, mask)
        front_ps = [ph.ps(f"front{i}", [P, 512]) for i in range(2)]
        norm_vector, norm_scalar, norm_tensor = token_norm(
            nc, ph, com, front_ps[0][:, 0:D].rearrange("p (k n) -> p k n", k=KT))
        loaded, rows_made, mask_made, front_full, front_step, ready, y_full, x_step = (
            S(s) for s in ("loaded", "rows_made", "mask_made", "front_full", "front_step", "ready", "y_full", "x_step"))
        with nc.Block() as block:
            @block.sync
            def _(sp):
                for m in "qkvo":
                    sp.dma_start(w[m][:, :, :], a["L3_attn_W" + m].rearrange("(k p) n -> p k n", p=P)).then_inc(loaded, 16)
                for t, src in ((bq, a["L3_attn_bq"]), (bk, a["L3_attn_bk"])):
                    sp.dma_start(t[:, :], src.rearrange("(k p) -> p k", p=P),
                                 allow_slow_non_contiguous=True).then_inc(loaded, 16)
                for t, src in ((bv, a["L3_attn_bv"]), (bo, a["L3_attn_bo"])):
                    sp.dma_start(t[:, :], src.partition_broadcast(P)).then_inc(loaded, 16)

            @block.gpsimd
            def _(pool):
                make_head_rows(nc, pool, rows, n, W, rows_made)
                nc.gpsimd.memset(mask[:, :], -FILL).then_inc(mask_made, 1)
                pool.wait_ge(mask_made, 1)
                nc.gpsimd.affine_select(out=mask[:, :], in_=mask[:, :], compare_op=ALU.is_ge, fill=fill, base=0,
                                        pattern=[[-1, P]], channel_multiplier=1).then_inc(mask_made, 1)
                pool.wait_ge(mask_made, 2)
                nc.gpsimd.affine_select(out=mask[:, :], in_=mask[:, :], compare_op=ALU.is_ge, fill=fill,
                                        base=window - 1, pattern=[[1, P]], channel_multiplier=-1).then_inc(mask_made, 1)

            @block.tensor
            def _(pe):
                norm_tensor(pe)
                pe.wait_ge(loaded, 16 * 8)
                for m, at in (("q", 0), ("k", D)):
                    for t in range(KT):
                        for k in range(KT):
                            last = nc.tensor.matmul(front_ps[1][:, at + t * P:at + (t + 1) * P],
                                                    w[m][:, k, t * P:(t + 1) * P], com.xnT[:, k, :],
                                                    start=(k == 0), stop=(k == KT - 1))
                    last.then_inc(front_full, 1)
                for k in range(KT):
                    last = nc.tensor.matmul(front_ps[0][:, D:2 * D], com.xnT[:, k, :], w["v"][:, k, :],
                                            start=(k == 0), stop=(k == KT - 1))
                last.then_inc(front_full, 1)
                pe.wait_ge(ready, 1 + KT + KT)
                fk.on_tensor(pe)
                for k in range(KT):
                    last = nc.tensor.matmul(front_ps[0][:, 0:D], fk.attT[:, k, :], w["o"][:, k, :],
                                            start=(k == 0), stop=(k == KT - 1))
                last.then_inc(y_full, 1)

            @block.vector
            def _(dve):
                norm_vector(dve)
                dve.wait_ge(loaded, 16 * 8)
                dve.wait_ge(front_full, 2)
                for t in range(KT):
                    nc.vector.tensor_scalar(qT[:, t, :], front_ps[1][:, t * P:(t + 1) * P], bq[:, t:t + 1], 0.25,
                                            ALU.add, ALU.mult).then_inc(front_step, 1)
                dve.wait_ge(front_step, KT)
                dve.wait_ge(rows_made, 3)
                for t in range(KT):
                    nc.vector.tensor_tensor(qm[:, t * n:(t + 1) * n, :], qT[:, t, :].unsqueeze(1).to_broadcast([P, n, P]),
                                            rows[:, :].unsqueeze(2).to_broadcast([P, n, P]), ALU.mult).then_inc(ready, 1)
                for t in range(KT):
                    nc.vector.tensor_scalar(kT[:, t, :], front_ps[1][:, D + t * P:D + (t + 1) * P], bk[:, t:t + 1], None,
                                            ALU.add).then_inc(ready, 1)
                dve.wait_ge(front_full, 3)
                nc.vector.tensor_tensor(v[:, 0, :], front_ps[0][:, D:2 * D], bv[:, :], ALU.add).then_inc(ready, 1)
                nc.vector.tensor_tensor(com.x[:, :], com.x[:, :], bo[:, :], ALU.add).then_inc(x_step, 1)
                dve.wait_ge(mask_made, 3)
                fk.on_vector(dve)
                dve.wait_ge(y_full, 1)
                dve.wait_ge(x_step, 1)
                nc.vector.tensor_tensor(com.x[:, :], front_ps[0][:, 0:D], com.x[:, :], ALU.add).then_inc(x_step, 1)
                dve.wait_ge(x_step, 2)

            @block.scalar
            def _(act):
                norm_scalar(act)
                fk.on_scalar(act)


def l2_attention(nc, com, a):
    W, LD = 64, a["L2_attn_Wkv_down"].shape[1]
    AW = HEADS * W
    NT = AW // P
    with phase(nc, "l2a") as ph:
        S = ph.sem
        wq, wd = ph.sb("wq", [P, KT, AW]), ph.sb("wd", [P, KT, LD])
        wk, wv = ph.sb("wk", [LD, AW]), ph.sb("wv", [LD, AW])
        wo = ph.sb("wo", [P, NT, D])
        rows, mask = ph.sb("rows", [P, 2]), ph.sb("mask", [P, P])
        latT = ph.sb("latT", [LD, P])
        kT = ph.sb("kT", [P, NT, P])
        qm, v = ph.sb("qm", [P, HEADS, P]), ph.sb("v", [P, 1, AW])
        fk = FewKeys(nc, ph, com, P, W, qm, kT, v, mask)
        front_ps = [ph.ps(f"front{i}", [P, 512]) for i in range(2)]
        norm_vector, norm_scalar, norm_tensor = token_norm(
            nc, ph, com, front_ps[0][:, 0:D].rearrange("p (k n) -> p k n", k=KT))
        loaded, wo_loaded, rows_made, mask_made, latent_full, latT_ready, q_full, k_full, v_full = (
            S(s) for s in ("loaded", "wo_loaded", "rows_made", "mask_made", "latent_full", "latT_ready", "q_full",
                           "k_full", "v_full"))
        qm_ready, kT_ready, v_ready, y_full, x_ready = (
            S(s) for s in ("qm_ready", "kT_ready", "v_ready", "y_full", "x_ready"))
        q_ps, k_ps, v_ps = fk.s_ps, fk.o_ps, fk.t_ps
        with nc.Block() as block:
            @block.sync
            def _(sp):
                sp.dma_start(wd[:, :, :], a["L2_attn_Wkv_down"].rearrange("(k p) n -> p k n", p=P)).then_inc(loaded, 16)
                for t, name in ((wk, "L2_attn_Wk_up"), (wv, "L2_attn_Wv_up")):
                    sp.dma_start(t[:, :], a[name].rearrange("c h e -> c (h e)")).then_inc(loaded, 16)
                sp.dma_start(wq[:, :, :], a["L2_attn_Wq"].rearrange("(k p) h e -> p k (h e)", p=P)).then_inc(loaded, 16)
                sp.dma_start(wo[:, :, :], a["L2_attn_Wout"].rearrange("h e n -> (h e) n")
                             .rearrange("(k p) n -> p k n", p=P)).then_inc(wo_loaded, 16)

            @block.gpsimd
            def _(pool):
                make_head_rows(nc, pool, rows, 2, W, rows_made)
                nc.gpsimd.memset(mask[:, :], -FILL).then_inc(mask_made, 1)
                pool.wait_ge(mask_made, 1)
                nc.gpsimd.affine_select(out=mask[:, :], in_=mask[:, :], compare_op=ALU.is_ge,
                                        fill=float(np.finfo(np.float32).min), base=0, pattern=[[-1, P]],
                                        channel_multiplier=1).then_inc(mask_made, 1)

            @block.tensor
            def _(pe):
                norm_tensor(pe)
                pe.wait_ge(loaded, 16 * 4)
                for k in range(KT):
                    last = nc.tensor.matmul(front_ps[1][0:LD, 0:P], wd[:, k, :], com.xnT[:, k, :],
                                            start=(k == 0), stop=(k == KT - 1))
                last.then_inc(latent_full, 1)
                for t in range(NT):
                    for k in range(KT):
                        last = nc.tensor.matmul(q_ps[t // 4][:, t % 4 * P:(t % 4 + 1) * P], wq[:, k, t * P:(t + 1) * P],
                                                com.xnT[:, k, :], start=(k == 0), stop=(k == KT - 1))
                    if t % 4 == 3:
                        last.then_inc(q_full, 1)
                pe.wait_ge(latT_ready, 1)
                for t in range(NT):
                    last = nc.tensor.matmul(k_ps[t // 4][:, t % 4 * P:(t % 4 + 1) * P], wk[:, t * P:(t + 1) * P],
                                            latT[:, :], start=True, stop=True)
                last.then_inc(k_full, 1)
                for i in range(2):
                    last = nc.tensor.matmul(v_ps[i][:, :], latT[:, :], wv[:, i * 512:(i + 1) * 512], start=True, stop=True)
                last.then_inc(v_full, 1)
                pe.wait_ge(qm_ready, 2 * 2)
                pe.wait_ge(kT_ready, 2)
                pe.wait_ge(v_ready, 2)
                fk.on_tensor(pe)
                pe.wait_ge(wo_loaded, 16)
                for k in range(NT):
                    last = nc.tensor.matmul(front_ps[0][:, 0:D], fk.attT[:, k, :], wo[:, k, :],
                                            start=(k == 0), stop=(k == NT - 1))
                last.then_inc(y_full, 1)

            @block.vector
            def _(dve):
                norm_vector(dve)
                dve.wait_ge(latent_full, 1)
                nc.vector.tensor_copy(latT[:, :], front_ps[1][0:LD, 0:P]).then_inc(latT_ready, 1)
                dve.wait_ge(rows_made, 3)
                for i in range(2):
                    dve.wait_ge(q_full, i + 1)
                    for j in range(2):
                        nc.vector.tensor_scalar(qm[:, i * 8:(i + 1) * 8, :].rearrange("p (t two) n -> p two t n", two=2)[:, j],
                                                q_ps[i][:, :].rearrange("p (t n) -> p t n", n=P), rows[:, j:j + 1], 0.125,
                                                ALU.mult, ALU.mult).then_inc(qm_ready, 1)
                dve.wait_ge(mask_made, 2)
                fk.on_vector(dve)
                dve.wait_ge(y_full, 1)
                nc.vector.tensor_tensor(com.x[:, :], front_ps[0][:, 0:D], com.x[:, :], ALU.add).then_inc(x_ready, 1)
                dve.wait_ge(x_ready, 1)

            @block.scalar
            def _(act):
                norm_scalar(act)
                act.wait_ge(k_full, 1)
                for i in range(2):
                    nc.scalar.copy(kT[:, i * 4:(i + 1) * 4, :].rearrange("p t n -> p (t n)"), k_ps[i][:, :]).then_inc(kT_ready, 1)
                act.wait_ge(v_full, 1)
                for i in range(2):
                    nc.scalar.copy(v[:, 0, i * 512:(i + 1) * 512], v_ps[i][:, :]).then_inc(v_ready, 1)
                fk.on_scalar(act)


def l1_state_space(nc, com, a):
    RING = 4
    with phase(nc, "l1a") as ph:
        S = ph.sem
        nat = {m: ph.sb("nat_" + m, [P, KT, D]) for m in ("in", "out")}
        wT = {m: ph.sb("T_" + m, [P, KT, D]) for m in ("in", "out")}
        b_in, skip = (ph.sb(m, [P, KT]) for m in ("b_in", "skip"))
        b_out = ph.sb("b_out", [P, D])
        uT, yT = ph.sb("uT", [P, KT, P]), ph.sb("yT", [P, KT, P])
        products = ph.sb("products", [P, RING, KT, P])
        turned_ps = [ph.ps(f"turned{i}", [P, 512]) for i in range(2)]
        u_ps, y_ps, misc_ps = ph.ps("u", [P, 512]), ph.ps("y", [P, 512]), ph.ps("misc", [P, 512])
        norm_vector, norm_scalar, norm_tensor = token_norm(
            nc, ph, com, misc_ps[:, 0:D].rearrange("p (k n) -> p k n", k=KT))
        loaded, turned, wT_ready, u_full, u_ready = (
            S(s) for s in ("loaded", "turned", "wT_ready", "u_full", "u_ready"))
        conv_done, y_ready, out_full, x_step = (S(s) for s in ("conv_done", "y_ready", "out_full", "x_step"))
        with nc.Block() as block:
            @block.sync
            def _(sp):
                for t, name in ((b_in, "bin_"), (skip, "Dp")):
                    sp.dma_start(t[:, :], a["L1_attn_" + name].rearrange("(k p) -> p k", p=P),
                                 allow_slow_non_contiguous=True).then_inc(loaded, 16)
                for m in ("in", "out"):
                    sp.dma_start(nat[m][:, :, :], a["L1_attn_W" + m].rearrange("(k p) n -> p k n", p=P)).then_inc(loaded, 16)
                sp.dma_start(b_out[:, :], a["L1_attn_bout"].partition_broadcast(P)).then_inc(loaded, 16)

            @block.tensor
            def _(pe):
                pe.wait_ge(loaded, 80)
                for i, m in enumerate(("in", "out")):
                    for k in range(KT):
                        for o in range(KT):
                            last = nc.tensor.transpose(turned_ps[i][:, k * D + o * P:k * D + (o + 1) * P],
                                                       nat[m][:, o, k * P:(k + 1) * P], com.ident[:, :])
                    last.then_inc(turned, 1)
                norm_tensor(pe)
                pe.wait_ge(wT_ready, 1)
                for t in range(KT):
                    for k in range(KT):
                        last = nc.tensor.matmul(u_ps[:, t * P:(t + 1) * P], wT["in"][:, k, t * P:(t + 1) * P],
                                                com.xnT[:, k, :], start=(k == 0), stop=(k == KT - 1))
                last.then_inc(u_full, 1)
                pe.wait_ge(wT_ready, 2)
                pe.wait_ge(y_ready, KT)
                for k in range(KT):
                    last = nc.tensor.matmul(y_ps[:, 0:D], yT[:, k, :], wT["out"][:, k, :],
                                            start=(k == 0), stop=(k == KT - 1))
                last.then_inc(out_full, 1)

            @block.scalar
            def _(act):
                norm_scalar(act)
                for i, m in enumerate(("in", "out")):
                    act.wait_ge(turned, i + 1)
                    nc.scalar.copy(wT[m][:, :, :].rearrange("p k n -> p (k n)"), turned_ps[i][:, :]).then_inc(wT_ready, 1)

            @block.vector
            def _(dve):
                norm_vector(dve)
                dve.wait_ge(loaded, 80)
                dve.wait_ge(u_full, 1)
                for t in range(KT):
                    nc.vector.tensor_scalar(uT[:, t, :], u_ps[:, t * P:(t + 1) * P], b_in[:, t:t + 1], None,
                                            ALU.add).then_inc(u_ready, 1)
                nc.vector.tensor_tensor(com.x[:, :], com.x[:, :], b_out[:, :], ALU.add).then_inc(x_step, 1)
                dve.wait_ge(u_ready, KT)
                for l in range(P):
                    for t in range(KT):
                        if l >= RING:
                            dve.wait_ge(conv_done, (l - RING) * KT + t + 1)
                        nc.vector.tensor_tensor_reduce(out=products[:, l % RING, t, 0:l + 1],
                                                       in0=com.k_rev[:, t, P - 1 - l:P], in1=uT[:, t, 0:l + 1],
                                                       op0=ALU.mult, op1=ALU.add, scale=1.0, scalar=0.0,
                                                       accum_out=yT[:, t, l:l + 1]).then_inc(conv_done, 1)
                dve.wait_ge(conv_done, P * KT)
                for t in range(KT):
                    nc.vector.scalar_tensor_tensor(out=yT[:, t, :], in0=uT[:, t, :], scalar=skip[:, t:t + 1],
                                                   in1=yT[:, t, :], op0=ALU.mult, op1=ALU.add).then_inc(y_ready, 1)
                dve.wait_ge(out_full, 1)
                dve.wait_ge(x_step, 1)
                nc.vector.tensor_tensor(com.x[:, :], y_ps[:, 0:D], com.x[:, :], ALU.add).then_inc(x_step, 1)
                dve.wait_ge(x_step, 2)


def l0_attention(nc, com, a):
    W = 64
    VW = W + 1
    AW = HEADS * W
    NT, ST = AW // P, a["L0_attn_source_embedding"].shape[0] // P
    TILES = ST + 1
    Q = ST
    with phase(nc, "l0a") as ph:
        S = ph.sem
        emb = {m: ph.sb("emb_" + m, [P, ST, D]) for m in "kv"}
        embT = {m: ph.sb("embT_" + m, [P, KT, ST * P]) for m in "kv"}
        w = {m: ph.sb("w" + m, [P, KT, AW]) for m in "kqv"}
        wo = ph.sb("wo", [P, NT, D])
        bias = {m: ph.sb("b" + m, [P, AW]) for m in "kqv"}
        bo, ln_g, ln_b = (ph.sb(m, [P, D]) for m in ("bo", "ln_g", "ln_b"))
        rows = ph.sb("rows", [P, 2])
        feature, low = ph.sb("feature", [P, TILES, AW]), [ph.sb(f"low{i}", [P, AW]) for i in range(2)]
        inverse = ph.sb("inverse", [P, TILES, HEADS])
        kT, v = ph.sb("kT", [P, NT, ST * P]), ph.sb("v", [P, ST, HEADS * VW])
        qm = ph.sb("qm", [P, HEADS, P])
        res, stats, mv, rstd = ph.sb("res", [P, D]), ph.sb("stats2", [P, 6]), ph.sb("mv2", [P, 2]), ph.sb("rstd2", [P, 1])
        over, att = ph.sb("over", [P, NT, 2, 1]), ph.sb("att", [P, AW])
        probs = [feature[:, i, :] for i in range(4)]
        attT = feature[:, 4, :].rearrange("p (t n) -> p t n", n=P)
        pair = [ph.ps(f"pair{i}", [P, 1024]) for i in range(4)]
        halves = [[pair[i][:, 0:512], pair[i][:, 512:1024]] for i in range(4)]
        product_ps, turned_ps = halves[0:2], halves[2:4]
        value_ps = halves[2] + halves[3]
        scores_ps = pair[0:2]
        out_ps, y_ps = [halves[2][0], halves[3][0]], halves[3][1]
        norm_vector, norm_scalar, norm_tensor = token_norm(
            nc, ph, com, halves[1][0][:, 0:D].rearrange("p (k n) -> p k n", k=KT))
        emb_loaded = {m: S(f"emb_{m}_loaded") for m in "kv"}
        w_loaded = {m: S(f"w{m}_loaded") for m in "kqv"}
        small_loaded, rows_made, emb_turned, embT_ready, value_full, v_ready = (
            S(s) for s in ("small_loaded", "rows_made", "emb_turned", "embT_ready", "value_full", "v_ready"))
        product_full, z_ready, low_ready, exp_low, high_ready, feature_ready, square_ready, squares_summed = (
            S(s) for s in ("product_full", "z_ready", "low_ready", "exp_low", "high_ready", "feature_ready",
                           "square_ready", "squares_summed"))
        root_taken, inverse_step, unit_ready, unit_turned, unitT_ready, y_full, out_step, out_root = (
            S(s) for s in ("root_taken", "inverse_step", "unit_ready", "unit_turned", "unitT_ready", "y_full",
                           "out_step", "out_root"))
        ones_set, scores_full, exp_done, out_full, over_ready, out_taken, att_turned, attT_ready = (
            S(s) for s in ("ones_set", "scores_full", "exp_done", "out_full", "over_ready", "out_taken", "att_turned",
                           "attT_ready"))

        with nc.Block() as block:
            @block.sync
            def _(sp):
                for m, name in (("k", "source"), ("v", "value")):
                    sp.dma_start(emb[m][:, :, :], a[f"L0_attn_{name}_embedding"]
                                 .rearrange("(t p) n -> p t n", p=P)).then_inc(emb_loaded[m], 16)
                    sp.dma_start(w[m][:, :, :], a["L0_attn_W" + m].rearrange("(k p) n -> p k n", p=P)).then_inc(w_loaded[m], 16)
                    sp.dma_start(bias[m][:, :], a["L0_attn_b" + m].partition_broadcast(P)).then_inc(w_loaded[m], 16)
                sp.dma_start(w["q"][:, :, :], a["L0_attn_Wq"].rearrange("(k p) n -> p k n", p=P)).then_inc(w_loaded["q"], 16)
                sp.dma_start(bias["q"][:, :], a["L0_attn_bq"].partition_broadcast(P)).then_inc(w_loaded["q"], 16)
                for t, name in ((bo, "bo"), (ln_g, "ln_g"), (ln_b, "ln_b")):
                    sp.dma_start(t[:, :], a["L0_attn_" + name].partition_broadcast(P)).then_inc(small_loaded, 16)
                sp.dma_start(wo[:, :, :], a["L0_attn_Wo"].rearrange("(k p) n -> p k n", p=P)).then_inc(small_loaded, 16)

            @block.tensor
            def _(pe):
                for i, m in enumerate("kv"):
                    pe.wait_ge(emb_loaded[m], 16)
                    for k in range(KT):
                        for t in range(ST):
                            last = nc.tensor.transpose(turned_ps[i][k][:, t * P:(t + 1) * P],
                                                       emb[m][:, t, k * P:(k + 1) * P], com.ident[:, :])
                        last.then_inc(emb_turned, 1)
                norm_tensor(pe)
                for i in range(TILES):
                    m = "q" if i == Q else "k"
                    pe.wait_ge(w_loaded[m], 32)
                    if i == 0:
                        pe.wait_ge(embT_ready, KT)
                    if i >= 2:
                        pe.wait_ge(z_ready, 2 * (i - 1))
                    for half in range(2):
                        for k in range(KT):
                            lhs = com.xnT[:, k, :] if i == Q else embT["k"][:, k, i * P:(i + 1) * P]
                            last = nc.tensor.matmul(product_ps[i % 2][half][:, :], lhs,
                                                    w[m][:, k, half * 512:(half + 1) * 512],
                                                    start=(k == 0), stop=(k == KT - 1))
                        last.then_inc(product_full, 1)
                pe.wait_ge(w_loaded["v"], 32)
                pe.wait_ge(embT_ready, 2 * KT)
                for j in range(2 * ST):
                    if j >= 4:
                        pe.wait_ge(v_ready, j - 3)
                    t, half = j // 2, j % 2
                    for k in range(KT):
                        last = nc.tensor.matmul(value_ps[j % 4][:, :], embT["v"][:, k, t * P:(t + 1) * P],
                                                w["v"][:, k, half * 512:(half + 1) * 512],
                                                start=(k == 0), stop=(k == KT - 1))
                    last.then_inc(value_full, 1)
                pe.wait_ge(v_ready, 2 * ST)
                for i in range(TILES):
                    pe.wait_ge(unit_ready, i + 1)
                    if i >= 2:
                        pe.wait_ge(unitT_ready, 2 * (i - 1))
                    for t in range(NT):
                        last = nc.tensor.transpose(turned_ps[i % 2][t // 4][:, t % 4 * P:(t % 4 + 1) * P],
                                                   feature[:, i, t * P:(t + 1) * P], com.ident[:, :])
                        if t % 4 == 3:
                            last.then_inc(unit_turned, 1)
                pe.wait_ge(unitT_ready, 2 * ST + 4)
                pe.wait_ge(ones_set, 1)

                def scores(r):
                    if r >= 2:
                        pe.wait_ge(exp_done, r - 1)
                    for s in range(ST):
                        last = nc.tensor.matmul(scores_ps[r % 2][:, s * 2 * P:(s + 1) * 2 * P], kT[:, r, s * P:(s + 1) * P],
                                                qm[:, 2 * r:2 * r + 2, :].rearrange("p h n -> p (h n)"),
                                                start=True, stop=True)
                    last.then_inc(scores_full, 1)

                def weigh(r):
                    pe.wait_ge(exp_done, r + 1)
                    if r >= 2:
                        pe.wait_ge(out_taken, r - 1)
                    for j in range(2):
                        h = 2 * r + j
                        for s in range(ST):
                            last = nc.tensor.matmul(out_ps[r % 2][:, j * VW:(j + 1) * VW],
                                                    probs[r % 4][:, (2 * s + j) * P:(2 * s + j + 1) * P],
                                                    v[:, s, h * VW:(h + 1) * VW], start=(s == 0), stop=(s == ST - 1))
                    last.then_inc(out_full, 1)
                scores(0)
                scores(1)
                for r in range(NT):
                    if r + 2 < NT:
                        scores(r + 2)
                    weigh(r)
                pe.wait_ge(out_taken, NT)
                for t in range(NT):
                    last = nc.tensor.transpose(pair[0][:, t * P:(t + 1) * P], att[:, t * P:(t + 1) * P], com.ident[:, :])
                last.then_inc(att_turned, 1)
                pe.wait_ge(attT_ready, 1)
                pe.wait_ge(small_loaded, 64)
                for k in range(NT):
                    last = nc.tensor.matmul(y_ps[:, 0:D], attT[:, k, :], wo[:, k, :],
                                            start=(k == 0), stop=(k == NT - 1))
                last.then_inc(y_full, 1)

            @block.gpsimd
            def _(pool):
                make_head_rows(nc, pool, rows, 2, W, rows_made)
                nc.gpsimd.memset(v[:, :, :].rearrange("p s (h e) -> p s h e", e=VW)[:, :, :, W:VW], 1.0).then_inc(ones_set, 1)

            @block.scalar
            def _(act):
                norm_scalar(act)
                for i, m in enumerate("kv"):
                    for k in range(KT):
                        act.wait_ge(emb_turned, i * KT + k + 1)
                        nc.scalar.copy(embT[m][:, k, :], turned_ps[i][k][:, :]).then_inc(embT_ready, 1)
                for i in range(TILES):
                    act.wait_ge(low_ready, i + 1)
                    nc.scalar.activation(low[i % 2][:, :], low[i % 2][:, :], ACT.Exp).then_inc(exp_low, 1)
                    act.wait_ge(feature_ready, i + 1)
                    nc.scalar.activation(low[i % 2][:, :], feature[:, i, :], ACT.Square).then_inc(square_ready, 1)
                act.wait_ge(squares_summed, TILES)
                nc.scalar.activation(inverse[:, :, :], inverse[:, :, :], ACT.Sqrt).then_inc(root_taken, 1)
                for i in range(ST):
                    for half in range(2):
                        act.wait_ge(unit_turned, 2 * i + half + 1)
                        nc.scalar.copy(kT[:, half * 4:(half + 1) * 4, i * P:(i + 1) * P],
                                       turned_ps[i % 2][half][:, :].rearrange("p (t n) -> p t n", n=P)
                                       ).then_inc(unitT_ready, 1)
                for r in range(NT):
                    act.wait_ge(scores_full, r + 1)
                    if r >= 4:
                        act.wait_ge(out_full, r - 3)
                    nc.scalar.activation(probs[r % 4], scores_ps[r % 2][:, :], ACT.Exp).then_inc(exp_done, 1)
                act.wait_ge(out_step, 5)
                nc.scalar.activation(rstd[:, :], rstd[:, :], ACT.Sqrt).then_inc(out_root, 1)

            @block.vector
            def _(dve):
                def shift(i):
                    m = "q" if i == Q else "k"
                    dve.wait_ge(w_loaded[m], 32)
                    for half in range(2):
                        c = slice(half * 512, (half + 1) * 512)
                        dve.wait_ge(product_full, 2 * i + half + 1)
                        nc.vector.tensor_tensor(feature[:, i, c], product_ps[i % 2][half][:, :], bias[m][:, c],
                                                ALU.add).then_inc(z_ready, 1)
                    dve.wait_ge(z_ready, 2 * (i + 1))
                    if i >= 2:
                        dve.wait_ge(squares_summed, i - 1)
                    nc.vector.tensor_scalar(low[i % 2][:, :], feature[:, i, :], 0.0, None, ALU.min).then_inc(low_ready, 1)

                def elu(i):
                    dve.wait_ge(low_ready, i + 1)
                    nc.vector.tensor_scalar(feature[:, i, :], feature[:, i, :], 0.0, -1.0, ALU.max, ALU.add).then_inc(high_ready, 1)
                    dve.wait_ge(high_ready, i + 1)
                    dve.wait_ge(exp_low, i + 1)
                    nc.vector.tensor_tensor(feature[:, i, :], feature[:, i, :], low[i % 2][:, :], ALU.add).then_inc(feature_ready, 1)

                def sum_squares(i):
                    dve.wait_ge(square_ready, i + 1)
                    nc.vector.reduce_sum(inverse[:, i, :], low[i % 2][:, :].rearrange("p (h e) -> p h e", e=W),
                                         AX).then_inc(squares_summed, 1)
                norm_vector(dve)
                for i in range(TILES):
                    if i >= 2:
                        sum_squares(i - 2)
                    shift(i)
                    if i:
                        elu(i - 1)
                elu(TILES - 1)
                sum_squares(TILES - 2)
                sum_squares(TILES - 1)
                dve.wait_ge(root_taken, 1)
                nc.vector.reciprocal(inverse[:, :, :], inverse[:, :, :]).then_inc(inverse_step, 1)
                dve.wait_ge(inverse_step, 1)
                nc.vector.tensor_scalar(inverse[:, Q, :], inverse[:, Q, :], 0.125, None, ALU.mult).then_inc(inverse_step, 1)
                dve.wait_ge(w_loaded["v"], 32)
                for j in range(2 * ST):
                    t, c = j // 2, slice(j % 2 * 512, (j % 2 + 1) * 512)
                    dve.wait_ge(value_full, j + 1)
                    out = v[:, t, :].rearrange("p (h e) -> p h e", e=VW)[:, j % 2 * 8:(j % 2 + 1) * 8, 0:W]
                    nc.vector.tensor_tensor(out, value_ps[j % 4].rearrange("p (h e) -> p h e", e=W),
                                            bias["v"][:, c].rearrange("p (h e) -> p h e", e=W), ALU.add).then_inc(v_ready, 1)
                dve.wait_ge(inverse_step, 2)
                for i in range(TILES):
                    f = feature[:, i, :].rearrange("p (h e) -> p h e", e=W)
                    nc.vector.tensor_tensor(f, f, inverse[:, i, :].unsqueeze(2).to_broadcast([P, HEADS, W]),
                                            ALU.mult).then_inc(unit_ready, 1)
                dve.wait_ge(rows_made, 3)
                for half in range(2):
                    dve.wait_ge(unit_turned, 2 * Q + half + 1)
                    for j in range(2):
                        nc.vector.tensor_scalar(qm[:, half * 8:(half + 1) * 8, :].rearrange("p (t two) n -> p two t n", two=2)[:, j],
                                                turned_ps[Q % 2][half][:, :].rearrange("p (t n) -> p t n", n=P),
                                                rows[:, j:j + 1], None, ALU.mult).then_inc(unitT_ready, 1)
                dve.wait_ge(small_loaded, 64)
                nc.vector.tensor_tensor(res[:, :], com.xn[:, :], bo[:, :], ALU.add).then_inc(out_step, 1)
                for r in range(NT):
                    dve.wait_ge(out_full, r + 1)
                    o = out_ps[r % 2][:, 0:2 * VW].rearrange("p (h e) -> p h e", e=VW)
                    nc.vector.reciprocal(over[:, r, :, :], o[:, :, W:VW]).then_inc(over_ready, 1)
                    dve.wait_ge(over_ready, r + 1)
                    nc.vector.tensor_tensor(att[:, r * P:(r + 1) * P].rearrange("p (h e) -> p h e", e=W), o[:, :, 0:W],
                                            over[:, r, :, :].to_broadcast([P, 2, W]), ALU.mult).then_inc(out_taken, 1)
                dve.wait_ge(att_turned, 1)
                nc.vector.tensor_copy(feature[:, 4, :], pair[0][:, :]).then_inc(attT_ready, 1)
                dve.wait_ge(y_full, 1)
                dve.wait_ge(out_step, 1)
                nc.vector.tensor_tensor(res[:, :], y_ps[:, 0:D], res[:, :], ALU.add).then_inc(out_step, 1)
                dve.wait_ge(out_step, 2)
                nc.vector.bn_stats(stats[:, :], res[:, :]).then_inc(out_step, 1)
                dve.wait_ge(out_step, 3)
                nc.vector.bn_aggr(mv[:, :], stats[:, :]).then_inc(out_step, 1)
                dve.wait_ge(out_step, 4)
                nc.vector.tensor_scalar(rstd[:, :], mv[:, 1:2], 1e-12, None, ALU.add).then_inc(out_step, 1)
                dve.wait_ge(out_root, 1)
                nc.vector.reciprocal(rstd[:, :], rstd[:, :]).then_inc(out_step, 1)
                dve.wait_ge(out_step, 6)
                nc.vector.tensor_scalar(res[:, :], res[:, :], mv[:, 0:1], rstd[:, 0:1], ALU.subtract,
                                        ALU.mult).then_inc(out_step, 1)
                dve.wait_ge(out_step, 7)
                nc.vector.tensor_tensor(res[:, :], res[:, :], ln_g[:, :], ALU.mult).then_inc(out_step, 1)
                nc.vector.tensor_tensor(com.x[:, :], com.x[:, :], ln_b[:, :], ALU.add).then_inc(out_step, 1)
                dve.wait_ge(out_step, 9)
                nc.vector.tensor_tensor(com.x[:, :], com.x[:, :], res[:, :], ALU.add).then_inc(out_step, 1)
                dve.wait_ge(out_step, 10)



_INS = [
        'x', 'ctx_1024', 'fside_Bx16xSxS2_0', 'mask_BxS2_bf1', 'L0_xattn_W_q', 'L0_xattn_W_k', 'L0_xattn_W_v',
        'L0_attn_source_embedding', 'L0_attn_value_embedding', 'L0_attn_Wq', 'L0_attn_bq', 'L0_attn_Wk',
        'L0_attn_bk', 'L0_attn_Wv', 'L0_attn_bv', 'L0_attn_Wo', 'L0_attn_bo', 'L0_attn_ln_g', 'L0_attn_ln_b',
        'L0_ffn_Wr', 'L0_ffn_Wg', 'L0_ffn_Wu', 'L0_ffn_Wd', 'L0_ffn_Sg', 'L0_ffn_Su', 'L0_ffn_Sd',
        'L1_xattn_Wq', 'L1_xattn_bq', 'L1_xattn_Wk', 'L1_xattn_bk', 'L1_xattn_Wv', 'L1_xattn_bv',
        'L1_xattn_Wo', 'L1_xattn_bo', 'L1_attn_Win', 'L1_attn_bin_', 'L1_attn_A_log', 'L1_attn_B',
        'L1_attn_C', 'L1_attn_Dp', 'L1_attn_dt', 'L1_attn_Wout', 'L1_attn_bout', 'L1_ffn_Wg', 'L1_ffn_bg',
        'L1_ffn_We', 'L1_ffn_be', 'L2_xattn_Wq', 'L2_xattn_Wk', 'L2_xattn_Wv', 'L2_xattn_Wo', 'L2_attn_Wq',
        'L2_attn_Wkv_down', 'L2_attn_Wk_up', 'L2_attn_Wv_up', 'L2_attn_Wout', 'L2_ffn_router_w',
        'L2_ffn_router_b', 'L2_ffn_w1', 'L2_ffn_b1', 'L2_ffn_w2', 'L2_ffn_b2', 'L3_xattn_Wq', 'L3_xattn_bq',
        'L3_xattn_Wk', 'L3_xattn_bk', 'L3_xattn_Wv', 'L3_xattn_bv', 'L3_xattn_Wo', 'L3_xattn_bo',
        'L3_attn_Wq', 'L3_attn_bq', 'L3_attn_Wk', 'L3_attn_bk', 'L3_attn_Wv', 'L3_attn_bv', 'L3_attn_Wo',
        'L3_attn_bo', 'L3_ffn_Ws1', 'L3_ffn_bs1', 'L3_ffn_Ws2', 'L3_ffn_bs2', 'L3_ffn_We1', 'L3_ffn_be1',
        'L3_ffn_We2', 'L3_ffn_be2', 'L3_ffn_Wr', 'L3_ffn_br']
_OUTS = [((1, 128, 256), "float32")]


def latent_decoder(nc, a, out):
    with ExitStack() as ctx:
        com, scr = common(nc, ctx)
        setup(nc, com, a)
        prepare_context(nc, com, a, scr)
        l0_cross_attention(nc, com, a, scr)
        l0_attention(nc, com, a)
        l0_experts(nc, com, a)
        cross_attention_16(nc, com, a, scr, "L1")
        l1_state_space(nc, com, a)
        l1_experts(nc, com, a)
        l2_cross_attention(nc, com, a, scr)
        l2_attention(nc, com, a)
        l2_experts(nc, com, a)
        cross_attention_16(nc, com, a, scr, "L3")
        l3_attention(nc, com, a)
        l3_experts(nc, com, a)
        with phase(nc, "end") as ph:
            stored = ph.sem("stored")
            with nc.Block() as block:
                @block.sync
                def _(sp):
                    sp.dma_start(out[0], com.x[:, :]).then_inc(stored, 16)
                    sp.wait_ge(stored, 16)


def kernel(**inputs):
    import numpy as _np
    import concourse.bacc as _bacc
    from concourse import mybir as _mybir
    from concourse.bass_utils import run_bass_kernel_spmd as _run

    nc = _bacc.Bacc("TRN2", target_bir_lowering=False, num_devices=1)
    arrays, args = {}, {}
    for name in _INS:
        a = _np.ascontiguousarray(inputs[name])
        arrays[f"in_{name}_dram"] = a
        args[name] = nc.dram_tensor(f"in_{name}_dram", a.shape, _mybir.dt.from_np(a.dtype), kind="ExternalInput").ap()
    outs = []
    for i, (shape, dtype) in enumerate(_OUTS):
        dt = _mybir.dt.from_np(_np.dtype(dtype))
        outs.append(nc.dram_tensor(f"out_{i}_dram", shape, dt, kind="ExternalOutput").ap())
    latent_decoder(nc, args, outs[0])
    r = _run(nc, [arrays], core_ids=[0])
    return r.results[0]["out_0_dram"]
```
